# Optimizing a Trainium2 kernel written in Bass

```python
import numpy as np
import jax
import jax.numpy as jnp

def _softmax(x, axis=-1):
    return jax.nn.softmax(x, axis=axis)

def _gelu(x):
    return jax.nn.gelu(x, approximate=True)

def _silu(x):
    return jax.nn.silu(x)

def _sigmoid(x):
    return jax.nn.sigmoid(x)

def _layernorm(x, axis=-1, eps=1e-05):
    m = jnp.mean(x, axis=axis, keepdims=True)
    v = jnp.var(x, axis=axis, keepdims=True)
    return (x - m) / jnp.sqrt(v + eps)

def _scatter_add(tgt, idx, src, axis=0):
    return tgt.at[idx].add(src)

def _segment_sum(src, seg, n):
    return jax.ops.segment_sum(src, seg, n)
kernel_name = 'mk_sandwich_d2_jaxref_r8_98d689'

def setup_inputs(seed: int=0):
    np.random.seed(seed)
    _w = jnp.asarray

    def _L0_attn_setup():
        import jax, jax.numpy as jnp
        from jax import lax
        import numpy as np
        DIM = 128
        HEADS = 16
        B, N = (2, 256)

        def sn_dense(x, W, u, sigma_param):
            v = lax.stop_gradient(W @ u)
            v = lax.stop_gradient(v / jnp.linalg.norm(v, ord=2))
            u2 = lax.stop_gradient(W.T @ v)
            u2 = lax.stop_gradient(u2 / jnp.linalg.norm(u2, ord=2))
            sigma = jnp.einsum('c,cd,d->', v, W, u2)
            return x @ (sigma_param[0] / sigma * W)
        key = jax.random.key(seed)
        ks = jax.random.split(key, 5)
        std = 0.1
        batch = jax.random.normal(ks[0], (B, N, DIM), dtype=jnp.float32)
        W_qkv = jax.random.normal(ks[1], (DIM, 3 * DIM), dtype=jnp.float32) * std
        W_proj = jax.random.normal(ks[2], (DIM, DIM), dtype=jnp.float32) * std
        u_qkv = jax.random.normal(ks[3], (3 * DIM,), dtype=jnp.float32)
        u_qkv = u_qkv / jnp.linalg.norm(u_qkv)
        u_proj = jax.random.normal(ks[4], (DIM,), dtype=jnp.float32)
        u_proj = u_proj / jnp.linalg.norm(u_proj)
        sigma_qkv = jnp.ones((1,), dtype=jnp.float32)
        sigma_proj = jnp.ones((1,), dtype=jnp.float32)
        return {'batch': batch, 'W_qkv': W_qkv, 'u_qkv': u_qkv, 'sigma_qkv': sigma_qkv, 'W_proj': W_proj, 'u_proj': u_proj, 'sigma_proj': sigma_proj}
    _L0_attn_in = _L0_attn_setup()

    def _L0_ffn_setup():
        import jax, jax.numpy as jnp
        import numpy as np
        B, S, D, E, K = (2, 256, 128, 8, 2)
        H = 4 * D
        key = jax.random.key(seed)
        ks = jax.random.split(key, 6)
        x = jax.random.normal(ks[0], (B, S, D), dtype=jnp.float32)
        lim_g = np.sqrt(6.0 / (D + E)).astype(np.float32)
        W_gate = jax.random.uniform(ks[1], (D, E), minval=-lim_g, maxval=lim_g, dtype=jnp.float32)
        lim1 = np.sqrt(1.0 / D).astype(np.float32)
        lim2 = np.sqrt(1.0 / H).astype(np.float32)
        W1 = jax.random.uniform(ks[2], (E, D, H), minval=-lim1, maxval=lim1, dtype=jnp.float32)
        b1 = jax.random.uniform(ks[3], (E, H), minval=-lim1, maxval=lim1, dtype=jnp.float32)
        W2 = jax.random.uniform(ks[4], (E, H, D), minval=-lim2, maxval=lim2, dtype=jnp.float32)
        b2 = jax.random.uniform(ks[5], (E, D), minval=-lim2, maxval=lim2, dtype=jnp.float32)
        return {'x': x, 'W_gate': W_gate, 'W1': W1, 'b1': b1, 'W2': W2, 'b2': b2}
    _L0_ffn_in = _L0_ffn_setup()

    def _L1_attn_setup():
        import jax, jax.numpy as jnp
        import numpy as np
        D_MODEL = 128
        NHEAD = 16
        HEAD_DIM = D_MODEL // NHEAD
        NPOS_MAX = 125
        SEQ = 128
        BATCH = 4

        def _cope(query, attn_logits, pos_emb):
            gates = jax.nn.sigmoid(attn_logits)
            pos = jnp.cumsum(gates[..., ::-1], axis=-1)[..., ::-1]
            pos = jnp.minimum(pos, NPOS_MAX - 1)
            pos_ceil = jnp.ceil(pos).astype(jnp.int32)
            pos_floor = jnp.floor(pos).astype(jnp.int32)
            logits_int = jnp.einsum('hbsd,dn->hbsn', query, pos_emb[0])
            logits_ceil = jnp.take_along_axis(logits_int, pos_ceil, axis=-1)
            logits_floor = jnp.take_along_axis(logits_int, pos_floor, axis=-1)
            w = pos - pos_floor.astype(pos.dtype)
            return logits_ceil * w + logits_floor * (1.0 - w)
        key = jax.random.key(seed)
        ks = jax.random.split(key, 10)
        s = 0.02
        return {'x': jax.random.normal(ks[0], (SEQ, BATCH, D_MODEL), dtype=jnp.float32), 'Wq': jax.random.normal(ks[1], (D_MODEL, D_MODEL), dtype=jnp.float32) * s, 'bq': jnp.zeros((D_MODEL,), dtype=jnp.float32), 'Wk': jax.random.normal(ks[2], (D_MODEL, D_MODEL), dtype=jnp.float32) * s, 'bk': jnp.zeros((D_MODEL,), dtype=jnp.float32), 'Wv': jax.random.normal(ks[3], (D_MODEL, D_MODEL), dtype=jnp.float32) * s, 'bv': jnp.zeros((D_MODEL,), dtype=jnp.float32), 'Wo': jax.random.normal(ks[4], (D_MODEL, D_MODEL), dtype=jnp.float32) * s, 'bo': jnp.zeros((D_MODEL,), dtype=jnp.float32), 'pos_emb': jax.random.normal(ks[5], (1, HEAD_DIM, NPOS_MAX), dtype=jnp.float32) * s}
    _L1_attn_in = _L1_attn_setup()

    def _L1_ffn_setup():
        import jax, jax.numpy as jnp
        import numpy as np
        D_MODEL = 128
        M = 64
        INNER = 16
        key = jax.random.key(seed)
        ks = jax.random.split(key, 9)

        def init(k, shape, fan_in):
            bound = 1.0 / np.sqrt(fan_in)
            return jax.random.uniform(k, shape, jnp.float32, -bound, bound)
        x = jax.random.normal(ks[0], (16, 512, D_MODEL), dtype=jnp.float32)
        Win = init(ks[1], (D_MODEL, M), D_MODEL)
        bin_ = init(ks[2], (M,), D_MODEL)
        W1 = init(ks[3], (M, INNER), 1)
        b1 = init(ks[4], (M, INNER), 1)
        W2 = init(ks[5], (M, INNER), INNER)
        b2 = init(ks[6], (M,), INNER)
        Wout = init(ks[7], (M, D_MODEL), M)
        bout = init(ks[8], (D_MODEL,), M)
        return {'x': x, 'Win': Win, 'bin_': bin_, 'W1': W1, 'b1': b1, 'W2': W2, 'b2': b2, 'Wout': Wout, 'bout': bout}
    _L1_ffn_in = _L1_ffn_setup()
    _d = {'L0_attn_batch': _L0_attn_in['batch'], 'L0_attn_W_qkv': _L0_attn_in['W_qkv'], 'L0_attn_u_qkv': _L0_attn_in['u_qkv'], 'L0_attn_sigma_qkv': _L0_attn_in['sigma_qkv'], 'L0_attn_W_proj': _L0_attn_in['W_proj'], 'L0_attn_u_proj': _L0_attn_in['u_proj'], 'L0_attn_sigma_proj': _L0_attn_in['sigma_proj'], 'L0_ffn_W_gate': _L0_ffn_in['W_gate'], 'L0_ffn_W1': _L0_ffn_in['W1'], 'L0_ffn_b1': _L0_ffn_in['b1'], 'L0_ffn_W2': _L0_ffn_in['W2'], 'L0_ffn_b2': _L0_ffn_in['b2'], 'L1_attn_Wq': _L1_attn_in['Wq'], 'L1_attn_bq': _L1_attn_in['bq'], 'L1_attn_Wk': _L1_attn_in['Wk'], 'L1_attn_bk': _L1_attn_in['bk'], 'L1_attn_Wv': _L1_attn_in['Wv'], 'L1_attn_bv': _L1_attn_in['bv'], 'L1_attn_Wo': _L1_attn_in['Wo'], 'L1_attn_bo': _L1_attn_in['bo'], 'L1_attn_pos_emb': _L1_attn_in['pos_emb'], 'L1_ffn_Win': _L1_ffn_in['Win'], 'L1_ffn_bin_': _L1_ffn_in['bin_'], 'L1_ffn_W1': _L1_ffn_in['W1'], 'L1_ffn_b1': _L1_ffn_in['b1'], 'L1_ffn_W2': _L1_ffn_in['W2'], 'L1_ffn_b2': _L1_ffn_in['b2'], 'L1_ffn_Wout': _L1_ffn_in['Wout'], 'L1_ffn_bout': _L1_ffn_in['bout']}
    _x0 = _d['L0_attn_batch']
    _d['L0_attn_batch'] = jax.random.normal(jax.random.fold_in(jax.random.key(seed), 1), (16, 512, 128), dtype=_x0.dtype)
    del _x0
    return _d

def reference(L0_attn_batch, L0_attn_W_qkv, L0_attn_u_qkv, L0_attn_sigma_qkv, L0_attn_W_proj, L0_attn_u_proj, L0_attn_sigma_proj, L0_ffn_W_gate, L0_ffn_W1, L0_ffn_b1, L0_ffn_W2, L0_ffn_b2, L1_attn_Wq, L1_attn_bq, L1_attn_Wk, L1_attn_bk, L1_attn_Wv, L1_attn_bv, L1_attn_Wo, L1_attn_bo, L1_attn_pos_emb, L1_ffn_Win, L1_ffn_bin_, L1_ffn_W1, L1_ffn_b1, L1_ffn_W2, L1_ffn_b2, L1_ffn_Wout, L1_ffn_bout):

    def _L0_attn_ref(batch, W_qkv, u_qkv, sigma_qkv, W_proj, u_proj, sigma_proj):
        import jax, jax.numpy as jnp
        from jax import lax
        import numpy as np
        DIM = 128
        HEADS = 16
        B, N = (2, 256)

        def sn_dense(x, W, u, sigma_param):
            v = lax.stop_gradient(W @ u)
            v = lax.stop_gradient(v / jnp.linalg.norm(v, ord=2))
            u2 = lax.stop_gradient(W.T @ v)
            u2 = lax.stop_gradient(u2 / jnp.linalg.norm(u2, ord=2))
            sigma = jnp.einsum('c,cd,d->', v, W, u2)
            return x @ (sigma_param[0] / sigma * W)
        b, n, d = batch.shape
        h = HEADS
        hd = d // h
        qkv = sn_dense(batch, W_qkv, u_qkv, sigma_qkv)
        q, k, v = jnp.split(qkv, 3, axis=-1)
        split_heads = lambda t: t.reshape(b, n, h, hd).transpose(0, 2, 1, 3)
        q, k, v = (split_heads(q), split_heads(k), split_heads(v))
        scale = hd ** (-0.5)
        att = jnp.einsum('bhqd,bhkd->bhqk', q, k) * scale
        causal = jnp.tril(jnp.ones((n, n), dtype=jnp.float32))
        big_neg = jnp.finfo(att.dtype).min
        att = jnp.where(causal[None, None] == 0, big_neg, att)
        att = jax.nn.softmax(att, axis=-1)
        x = jnp.einsum('bhqk,bhkd->bhqd', att, v)
        x = x.transpose(0, 2, 1, 3).reshape(b, n, d)
        x = sn_dense(x, W_proj, u_proj, sigma_proj)
        return x

    def _L0_ffn_ref(x, W_gate, W1, b1, W2, b2):
        import jax, jax.numpy as jnp
        import numpy as np
        B, S, D, E, K = (2, 256, 128, 8, 2)
        H = 4 * D
        gate = jnp.einsum('bsd,de->bse', x, W_gate)
        kth = jax.lax.top_k(gate, K)[0][..., -1:]
        mask = jax.nn.softmax(jnp.where(gate >= kth, gate, -jnp.inf), axis=-1)
        h = jax.nn.relu(jnp.einsum('bsd,edh->bseh', x, W1) + b1)
        y = jnp.einsum('bseh,ehd->bsed', h, W2) + b2
        return (y * mask[..., None]).mean(axis=-2)

    def _L1_attn_ref(x, Wq, bq, Wk, bk, Wv, bv, Wo, bo, pos_emb):
        import jax, jax.numpy as jnp
        import numpy as np
        D_MODEL = 128
        NHEAD = 16
        HEAD_DIM = D_MODEL // NHEAD
        NPOS_MAX = 125
        SEQ = 128
        BATCH = 4

        def _cope(query, attn_logits, pos_emb):
            gates = jax.nn.sigmoid(attn_logits)
            pos = jnp.cumsum(gates[..., ::-1], axis=-1)[..., ::-1]
            pos = jnp.minimum(pos, NPOS_MAX - 1)
            pos_ceil = jnp.ceil(pos).astype(jnp.int32)
            pos_floor = jnp.floor(pos).astype(jnp.int32)
            logits_int = jnp.einsum('hbsd,dn->hbsn', query, pos_emb[0])
            logits_ceil = jnp.take_along_axis(logits_int, pos_ceil, axis=-1)
            logits_floor = jnp.take_along_axis(logits_int, pos_floor, axis=-1)
            w = pos - pos_floor.astype(pos.dtype)
            return logits_ceil * w + logits_floor * (1.0 - w)
        S, B, _ = x.shape

        def split_heads(t):
            return t.reshape(S, B, NHEAD, HEAD_DIM).transpose(2, 1, 0, 3)
        q = split_heads(x @ Wq + bq)
        k = split_heads(x @ Wk + bk)
        v = split_heads(x @ Wv + bv)
        scale = 1.0 / HEAD_DIM ** 0.5
        attn_logits = jnp.einsum('hbsd,hbtd->hbst', q, k) * scale
        attn_logits = attn_logits + _cope(q, attn_logits, pos_emb)
        attn = jax.nn.softmax(attn_logits, axis=-1)
        out = jnp.einsum('hbst,hbtd->hbsd', attn, v)
        out = out.transpose(2, 1, 0, 3).reshape(S, B, D_MODEL)
        return out @ Wo + bo

    def _L1_ffn_ref(x, Win, bin_, W1, b1, W2, b2, Wout, bout):
        import jax, jax.numpy as jnp
        import numpy as np
        D_MODEL = 128
        M = 64
        INNER = 16
        s = jnp.einsum('btd,dm->btm', x, Win) + bin_
        h = jax.nn.relu(s[..., None] * W1 + b1)
        g = jnp.einsum('btmh,mh->btm', h, W2) + b2
        out = jnp.einsum('btm,md->btd', g, Wout) + bout
        return out
    x = L0_attn_batch
    x = x + _layernorm(_L0_attn_ref(_layernorm(x, axis=-1), L0_attn_W_qkv, L0_attn_u_qkv, L0_attn_sigma_qkv, L0_attn_W_proj, L0_attn_u_proj, L0_attn_sigma_proj), axis=-1)
    x = x + _layernorm(_L0_ffn_ref(_layernorm(x, axis=-1), L0_ffn_W_gate, L0_ffn_W1, L0_ffn_b1, L0_ffn_W2, L0_ffn_b2), axis=-1)
    x = x + _layernorm(_L1_attn_ref(_layernorm(x, axis=-1), L1_attn_Wq, L1_attn_bq, L1_attn_Wk, L1_attn_bk, L1_attn_Wv, L1_attn_bv, L1_attn_Wo, L1_attn_bo, L1_attn_pos_emb), axis=-1)
    x = x + _layernorm(_L1_ffn_ref(_layernorm(x, axis=-1), L1_ffn_Win, L1_ffn_bin_, L1_ffn_W1, L1_ffn_b1, L1_ffn_W2, L1_ffn_b2, L1_ffn_Wout, L1_ffn_bout), axis=-1)
    return x

_drawn_inputs = setup_inputs


def setup_inputs(seed=0):
    import zlib

    import numpy as np

    out = dict(_drawn_inputs(seed))
    spreads = {'L1_attn_bq': (0.0, 0.8),
     'L1_attn_bk': (0.0, 0.8),
     'L1_attn_bv': (0.0, 0.1),
     'L1_attn_bo': (0.0, 0.1)}
    factors = {'L0_attn_u_proj': 8.0,
     'L1_attn_Wq': 8.0,
     'L1_attn_Wk': 8.0,
     'L1_attn_pos_emb': 8.0,
     'L1_ffn_bin_': 4.294}
    for name, (base, spread) in spreads.items():
        noise = np.random.default_rng([zlib.crc32(name.encode()), seed]).standard_normal(out[name].shape)
        drawn = base * np.exp(spread * noise) if base else spread * noise
        out[name] = jnp.asarray(drawn.astype(out[name].dtype))
    for name, factor in factors.items():
        out[name] = (out[name] * factor).astype(out[name].dtype)
    return out
```

```python
import concourse.bass as bass
from concourse import mybir
from contextlib import ExitStack

F32 = mybir.dt.float32
BF16 = mybir.dt.bfloat16
ALU = mybir.AluOpType
ACT = mybir.ActivationFunctionType
AX = mybir.AxisListType

P = 128
S, N, D = 16, 512, 128
C = N // P
T = S * C
H, HD = 16, 8
SCALE = HD ** -0.5
EPS = 1e-5
E, HID = 8, 512
F = HID // P
PARTS = 6
KS = PARTS * HD
MR = 3
NPOS = S
M2, J2 = 64, 16
K2 = M2 * J2 // P
NEG = -3.0e38
LOWEST = -3.4028e38


class Ticks:

    def __init__(self, sem, base=0):
        self.sem, self.base, self.n = sem, base, 0

    def __call__(self, instruction, by=1):
        instruction.then_inc(self.sem, by)
        self.n += by

    def value(self):
        return self.base + self.n


def await_(eng, passed, sem, value):
    eng.wait_ge(sem, value)
    eng.sem_inc(passed, 1)


def load_and_prepare(nc, a, t, sem):
    x_in = a["L0_attn_batch"].rearrange("s (c p) d -> s p c d", p=P)
    x_sb = t.x[:, :, :].rearrange("p (c s) d -> p c s d", s=S)
    s_norm, s_attn, s_ffn = sem("norm_weights_loaded"), sem("attn_weights_loaded"), sem("ffn_weights_loaded")
    s_pool, s_vec, s_pe, s_act = sem("pool_step"), sem("vector_step"), sem("tensor_step"), sem("scalar_step")
    norm_loads, attn_loads, ffn_loads = [], [], []

    def row(v, n):
        return v.rearrange("(o n) -> o n", o=1).broadcast_to([P, n])

    with ExitStack() as ctx:
        def sb(name, shape, dt=F32):
            return ctx.enter_context(nc.sbuf_tensor(name, shape, dt))

        def ps(name):
            return ctx.enter_context(nc.psum_tensor(name, [P, 512], F32))

        u_row, up_row = sb("u_row", [P, 384]), sb("up_row", [P, D])
        sigma, norms, junk = sb("sigma", [P, 2]), sb("norms", [P, 8]), sb("junk", [P, 384])
        wu, wu_rep = sb("wu", [P, 2]), sb("wu_rep", [P, 2, P])
        b1_rows, b2_rows = sb("b1_rows", [E * F, P]), sb("b2_rows", [E, D])
        wq_t, pe_rep, kink = sb("wq_t", [P, P]), sb("pe_rep", [P, NPOS + 2]), sb("kink", [P, 2 * NPOS])
        blocks, bq_col, bq_rep = sb("blocks", [P, 2 * NPOS, H]), sb("bq_col", [P, 1]), sb("bq_rep", [P, P])
        head_of = sb("head_of", [P, H])
        win, wout = sb("win", [P, M2]), sb("wout", [M2, D])
        w1_row, b1_row, bin_row = sb("w1_row", [P, M2 * J2]), sb("b1_row", [1, M2 * J2]), sb("bin_row", [1, M2])
        w2_in, w2_spread = sb("w2_in", [M2, J2]), sb("w2_spread", [M2, M2, J2])
        b2_col, bout_col = sb("b2_col", [M2, 1]), sb("bout_col", [P, 1])
        pa, pb, pc, pd, pe2 = ps("pa"), ps("pb"), ps("pc"), ps("pd"), ps("pe2")
        junk2, junk3, s_mid = sb("junk2", [P, 2]), sb("junk3", [1, M2 * J2]), sem("kink_step")
        half = sb("half", [P, 2])

        norm_loads += [
            (t.w_qkv[:, :], a["L0_attn_W_qkv"]), (t.w_proj[:, :], a["L0_attn_W_proj"]),
            (u_row[:, :], row(a["L0_attn_u_qkv"], 384)), (up_row[:, :], row(a["L0_attn_u_proj"], D)),
            (sigma[:, 0:1], row(a["L0_attn_sigma_qkv"], 1)), (sigma[:, 1:2], row(a["L0_attn_sigma_proj"], 1)),
        ]
        attn_loads += [(t.w_at[:, i * D:(i + 1) * D], a["L1_attn_" + n]) for i, n in enumerate(["Wq", "Wk", "Wv"])]
        attn_loads += [(t.b_at[:, i * D:(i + 1) * D], row(a["L1_attn_" + n], D)) for i, n in enumerate(["bq", "bk", "bv"])]
        attn_loads += [
            (t.w_o[:, :], a["L1_attn_Wo"]), (t.b_o[:, :], row(a["L1_attn_bo"], D)),
            (bq_col[:, :], a["L1_attn_bq"].rearrange("(n o) -> n o", o=1)),
        ]
        attn_loads += [(pe_rep[HD * h:HD * h + HD, :], a["L1_attn_pos_emb"][0, :, 0:NPOS + 2]) for h in range(H)]
        ffn_loads += [
            (t.w_gate[:, :], a["L0_ffn_W_gate"]),
            (t.w1[:, :, :], a["L0_ffn_W1"].rearrange("e d h -> d e h")),
            (t.w2[:, :, :], a["L0_ffn_W2"].rearrange("e (f p) d -> p (e f) d", p=P)),
            (b1_rows[:, :], a["L0_ffn_b1"].rearrange("e (f p) -> (e f) p", p=P)),
            (b2_rows[:, :], a["L0_ffn_b2"]),
            (win[:, :], a["L1_ffn_Win"]), (wout[:, :], a["L1_ffn_Wout"]),
            (w1_row[:, :], row(a["L1_ffn_W1"].rearrange("m j -> (m j)"), M2 * J2)),
            (b1_row[:, :], a["L1_ffn_b1"].rearrange("m j -> (m j)").rearrange("(o n) -> o n", o=1)),
            (bin_row[:, :], a["L1_ffn_bin_"].rearrange("(o n) -> o n", o=1)),
            (w2_in[:, :], a["L1_ffn_W2"]), (b2_col[:, :], a["L1_ffn_b2"].rearrange("(n o) -> n o", o=1)),
            (bout_col[:, :], a["L1_ffn_bout"].rearrange("(n o) -> n o", o=1)),
        ]

        with nc.Block() as block:
            @block.sync
            def _(sp):
                for dst, src in norm_loads:
                    sp.dma_start(dst, src).then_inc(s_norm, 16)
                sp.dma_start(x_sb[:, :, 0, :], x_in[0]).then_inc(t.first_x_loaded, 16)
                for dst, src in attn_loads:
                    sp.dma_start(dst, src).then_inc(s_attn, 16)
                for s in range(1, S):
                    sp.dma_start(x_sb[:, :, s, :], x_in[s]).then_inc(t.rest_x_loaded, 16)

            @block.gpsimd
            def _(pool):
                done = Ticks(s_pool)
                done(pool.memset(t.ones[:, :], 1.0))
                done(pool.memset(t.ident[:, :], 0.0))
                done(pool.memset(t.causal[:, :], 0.0))
                done(pool.memset(head_of[:, :], 1.0))
                pool.wait_ge(s_pool, done.value())
                done(pool.affine_select(out=t.ident[:, :], in_=t.ident[:, :], compare_op=ALU.not_equal, fill=1.0,
                                        base=0, pattern=[[-1, P]], channel_multiplier=1))
                last = t.causal[:, N - P:N]
                done(pool.affine_select(out=last, in_=last, compare_op=ALU.is_ge, fill=NEG,
                                        base=0, pattern=[[-1, P]], channel_multiplier=1))
                done(pool.affine_select(out=head_of[:, :], in_=head_of[:, :], compare_op=ALU.is_ge, fill=0.0,
                                        base=0, pattern=[[-HD, H]], channel_multiplier=1))
                pool.wait_ge(s_pool, done.value())
                done(pool.affine_select(out=head_of[:, :], in_=head_of[:, :], compare_op=ALU.is_ge, fill=0.0,
                                        base=HD - 1, pattern=[[HD, H]], channel_multiplier=-1))
                assert done.n == 8
                done(pool.tensor_copy(t.ident16[:, :], t.ident[:, :]))
                done(pool.memset(t.k_stack[:, :, :], 1.0))
                done(pool.memset(t.v_ext[:, :, :, :], 0.0))
                pool.wait_ge(s_pool, done.value())
                pool.memset(t.v_ext[:, :, :, HD:HD + 1], 1.0)
                pool.memset(t.minus_half[:, :], -0.5)
                done(pool.memset(half[:, :], 0.5))
                pool.wait_ge(s_ffn, 16 * len(ffn_loads))
                done(pool.affine_select(out=w2_spread[:, :, :],
                                        in_=w2_in[:, :].unsqueeze(1).broadcast_to([M2, M2, J2]),
                                        compare_op=ALU.is_equal, fill=0.0,
                                        base=0, pattern=[[-1, M2], [0, J2]], channel_multiplier=1))
                assert done.n == 13
                pool.wait_ge(s_pool, done.value())
                pool.wait_ge(s_vec, 6)
                done(pool.tensor_tensor(norms[:, 4:6], norms[:, 2:4], half[:, :], ALU.pow))
                assert done.n == 14

            @block.scalar
            def _(act):
                for dst, src in ffn_loads:
                    act.dma_start(dst, src).then_inc(s_ffn, 16)
                act.wait_ge(s_pe, 3)
                act.activation(junk[:, 0:384], pa[:, 0:384], ACT.Square, accum_out=norms[:, 0:1]).then_inc(s_act, 1)
                act.wait_ge(s_act, 1)
                act.activation(junk[:, 0:D], pb[:, 0:D], ACT.Square, accum_out=norms[:, 1:2]).then_inc(s_act, 1)

            @block.tensor
            def _(pe):
                done = Ticks(s_pe)
                pe.wait_ge(s_vec, 4)
                done(pe.matmul(pa[:, 0:384], wu_rep[:, 0, :], t.w_qkv[:, :], start=True, stop=True))
                done(pe.matmul(pb[:, 0:D], wu_rep[:, 1, :], t.w_proj[:, :], start=True, stop=True))
                done(pe.matmul(pc[:, 0:2], t.ones[:, :], junk2[:, 0:2], start=True, stop=True))
                pe.wait_ge(s_pool, 8)
                pe.wait_ge(s_attn, 16 * len(attn_loads))
                done(pe.transpose(pd[:, 0:P], t.w_at[:, 0:D], t.ident[:, :]))
                pe.wait_ge(s_vec, 11)
                done(pe.matmul(pa[:, :], wq_t[:, :], blocks[:, :, :].rearrange("p n h -> p (n h)"), start=True, stop=True))
                done(pe.matmul(pb[:, :], bq_rep[:, :], blocks[:, :, :].rearrange("p n h -> p (n h)"), start=True, stop=True))
                pe.wait_ge(s_ffn, 16 * len(ffn_loads))
                done(pe.transpose(pd[:, 128:128 + E * F], b1_rows[:, :], t.ident[0:E * F, 0:E * F]))
                done(pe.transpose(pd[:, 192:192 + E], b2_rows[:, :], t.ident[0:E, 0:E]))
                done(pe.matmul(pd[:, 224:225], wout[:, :], b2_col[:, :], start=True, stop=True))
                pe.wait_ge(s_vec, 14)
                for k in range(K2):
                    mm = pe.matmul(pd[:, 240 + k:241 + k], b1_row[:, k * P:(k + 1) * P], t.ones[0:1, 0:1],
                                   start=True, stop=True)
                done(mm)
                pe.wait_ge(s_pool, 13)
                for k in range(K2):
                    dst = (pc, pe2)[k // 4]
                    mm = pe.matmul(dst[:, (k % 4) * P:(k % 4 + 1) * P],
                                   w2_spread[:, k * 8:(k + 1) * 8, :].rearrange("m a j -> m (a j)"), wout[:, :],
                                   start=True, stop=True)
                done(mm)
                assert done.n == 11

            @block.vector
            def _(dve):
                done = Ticks(s_vec)
                dve.wait_ge(s_norm, 16 * len(norm_loads))
                dve.wait_ge(s_pool, 1)
                dve.tensor_tensor_reduce(junk[:, 0:384], t.w_qkv[:, :], u_row[:, :], 1.0, 0.0, ALU.mult, ALU.add,
                                         wu[:, 0:1]).then_inc(s_vec, 1)
                dve.tensor_tensor_reduce(up_row[:, :], t.w_proj[:, :], up_row[:, :], 1.0, 0.0, ALU.mult, ALU.add,
                                         wu[:, 1:2]).then_inc(s_vec, 1)
                dve.wait_ge(s_vec, 2)
                dve.tensor_tensor(junk2[:, :], wu[:, :], wu[:, :], ALU.mult)
                dve.tensor_scalar(wu_rep[:, 0, :], t.ones[:, :], wu[:, 0:1], None, ALU.mult).then_inc(s_vec, 1)
                dve.tensor_scalar(wu_rep[:, 1, :], t.ones[:, :], wu[:, 1:2], None, ALU.mult).then_inc(s_vec, 1)
                done.n = 4
                dve.wait_ge(s_act, 2)
                done(dve.reciprocal(norms[:, 6:8], norms[:, 0:2]))
                dve.wait_ge(s_vec, done.value())
                done(dve.tensor_tensor(norms[:, 2:4], pc[:, 0:2], norms[:, 6:8], ALU.mult))
                dve.wait_ge(s_pool, 14)
                done(dve.tensor_tensor(sigma[:, :], norms[:, 4:6], sigma[:, :], ALU.mult))
                dve.wait_ge(s_vec, done.value())
                dve.tensor_scalar(t.w_qkv[:, :], t.w_qkv[:, :], sigma[:, 0:1], None, ALU.mult)
                done(dve.tensor_scalar(t.w_proj[:, :], t.w_proj[:, :], sigma[:, 1:2], None, ALU.mult))
                dve.wait_ge(s_attn, 16 * len(attn_loads))
                tmp = junk[:, 0:NPOS]
                mid = Ticks(s_mid)
                mid(dve.scalar_tensor_tensor(tmp, pe_rep[:, 1:NPOS + 1], -2.0, pe_rep[:, 0:NPOS], ALU.mult, ALU.add))
                mid(dve.tensor_tensor(kink[:, 0:1], pe_rep[:, 1:2], pe_rep[:, 0:1], ALU.subtract))
                for k in range(NPOS):
                    col = kink[:, 2 * NPOS - 1 - k:2 * NPOS - k]
                    mid(dve.tensor_scalar(col, pe_rep[:, k:k + 1], float(k + 1), None, ALU.mult))
                dve.wait_ge(s_mid, mid.value())
                mid(dve.tensor_tensor(kink[:, 1:NPOS], tmp[:, 0:NPOS - 1], pe_rep[:, 2:NPOS + 1], ALU.add))
                for k in range(NPOS):
                    col = kink[:, 2 * NPOS - 1 - k:2 * NPOS - k]
                    mid(dve.scalar_tensor_tensor(col, pe_rep[:, k + 1:k + 2], float(-k), col, ALU.mult, ALU.add))
                dve.wait_ge(s_mid, mid.value())
                dve.wait_ge(s_pool, 8)
                done(dve.tensor_tensor(blocks[:, :, :], kink[:, :].unsqueeze(2).broadcast_to([P, 2 * NPOS, H]),
                                       head_of[:, :].unsqueeze(1).broadcast_to([P, 2 * NPOS, H]), ALU.mult))
                done(dve.tensor_scalar(bq_rep[:, :], t.ones[:, :], bq_col[:, 0:1], None, ALU.mult))
                dve.wait_ge(s_pe, 4)
                done(dve.tensor_copy(wq_t[:, :], pd[:, 0:P]))
                assert done.n == 11
                dve.wait_ge(s_pe, 6)
                done(dve.tensor_copy(t.w_kink[:, :], pa[:, :]))
                done(dve.tensor_copy(t.b_kink[:, :], pb[:, :]))
                dve.wait_ge(s_ffn, 16 * len(ffn_loads))
                inner = junk3[:, :].rearrange("p (m j) -> p m j", j=J2)
                mid(dve.tensor_tensor(inner, bin_row[:, :].unsqueeze(2).broadcast_to([1, M2, J2]),
                                      w1_row[0:1, :].rearrange("p (m j) -> p m j", j=J2), ALU.mult))
                dve.wait_ge(s_mid, mid.value())
                done(dve.tensor_tensor(b1_row[:, :], junk3[:, :], b1_row[:, :], ALU.add))
                assert done.n == 14
                dve.tensor_tensor(t.w_in[:, :].rearrange("p (m j) -> p m j", j=J2),
                                  win[:, :].unsqueeze(2).broadcast_to([P, M2, J2]),
                                  w1_row[:, :].rearrange("p (m j) -> p m j", j=J2), ALU.mult)
                dve.wait_ge(s_pe, 10)
                dve.tensor_copy(t.b1[:, :], pd[:, 128:128 + E * F])
                dve.tensor_copy(t.b2[:, :], pd[:, 192:192 + E])
                dve.tensor_tensor(t.b_out[:, :], pd[:, 224:225], bout_col[:, :], ALU.add)
                dve.tensor_copy(t.b_in[:, :], pd[:, 240:240 + K2])
                dve.wait_ge(s_pe, 11)
                dve.tensor_copy(t.w_out[:, 0:4, :], pc[:, :].rearrange("p (k d) -> p k d", d=D))
                dve.tensor_copy(t.w_out[:, 4:8, :], pe2[:, :].rearrange("p (k d) -> p k d", d=D)).then_inc(s_vec, 1)


NQ = 4
PAIRS = H // 2
Q_ORDER = [3, 2, 1, 0]
VECTOR_STEPS_BEFORE, VECTOR_STEPS_ROW = 12, 38


def causal_attention(nc, a, t, sem):
    scratch = {k: nc.dram_tensor("stack_" + k, [H, PARTS, HD, N], BF16, kind="Internal").ap() for k in "qk"}
    part_of = {"q": [0, 0, 0, 1, 1, 2], "k": [0, 1, 2, 0, 1, 0]}
    x_t = t.x[:, :, :].rearrange("p (c s) d -> p c s d", s=S)

    s_scores, s_tile_max = sem("scores_for_maxima"), sem("tile_maxima")
    s_mparts, s_mt, s_mt_copied = sem("max_parts_ready"), sem("max_parts_turned"), sem("max_rows_copied")
    s_mrow = [sem("max_rows_in_stack_even"), sem("max_rows_in_stack_odd")]
    s_st, s_exp, s_masked = sem("scores_turned"), sem("exp_done"), sem("diagonal_masked")
    s_av, s_vext = sem("values_product"), sem("values_in_place")
    s_o_copied, s_o_turned, s_o_norm = sem("outputs_copied"), sem("outputs_turned"), sem("outputs_normalised")
    s_misc, s_misc_read = sem("misc_bank_filled"), sem("misc_bank_read")
    s_vec, s_pool, s_row_done = sem("vector_step0"), sem("pool_step0"), sem("batch_row_done")
    s_var, s_shifted, s_rstd, s_xn = sem("variances"), sem("variances_shifted"), sem("inverse_deviations"), sem("rows_normalised")
    s_parts = {k: sem("all_parts_" + k) for k in "qk"}
    s_written, s_half = sem("stacks_written"), [sem("stack_half_0"), sem("stack_half_1")]
    passed = {k: sem("passed_" + k) for k in ("vector", "scalar", "pool", "sync")}

    def fill_in(b, piece, first=False):
        return (piece + 1) if first else 6 * b + piece - 1

    def fill_out(b, piece, last=False):
        return 6 * b + piece + (5 if last else 9)

    with ExitStack() as ctx:
        def sb(name, shape, dt=F32):
            return ctx.enter_context(nc.sbuf_tensor(name, shape, dt))

        banks = [ctx.enter_context(nc.psum_tensor(f"bank{i}", [P, 512], F32)) for i in range(7)]
        max_bank = ctx.enter_context(nc.psum_tensor("max_bank", [P, 1024], BF16))
        s_bank, st_bank, o_bank, turn_bank, misc = banks[0:2], banks[2:4], banks[4], banks[5], banks[6]
        junk = sb("scores_junk", [P, 2, N])
        mx, mres = sb("maxima", [P, 2, 2, NQ]), sb("max_rest", [P, 2, NQ])
        mparts = sb("max_parts", [P, 2, 2, MR, NQ], BF16)
        mrows = sb("max_rows", [2 * MR * NQ, 2, P], BF16)
        probs = sb("probs", [P, 2, 2, N])
        outs, attn = sb("outs", [P, N]), sb("attn", [P, NQ, D])
        attn_t, rden = sb("attn_t", [P, N]), sb("rden", [P, NQ, 4])
        xn, xn_t = sb("xn", [P, NQ, D]), sb("xn_t", [P, N])
        stats, mv, rstd = sb("stats", [P, NQ, 6]), sb("mv", [P, NQ, 2]), sb("rstd", [P, NQ])
        stats2, mv2, rstd2, y = sb("stats2", [P, NQ, 6]), sb("mv2", [P, NQ, 2]), sb("rstd2", [P, NQ]), sb("y", [P, NQ, D])
        parts = {k: sb("parts_" + k, [P, MR, N], BF16) for k in "qk"}
        rest = {k: sb("rest_" + k, [P, N]) for k in "qk"}
        v_next = sb("v_next", [P, NQ, D])

        def ahead(b, u):
            return (b, u + 2) if u + 2 < PAIRS else (b + 1, u + 2 - PAIRS)

        def pe_scores(pe, b, u, i):
            qt = Q_ORDER[i]
            if i == 0 and u % 4 == 0:
                pe.wait_ge(s_half[u // 4], 64 * b + 64)
            for e in range(2):
                pe.wait_ge(s_tile_max, 64 * b + 8 * u + 2 * i + e + 7)
                pe.matmul(s_bank[e][:, 0:(qt + 1) * P], t.q_stack[64 * e:64 * e + KS, u, qt * P:(qt + 1) * P],
                          t.k_stack[64 * e:64 * e + KS, u, 0:(qt + 1) * P], start=True, stop=True).then_inc(s_scores, 1)

        def pe_turn_max(pe, b, u):
            pe.wait_ge(s_mparts, 8 * b + u + 1)
            pe.wait_ge(s_mt_copied, 8 * b + u + 1)
            pe.transpose(max_bank[0:2 * MR * NQ, 0:P], mparts[:, u % 2, :, :, :].rearrange("p e r q -> p (e r q)"),
                         t.ident16[:, :]).then_inc(s_mt, 1)

        def pe_scores_turned(pe, b, u, kt):
            if kt == 0:
                pe.wait_ge(s_mrow[u % 2], 128 * b + 32 * (u // 2) + 64)
            for e in range(2):
                pe.wait_ge(s_exp, 64 * b + 8 * u + 2 * kt + e + 7)
                pe.matmul(st_bank[e][:, 0:N - kt * P], t.k_stack[64 * e:64 * e + KS + MR, u, kt * P:(kt + 1) * P],
                          t.q_stack[64 * e:64 * e + KS + MR, u, kt * P:N], start=True, stop=True).then_inc(s_st, 1)

        def pe_values(pe, b, u, kt):
            if kt == 0 and u == 0:
                pe.wait_ge(s_vext, b + 1)
            if kt == 0 and u % 2 == 0:
                pe.wait_ge(s_o_copied, 4 * b + u // 2 + 1)
            pe.wait_ge(s_masked, 32 * b + 4 * u + kt + 1)
            for e in range(2):
                g = 2 * (u % 2) + e
                mm = pe.matmul(o_bank[32 * g:32 * g + 32, kt * P:N], t.v_ext[:, kt, 2 * u + e, :],
                               probs[:, kt % 2, e, 0:N - kt * P], start=(kt == 0), stop=(kt == NQ - 1),
                               skip_group_check=True)
            mm.then_inc(s_av, 1)

        def pe_turn_outputs(pe, b, w):
            pe.wait_ge(s_o_copied, 4 * b + w + 2)
            pe.wait_ge(s_o_norm, 4 * b + w + 1)
            for qt in range(NQ):
                mm = pe.transpose(turn_bank[:, qt * P:(qt + 1) * P], outs[:, qt * P:(qt + 1) * P], t.ident[:, :])
            mm.then_inc(s_o_turned, 1)

        def pe_project_in(pe, b, piece, first=False):
            pe.wait_ge(s_misc_read, fill_in(b, piece, first))
            if piece == 0:
                pe.wait_ge(s_xn, b + 1)
                for c in range(NQ):
                    mm = pe.transpose(misc[:, c * P:(c + 1) * P], xn[:, c, :], t.ident[:, :])
            elif piece < 3:
                mm = pe.matmul(misc[:, :], t.w_qkv[:, (piece - 1) * D:piece * D], xn_t[:, :], start=True, stop=True)
            else:
                for c in range(NQ):
                    mm = pe.matmul(misc[:, c * P:(c + 1) * P], xn_t[:, c * P:(c + 1) * P], t.w_qkv[:, 2 * D:3 * D],
                                   start=True, stop=True)
            mm.then_inc(s_misc, 1)

        def pe_project_out(pe, b, last):
            pe.wait_ge(s_o_norm, 4 * b + 5)
            pe.wait_ge(s_misc_read, fill_out(b, 0, last))
            for c in range(NQ):
                mm = pe.transpose(misc[:, c * P:(c + 1) * P], attn[:, c, :], t.ident[:, :])
            mm.then_inc(s_misc, 1)
            pe.wait_ge(s_misc_read, fill_out(b, 1, last))
            for c in range(NQ):
                mm = pe.matmul(misc[:, c * P:(c + 1) * P], attn_t[:, c * P:(c + 1) * P], t.w_proj[:, :],
                               start=True, stop=True)
            mm.then_inc(s_misc, 1)

        def pe_row(pe, b, last):
            for u in range(PAIRS):
                b2, u2 = ahead(b, u)
                more = not (last and u + 2 >= PAIRS)
                if not (last and u == PAIRS - 1):
                    pe_turn_max(pe, *((b, u + 1) if u + 1 < PAIRS else (b + 1, 0)))
                for kt in range(NQ):
                    pe_scores_turned(pe, b, u, kt)
                    if more:
                        pe_scores(pe, b2, u2, kt)
                    if kt >= 1:
                        pe_values(pe, b, u, kt - 1)
                    if kt == 2 and u in (2, 4, 6):
                        pe_turn_outputs(pe, b, u // 2 - 1)
                if not last and 1 <= u <= 4:
                    pe_project_in(pe, b + 1, u - 1)
                pe_values(pe, b, u, NQ - 1)
            pe_turn_outputs(pe, b, 3)
            pe_project_out(pe, b, last)

        def v_maxima(dve, b, u, i):
            width = (Q_ORDER[i] + 1) * P
            for e in range(2):
                await_(dve, passed["vector"], s_scores, 64 * b + 8 * u + 2 * i + e + 1)
                dve.tensor_tensor_reduce(junk[:, e, 0:width], s_bank[e][:, 0:width], t.causal[:, N - width:N], 1.0, LOWEST,
                                         ALU.add, ALU.max, mx[:, u % 2, e, Q_ORDER[i]:Q_ORDER[i] + 1]).then_inc(s_tile_max, 1)

        def v_split_maxima(dve, own, b, u):
            m, p = mx[:, u % 2, :, :], mparts[:, u % 2, :, :, :]
            dve.wait_ge(s_tile_max, 64 * b + 8 * u + 16)
            own(dve.tensor_scalar(p[:, :, 0, :], m, -1.0, None, ALU.mult))
            dve.wait_ge(s_vec, own.value())
            own(dve.scalar_tensor_tensor(mres[:, :, :], m, -1.0, p[:, :, 0, :], ALU.mult, ALU.subtract))
            dve.wait_ge(s_vec, own.value())
            own(dve.tensor_copy(p[:, :, 1, :], mres[:, :, :]))
            dve.wait_ge(s_vec, own.value())
            dve.tensor_tensor(p[:, :, 2, :], mres[:, :, :], p[:, :, 1, :], ALU.subtract).then_inc(s_mparts, 1)

        def v_norm_outputs(dve, own, b, w):
            await_(dve, passed["vector"], s_o_turned, 4 * b + w + 2)
            tb = turn_bank[:, :].rearrange("p (q g r) -> p q g r", q=NQ, g=4)
            own(dve.reciprocal(rden[:, :, :], tb[:, :, :, HD]))
            dve.wait_ge(s_vec, own.value())
            out = attn[:, :, 32 * w:32 * w + 32].rearrange("p q (g d) -> p q g d", d=HD)
            dve.tensor_tensor(out, tb[:, :, :, 0:HD], rden[:, :, :].unsqueeze(3).broadcast_to([P, NQ, 4, HD]),
                              ALU.mult).then_inc(s_o_norm, 1)

        def v_stats(dve, own, rows, st, m):
            for c in range(NQ):
                own(dve.bn_stats(st[:, c, :], rows(c)))
            await_(dve, passed["vector"], s_vec, own.value())
            for c in range(NQ):
                ins = dve.bn_aggr(m[:, c, :], st[:, c, :])
            ins.then_inc(s_var, 1)

        def norm_in(b, first=False):
            return 1 if first else 2 * b

        def norm_out(b, last=False):
            return 2 * b + (2 if last else 3)

        def v_norm_in(dve, b, first=False):
            await_(dve, passed["vector"], s_rstd, norm_in(b, first))
            for c in range(NQ):
                ins = dve.tensor_scalar(xn[:, c, :], x_t[:, c, b, :], mv[:, c, 0:1], rstd[:, c:c + 1],
                                        ALU.subtract, ALU.mult)
            ins.then_inc(s_xn, 1)

        def v_first_part(dve, own, b, k, first=False):
            fill = fill_in(b, 1 + "qk".index(k), first)
            await_(dve, passed["vector"], s_misc, fill)
            own(dve.tensor_copy(parts[k][:, 0, :], misc[:, :]))
            dve.wait_ge(s_vec, own.value())
            dve.tensor_tensor(rest[k][:, :], misc[:, :], parts[k][:, 0, :], ALU.subtract).then_inc(s_misc_read, 1)

        def v_values(dve, b, first=False):
            await_(dve, passed["vector"], s_misc, fill_in(b, 3, first))
            dve.tensor_copy(v_next[:, :, :], misc[:, :].rearrange("p (c d) -> p c d", d=D)).then_inc(s_misc_read, 1)

        def v_place_values(dve, b, first=False):
            dve.wait_ge(s_misc_read, fill_in(b, 3, first) + 1)
            await_(dve, passed["vector"], s_av, 32 * b + 2)
            dve.tensor_copy(t.v_ext[:, :, :, 0:HD].rearrange("p c h d -> p (c h) d"),
                            v_next[:, :, :].rearrange("p c (h d) -> p (c h) d", d=HD)).then_inc(s_vext, 1)

        def v_project_out(dve, own, b, last):
            await_(dve, passed["vector"], s_misc, fill_out(b, 1, last))
            v_stats(dve, own, lambda c: misc[:, c * P:(c + 1) * P], stats2, mv2)
            await_(dve, passed["vector"], s_rstd, norm_out(b, last))
            for c in range(NQ):
                ins = dve.tensor_scalar(y[:, c, :], misc[:, c * P:(c + 1) * P], mv2[:, c, 0:1], rstd2[:, c:c + 1],
                                        ALU.subtract, ALU.mult)
            fill = fill_out(b, 1, last)
            ins.then_inc(s_misc_read, 1)
            await_(dve, passed["vector"], s_misc_read, fill + 1)
            dve.tensor_tensor(x_t[:, :, b, :], x_t[:, :, b, :], y[:, :, :], ALU.add).then_inc(s_row_done, 1)

        def v_row(dve, b, last):
            own = Ticks(s_vec, VECTOR_STEPS_BEFORE + VECTOR_STEPS_ROW * b)
            for u in range(PAIRS):
                if u == 0 and not last:
                    v_stats(dve, own, lambda c: x_t[:, c, b + 1, :], stats, mv)
                if not last and u in (3, 4):
                    v_first_part(dve, own, b + 1, "qk"[u - 3])
                if not last and u == 5:
                    v_values(dve, b + 1)
                if not (last and u + 2 >= PAIRS):
                    for i in range(NQ):
                        v_maxima(dve, *ahead(b, u), i)
                    v_split_maxima(dve, own, *ahead(b, u))
                if u == 0 and not last:
                    v_norm_in(dve, b + 1)
                if u in (2, 4, 6):
                    v_norm_outputs(dve, own, b, u // 2 - 1)
            if not last:
                v_place_values(dve, b + 1)
            v_norm_outputs(dve, own, b, 3)
            v_project_out(dve, own, b, last)
            assert last or own.n == VECTOR_STEPS_ROW, own.n

        def a_copy_max(act, b, u):
            act.wait_ge(s_mrow[u % 2], 128 * b + 32 * (u // 2) + 32 if u >= 2 else 128 * b + 32)
            await_(act, passed["scalar"], s_mt, 8 * b + u + 1)
            act.activation(mrows[:, u % 2, :], max_bank[0:2 * MR * NQ, 0:P], ACT.Copy).then_inc(s_mt_copied, 1)

        def a_exp(act, b, u, kt):
            width = N - kt * P
            act.wait_ge(s_av, 32 * b + 4 * u + kt + 1)
            for e in range(2):
                await_(act, passed["scalar"], s_st, 64 * b + 8 * u + 2 * kt + e + 1)
                act.activation(probs[:, kt % 2, e, 0:width], st_bank[e][:, 0:width], ACT.Exp, scale=SCALE)\
                   .then_inc(s_exp, 1)

        def a_copy_outputs(act, b, w):
            act.wait_ge(s_o_turned, 4 * b + w + 1)
            await_(act, passed["scalar"], s_av, 32 * b + 8 * w + 10)
            act.activation(outs[:, :], o_bank[:, :], ACT.Copy).then_inc(s_o_copied, 1)

        def a_copy_misc(act, dst, fill):
            await_(act, passed["scalar"], s_misc, fill)
            act.activation(dst[:, :], misc[:, :], ACT.Copy).then_inc(s_misc_read, 1)

        def a_row(act, b, last):
            for u in range(PAIRS):
                if not (last and u == PAIRS - 1):
                    a_copy_max(act, *((b, u + 1) if u + 1 < PAIRS else (b + 1, 0)))
                for kt in range(NQ):
                    a_exp(act, b, u, kt)
                if u == 1 and not last:
                    a_copy_misc(act, xn_t, fill_in(b + 1, 0))
                if u % 2 == 1:
                    a_copy_outputs(act, b, u // 2)
            a_copy_misc(act, attn_t, fill_out(b, 0, last))

        def p_mask(pool, b, u, kt):
            await_(pool, passed["pool"], s_exp, 64 * b + 8 * u + 2 * kt + 10)
            diagonal = probs[:, kt % 2, :, 0:P]
            pool.affine_select(out=diagonal, in_=diagonal, compare_op=ALU.is_ge, fill=0.0, base=0,
                               pattern=[[0, 2], [1, P]], channel_multiplier=-1).then_inc(s_masked, 1)

        def p_rstd(pool, m, r, number):
            await_(pool, passed["pool"], s_var, number)
            pool.tensor_scalar(r[:, :], m[:, :, 1], EPS, None, ALU.add).then_inc(s_shifted, 1)
            await_(pool, passed["pool"], s_shifted, number)
            pool.tensor_tensor(r[:, :], r[:, :], t.minus_half[:, :], ALU.pow).then_inc(s_rstd, 1)

        def p_parts(pool, b, k, first=False):
            fill = fill_in(b, 1 + "qk".index(k), first)
            await_(pool, passed["pool"], s_misc_read, fill + 1)
            pool.tensor_copy(parts[k][:, 1, :], rest[k][:, :]).then_inc(s_pool, 1)
            await_(pool, passed["pool"], s_pool, 2 * b + "qk".index(k) + 1)
            pool.tensor_tensor(parts[k][:, 2, :], rest[k][:, :], parts[k][:, 1, :], ALU.subtract).then_inc(s_parts[k], 1)

        def p_row(pool, b, last):
            for u in range(PAIRS):
                for kt in range(NQ):
                    p_mask(pool, b, u, kt)
                    if kt == 1 and not last:
                        if u == 0:
                            p_rstd(pool, mv, rstd, norm_in(b + 1))
                        if u in (3, 4):
                            p_parts(pool, b + 1, "qk"[u - 3])
            p_rstd(pool, mv2, rstd2, norm_out(b, last))

        def d_max_rows(sp, b, u):
            await_(sp, passed["sync"], s_mt_copied, 8 * b + u + 2)
            for e in range(2):
                lo = 64 * e + KS
                sp.dma_start(t.q_stack[lo:lo + MR, u, :], mrows[MR * NQ * e:MR * NQ * (e + 1), u % 2, :])\
                  .then_inc(s_mrow[u % 2], 16)

        def d_write(sp, b, k):
            await_(sp, passed["sync"], s_parts[k], b + 1)
            for r in range(PARTS):
                sp.dma_start(scratch[k][:, r, :, :], parts[k][:, part_of[k][r], :]).then_inc(s_written, 16)

        def d_load(sp, half):
            for k, stack in (("q", t.q_stack), ("k", t.k_stack)):
                src = scratch[k].rearrange("(u e) r d n -> e (r d) u n", e=2)
                for e in range(2):
                    sp.dma_start(stack[64 * e:64 * e + KS, 4 * half:4 * half + 4, :], src[e][:, 4 * half:4 * half + 4, :])\
                      .then_inc(s_half[half], 16)

        def d_row(sp, b, last):
            for u in range(PAIRS):
                if not (last and u == PAIRS - 1):
                    d_max_rows(sp, *((b, u + 1) if u + 1 < PAIRS else (b + 1, 0)))
                if u == 0:
                    await_(sp, passed["sync"], s_exp, 64 * b + 8)
                    d_load(sp, 1)
                if u == 3 and not last:
                    await_(sp, passed["sync"], s_half[1], 64 * b + 64)
                    d_write(sp, b + 1, "q")
                if u == 4 and not last:
                    d_write(sp, b + 1, "k")
                if u == 5 and not last:
                    await_(sp, passed["sync"], s_written, 192 * b + 384)
                    await_(sp, passed["sync"], s_st, 64 * b + 32)
                    d_load(sp, 0)

        with nc.Block() as block:
            @block.tensor
            def _(pe):
                pe.sem_inc(s_av, 2)
                pe.sem_inc(s_o_turned, 1)
                for piece in range(4):
                    pe_project_in(pe, 0, piece, first=True)
                for u in range(2):
                    for i in range(NQ):
                        pe_scores(pe, 0, u, i)
                    if u == 0:
                        pe_turn_max(pe, 0, 0)
                with pe.Fori(0, S - 1) as b:
                    pe_row(pe, b, last=False)
                pe_row(pe, S - 1, last=True)

            @block.vector
            def _(dve):
                dve.sem_inc(s_tile_max, 8)
                dve.sem_inc(s_o_norm, 1)
                dve.sem_inc(s_misc_read, 1)
                own = Ticks(s_vec)
                dve.wait_ge(t.first_x_loaded, 16)
                v_stats(dve, own, lambda c: x_t[:, c, 0, :], stats, mv)
                v_norm_in(dve, 0, first=True)
                v_first_part(dve, own, 0, "q", first=True)
                v_first_part(dve, own, 0, "k", first=True)
                v_values(dve, 0, first=True)
                v_place_values(dve, 0, first=True)
                for u in range(2):
                    for i in range(NQ):
                        v_maxima(dve, 0, u, i)
                    v_split_maxima(dve, own, 0, u)
                assert own.n == VECTOR_STEPS_BEFORE, own.n
                dve.wait_ge(t.rest_x_loaded, 16 * (S - 1))
                with dve.Fori(0, S - 1) as b:
                    v_row(dve, b, last=False)
                v_row(dve, S - 1, last=True)

            @block.scalar
            def _(act):
                act.sem_inc(s_exp, 8)
                act.sem_inc(s_mt_copied, 1)
                act.sem_inc(s_o_copied, 1)
                a_copy_misc(act, xn_t, fill_in(0, 0, first=True))
                a_copy_max(act, 0, 0)
                with act.Fori(0, S - 1) as b:
                    a_row(act, b, last=False)
                a_row(act, S - 1, last=True)

            @block.gpsimd
            def _(pool):
                p_rstd(pool, mv, rstd, 1)
                p_parts(pool, 0, "q", first=True)
                p_parts(pool, 0, "k", first=True)
                with pool.Fori(0, S - 1) as b:
                    p_row(pool, b, last=False)
                p_row(pool, S - 1, last=True)

            @block.sync
            def _(sp):
                sp.sem_inc(s_mrow[0], 32)
                sp.sem_inc(s_mrow[1], 32)
                d_write(sp, 0, "q")
                d_write(sp, 0, "k")
                sp.wait_ge(s_written, 192)
                d_load(sp, 0)
                d_max_rows(sp, 0, 0)
                with sp.Fori(0, S - 1) as b:
                    d_row(sp, b, last=False)
                d_row(sp, S - 1, last=True)


R = S // C
G = 4
STEPS1, STEPS2 = 28, 81


def experts_and_mixing(nc, a, t, sem, out):
    x_out = out.rearrange("s (c p) d -> p c s d", p=P)
    mask_scratch = nc.dram_tensor("mask_scratch", [E, N], F32, kind="Internal").ap()

    s_vec1, s_vec2 = sem("vector_step1"), sem("vector_step2")
    s_var1, s_shift1, s_rstd1, s_xn1 = sem("variances1"), sem("shifted1"), sem("inverse_dev1"), sem("rows_normalised1")
    s_var2, s_shift2, s_rstd2, s_xn2 = sem("variances2"), sem("shifted2"), sem("inverse_dev2"), sem("rows_normalised2")
    s_m1, s_m1_read = sem("bank_m1_filled"), sem("bank_m1_read")
    s_m2, s_m2_read = sem("bank_m2_filled"), sem("bank_m2_read")
    s_gated, s_gexp, s_mask = sem("gates_shifted"), sem("gates_exp"), sem("mask_ready")
    s_mask_t, s_mask_out, s_mask_in = sem("mask_turned"), sem("mask_written"), sem("mask_spread")
    s_h, s_relu, s_y, s_y_read = sem("hidden_ready"), sem("relu_done"), sem("expert_product"), sem("expert_read")
    s_acc = sem("experts_summed")
    s_g, s_g_read, s_y2, s_y2_read = sem("bank_g_filled"), sem("bank_g_read"), sem("inner_product"), sem("inner_read")
    s_keep, s_xs = sem("rows_kept"), sem("rows_recalled")
    s_kv = sem("keys_values_ready")
    s_lg, s_tanh, s_shifted, s_p = sem("logits_ready"), sem("gates_tanh"), sem("logits_shifted"), sem("weights_exp")
    s_o, s_x2 = sem("mixed_ready"), sem("x_after_last")
    s_out = sem("rows_written")
    passed = {k: sem("passed1_" + k) for k in ("vector", "scalar", "pool", "sync")}

    with ExitStack() as ctx:
        def sb(name, shape, dt=F32):
            return ctx.enter_context(nc.sbuf_tensor(name, shape, dt))

        banks = [ctx.enter_context(nc.psum_tensor(f"rest_bank{i}", [P, 512], F32)) for i in range(8)]
        h_bank, y_bank, m1, g_bank, y2_bank, m2 = banks[0:2], banks[2], banks[3], banks[4:6], banks[6], banks[7]
        xn1, xn1_t, xn1_t2 = sb("xn1", [P, G, D]), sb("xn1_t", [P, N]), sb("xn1_t2", [P, N])
        stats1, mv1, rstd1 = sb("stats1", [P, G, 6]), sb("mv1", [P, G, 2]), sb("rstd1", [P, G])
        stats2, mv2, rstd2 = sb("stats2b", [P, G, 6]), sb("mv2b", [P, G, 2]), sb("rstd2b", [P, G])
        gate, top, shifted, keep = sb("gate", [P, G, E]), sb("top", [P, G, 8]), sb("shifted", [P, G, E]), sb("keep", [P, G, E])
        gexp, gsum, mask_t = sb("gexp", [P, G, E]), sb("gsum", [P, G]), sb("mask_t", [E, N])
        mask_all = sb("mask_all", [P, E, N])
        hidden, term, total = sb("hidden", [P, 4, N]), sb("term", [P, N]), sb("total", [P, N])
        y1 = sb("y1", [P, G, D])
        kv = sb("kv", [P, 2 * S, 2 * D])
        kept, xs = sb("kept", [P, R, N]), sb("xs", [P, N])
        q = sb("q", [P, G, D])
        kinks = sb("kinks", [P, 2 * NPOS, G, H])
        prod = sb("prod", [P, S, D])
        logits, pos, acc = sb("logits", [P, S, G, H]), sb("pos", [P, S, G, H]), sb("acc", [P, S, G, H])
        kterm = logits
        peak, wsum = sb("peak", [P, G * H]), sb("wsum", [P, G * H])
        o, o_t, y2 = sb("o", [P, G, D]), sb("o_t", [P, N]), sb("y2", [P, G, D])
        hidden2 = sb("hidden2", [P, 4, N])
        z_t = xs

        def tiles(c, r):
            return t.x[:, bass.ds(16 * c + 4 * r, G), :]

        def pe_norm1(pe, i, fill, number):
            pe.wait_ge(s_m1_read, 7 * i + fill)
            pe.wait_ge(s_xn1, 2 * i + number)
            for j in range(G):
                mm = pe.transpose(m1[:, j * P:(j + 1) * P], xn1[:, j, :], t.ident[:, :])
            mm.then_inc(s_m1, 1)

        def pe_gates(pe, i):
            pe.wait_ge(s_m1_read, 7 * i + 2)
            for j in range(G):
                mm = pe.matmul(m1[:, j * E:(j + 1) * E], xn1_t[:, j * P:(j + 1) * P], t.w_gate[:, :], start=True, stop=True)
            mm.then_inc(s_m1, 1)

        def pe_mask(pe, i):
            pe.wait_ge(s_m1_read, 7 * i + 3)
            pe.wait_ge(s_mask, i + 1)
            for j in range(G):
                mm = pe.transpose(m1[0:E, j * P:(j + 1) * P], gexp[:, j, :], t.ident[:, :])
            mm.then_inc(s_m1, 1)

        def pe_hidden(pe, i, k):
            pe.wait_ge(s_relu, 32 * i + k + 1)
            pe.matmul(h_bank[k % 2][:, :], t.w1[:, k // F, (k % F) * P:(k % F + 1) * P], xn1_t[:, :],
                      start=True, stop=True).then_inc(s_h, 1)

        def pe_expert(pe, i, k):
            if k % F == 0:
                pe.wait_ge(s_y_read, 8 * i + k // F + 1)
            pe.wait_ge(s_relu, 32 * i + k + 3)
            pe.matmul(y_bank[:, :], t.w2[:, k, :], hidden[:, k % 4, :], start=(k % F == 0), stop=(k % F == F - 1))\
              .then_inc(s_y, 1)

        def pe_experts(pe, i):
            for k in range(E * F + 2):
                if k < E * F:
                    pe_hidden(pe, i, k)
                if k >= 2:
                    pe_expert(pe, i, k - 2)

        def pe_experts_out(pe, i):
            pe.wait_ge(s_m1_read, 7 * i + 4)
            pe.wait_ge(s_acc, i + 1)
            for j in range(G):
                mm = pe.transpose(m1[:, j * P:(j + 1) * P], total[:, j * P:(j + 1) * P], t.ident[:, :])
            mm.then_inc(s_m1, 1)

        def pe_keys_values(pe, i):
            for half in range(2):
                pe.wait_ge(s_m1_read, 7 * i + 6 + half)
                for j in range(2):
                    g = 2 * half + j
                    mm = pe.matmul(m1[:, j * 2 * D:(j + 1) * 2 * D], xn1_t2[:, g * P:(g + 1) * P], t.w_at[:, D:3 * D],
                                   start=True, stop=True)
                mm.then_inc(s_m1, 1)

        def pe_queries(pe, i):
            pe.wait_ge(s_xs, i + 1)
            pe.wait_ge(s_m2_read, 5 * i + 1)
            for j in range(G):
                mm = pe.matmul(m2[:, j * P:(j + 1) * P], xs[:, j * P:(j + 1) * P], t.w_at[:, 0:D], start=True, stop=True)
            mm.then_inc(s_m2, 1)
            for j in range(G):
                pe.wait_ge(s_g_read, 12 * i + j + 1)
                pe.matmul(g_bank[j % 2][:, :], xs[:, j * P:(j + 1) * P], t.w_kink[:, :], start=True, stop=True)\
                  .then_inc(s_g, 1)

        def pe_mixed_out(pe, i):
            pe.wait_ge(s_o, i + 1)
            pe.wait_ge(s_m2_read, 5 * i + 2)
            for j in range(G):
                mm = pe.transpose(m2[:, j * P:(j + 1) * P], o[:, j, :], t.ident[:, :])
            mm.then_inc(s_m2, 1)
            pe.wait_ge(s_m2_read, 5 * i + 3)
            for j in range(G):
                mm = pe.matmul(m2[:, j * P:(j + 1) * P], o_t[:, j * P:(j + 1) * P], t.w_o[:, :], start=True, stop=True)
            mm.then_inc(s_m2, 1)

        def pe_last(pe, i):
            pe.wait_ge(s_xn2, i + 1)
            pe.wait_ge(s_m2_read, 5 * i + 4)
            for j in range(G):
                mm = pe.transpose(m2[:, j * P:(j + 1) * P], o[:, j, :], t.ident[:, :])
            mm.then_inc(s_m2, 1)
            pe.wait_ge(s_m2_read, 5 * i + 5)
            for k in range(K2 + 2):
                if k < K2:
                    pe.wait_ge(s_g_read, 12 * i + 4 + k + 1)
                    pe.matmul(g_bank[k % 2][:, :], t.w_in[:, k * P:(k + 1) * P], o_t[:, :], start=True, stop=True)\
                      .then_inc(s_g, 1)
                if k >= 2:
                    if k == 2:
                        pe.wait_ge(s_y2_read, i + 1)
                    pe.wait_ge(s_g_read, 12 * i + 4 + k - 2 + 3)
                    pe.matmul(y2_bank[:, :], t.w_out[:, k - 2, :], hidden2[:, (k - 2) % 4, :],
                              start=(k == 2), stop=(k == K2 + 1)).then_inc(s_y2, 1)
            pe.wait_ge(s_y2_read, i + 2)
            for j in range(G):
                mm = pe.transpose(m2[:, j * P:(j + 1) * P], z_t[:, j * P:(j + 1) * P], t.ident[:, :])
            mm.then_inc(s_m2, 1)

        def pe_group(pe, c, r, one, two):
            i, i2 = 4 * c + r, 4 * (c - 1) + r
            if one:
                pe_norm1(pe, i, 1, 1)
                pe_gates(pe, i)
            if two:
                pe_queries(pe, i2)
            if one:
                pe_mask(pe, i)
                pe_experts(pe, i)
                pe_experts_out(pe, i)
            if two:
                pe_mixed_out(pe, i2)
            if one:
                pe_norm1(pe, i, 5, 2)
                pe_keys_values(pe, i)
            if two:
                pe_last(pe, i2)

        def v_stats(dve, own, s_vec, rows, st, m, s_var):
            for j in range(G):
                own(dve.bn_stats(st[:, j, :], rows(j)))
            await_(dve, passed["vector"], s_vec, own.value())
            for j in range(G):
                ins = dve.bn_aggr(m[:, j, :], st[:, j, :])
            ins.then_inc(s_var, 1)

        def v_scale(dve, s_rstd, number, rows, dst, m, r):
            await_(dve, passed["vector"], s_rstd, number)
            for j in range(G):
                ins = dve.tensor_scalar(dst[:, j, :], rows(j), m[:, j, 0:1], r[:, j:j + 1], ALU.subtract, ALU.mult)
            return ins

        def v_norm1(dve, own, c, r, number):
            i = 4 * c + r
            rows = lambda j: t.x[:, 16 * c + 4 * r + j, :]
            v_stats(dve, own, s_vec1, rows, stats1, mv1, s_var1)
            v_scale(dve, s_rstd1, 3 * i + (1 if number == 1 else 3), rows, xn1, mv1, rstd1).then_inc(s_xn1, 1)

        def v_gates(dve, own, i):
            await_(dve, passed["vector"], s_m1, 7 * i + 2)
            dve.tensor_copy(gate[:, :, :], m1[:, 0:G * E].rearrange("p (g e) -> p g e", e=E)).then_inc(s_m1_read, 1)
            await_(dve, passed["vector"], s_m1_read, 7 * i + 3)
            for j in range(G):
                own(dve.max(top[:, j, :], gate[:, j, :]))
            await_(dve, passed["vector"], s_vec1, own.value())
            dve.tensor_tensor(shifted[:, :, :], gate[:, :, :], top[:, :, 0:1].broadcast_to([P, G, E]), ALU.subtract)\
               .then_inc(s_gated, 1)
            own(dve.tensor_tensor(keep[:, :, :], gate[:, :, :], top[:, :, 1:2].broadcast_to([P, G, E]), ALU.is_ge))
            dve.wait_ge(s_vec1, own.value())
            await_(dve, passed["vector"], s_gexp, i + 1)
            own(dve.tensor_tensor(gexp[:, :, :], gexp[:, :, :], keep[:, :, :], ALU.mult))
            dve.wait_ge(s_vec1, own.value())
            own(dve.tensor_reduce(gsum[:, :], gexp[:, :, :], AX.X, ALU.add))
            dve.wait_ge(s_vec1, own.value())
            own(dve.reciprocal(gsum[:, :], gsum[:, :]))
            dve.wait_ge(s_vec1, own.value())
            own(dve.tensor_scalar(gsum[:, :], gsum[:, :], 1.0 / E, None, ALU.mult))
            dve.wait_ge(s_vec1, own.value())
            dve.tensor_tensor(gexp[:, :, :], gexp[:, :, :], gsum[:, :].unsqueeze(2).broadcast_to([P, G, E]), ALU.mult)\
               .then_inc(s_mask, 1)

        def v_expert(dve, own, i, e):
            if e == 0:
                dve.wait_ge(s_mask_in, 16 * i + 32)
            await_(dve, passed["vector"], s_y, 32 * i + 4 * e + 8)
            dst = total if e == 0 else term
            dve.scalar_tensor_tensor(dst[:, :], y_bank[:, :], t.b2[:, e:e + 1], mask_all[:, e, :], ALU.add, ALU.mult)\
               .then_inc(s_y_read, 1)
            if e >= 1:
                dve.wait_ge(s_y_read, 8 * i + e + 2)
                if e == E - 1:
                    dve.tensor_tensor(total[:, :], total[:, :], term[:, :], ALU.add).then_inc(s_acc, 1)
                else:
                    own(dve.tensor_tensor(total[:, :], total[:, :], term[:, :], ALU.add))
                    dve.wait_ge(s_vec1, own.value())

        def v_experts_out(dve, own, c, r):
            i = 4 * c + r
            await_(dve, passed["vector"], s_m1, 7 * i + 4)
            rows = lambda j: m1[:, j * P:(j + 1) * P]
            v_stats(dve, own, s_vec1, rows, stats1, mv1, s_var1)
            ins = v_scale(dve, s_rstd1, 3 * i + 2, rows, y1, mv1, rstd1)
            ins.then_inc(s_m1_read, 1)
            await_(dve, passed["vector"], s_m1_read, 7 * i + 5)
            own(dve.tensor_tensor(tiles(c, r), tiles(c, r), y1[:, :, :], ALU.add))
            await_(dve, passed["vector"], s_vec1, own.value())

        def v_keys_values(dve, own, c, r, slot):
            i = 4 * c + r
            for half in range(2):
                await_(dve, passed["vector"], s_m1, 7 * i + 6 + half)
                ins = dve.tensor_tensor(kv[:, bass.ds(slot * 16 + 4 * r + 2 * half, 2), :],
                                        m1[:, :].rearrange("p (g d) -> p g d", g=2),
                                        t.b_at[:, D:3 * D].unsqueeze(1).broadcast_to([P, 2, 2 * D]), ALU.add)
                ins.then_inc(s_m1_read, 1)

        def v_queries(dve, own, i):
            await_(dve, passed["vector"], s_m2, 5 * i + 1)
            dve.tensor_tensor(q[:, :, :], m2[:, :].rearrange("p (g d) -> p g d", g=G),
                              t.b_at[:, 0:D].unsqueeze(1).broadcast_to([P, G, D]), ALU.add).then_inc(s_m2_read, 1)
            for j in range(G):
                await_(dve, passed["vector"], s_g, 12 * i + j + 1)
                dve.tensor_tensor(kinks[:, :, j, :], g_bank[j % 2][:, :].rearrange("p (n h) -> p n h", h=H),
                                  t.b_kink[:, :].rearrange("p (n h) -> p n h", h=H), ALU.add).then_inc(s_g_read, 1)

        def v_logits(dve, own, i, slot, j):
            if j == 0:
                dve.wait_ge(s_m2_read, 5 * i + 2)
            keys = kv[:, bass.ds(slot * 16, S), 0:D]
            own(dve.tensor_tensor(prod[:, :, :], q[:, j, :].unsqueeze(1).broadcast_to([P, S, D]), keys, ALU.mult))
            dve.wait_ge(s_vec2, own.value())
            ins = dve.tensor_reduce(logits[:, :, j, :], prod[:, :, :].rearrange("p t (h d) -> p t h d", d=HD),
                                    AX.X, ALU.add)
            if j == G - 1:
                ins.then_inc(s_lg, 1)
                dve.wait_ge(s_lg, i + 1)
            else:
                own(ins)
                dve.wait_ge(s_vec2, own.value())

        def v_positions(dve, own, i):
            await_(dve, passed["vector"], s_tanh, i + 1)
            flat = pos[:, :, :, :].rearrange("p t g h -> p t (g h)")
            own(dve.tensor_scalar(flat, flat, 0.5, 0.5, ALU.mult, ALU.add))
            dve.wait_ge(s_vec2, own.value())
            for k in range(S - 2, -1, -1):
                own(dve.tensor_tensor(flat[:, k, :], flat[:, k, :], flat[:, k + 1, :], ALU.add))
                dve.wait_ge(s_vec2, own.value())
            dve.wait_ge(s_g_read, 12 * i + 6)
            own(dve.scalar_tensor_tensor(acc[:, :, :, :].rearrange("p t g h -> p (t g h)"),
                                         logits[:, :, :, :].rearrange("p t g h -> p (t g h)"), SCALE,
                                         kinks[:, NPOS:, :, :].rearrange("p t g h -> p (t g h)"), ALU.mult, ALU.add))
            dve.wait_ge(s_vec2, own.value())

        def v_kink(dve, own, n):
            keys = S - n
            f = lambda x: x[:, 0:keys, :, :].rearrange("p t g h -> p t (g h)")
            height = kinks[:, n, :, :].rearrange("p g h -> p (g h)").unsqueeze(1).broadcast_to([P, keys, G * H])
            own(dve.scalar_tensor_tensor(f(kterm), f(pos), float(n), height, ALU.max, ALU.mult))
            dve.wait_ge(s_vec2, own.value())
            own(dve.tensor_tensor(f(acc), f(acc), f(kterm), ALU.add))
            dve.wait_ge(s_vec2, own.value())

        def v_softmax(dve, own, i):
            by_key = lambda x: x[:, :, :, :].rearrange("p t g h -> p (g h) t")
            flat = lambda x: x[:, :, :, :].rearrange("p t g h -> p t (g h)")
            own(dve.tensor_reduce(peak[:, :], by_key(acc), AX.X, ALU.max))
            dve.wait_ge(s_vec2, own.value())
            dve.tensor_tensor(flat(acc), flat(acc), peak[:, :].unsqueeze(1).broadcast_to([P, S, G * H]), ALU.subtract)\
               .then_inc(s_shifted, 1)

        def v_weight_sums(dve, own, i):
            by_key = lambda x: x[:, :, :, :].rearrange("p t g h -> p (g h) t")
            await_(dve, passed["vector"], s_p, i + 1)
            own(dve.tensor_reduce(wsum[:, :], by_key(acc), AX.X, ALU.add))
            dve.wait_ge(s_vec2, own.value())
            own(dve.reciprocal(wsum[:, :], wsum[:, :]))
            dve.wait_ge(s_vec2, own.value())

        def v_values(dve, own, i, slot, j):
            values = kv[:, bass.ds(slot * 16, S), D:2 * D].rearrange("p t (h d) -> p t h d", d=HD)
            weights = acc[:, :, j, :].unsqueeze(3).broadcast_to([P, S, H, HD])
            own(dve.tensor_tensor(prod[:, :, :].rearrange("p t (h d) -> p t h d", d=HD), weights, values, ALU.mult))
            dve.wait_ge(s_vec2, own.value())
            own(dve.tensor_reduce(o[:, j, :], prod[:, :, :].rearrange("p t c -> p c t"), AX.X, ALU.add))
            dve.wait_ge(s_vec2, own.value())
            if j == G - 1:
                heads = o[:, :, :].rearrange("p g (h d) -> p (g h) d", d=HD)
                dve.tensor_tensor(heads, heads, wsum[:, :].unsqueeze(2).broadcast_to([P, G * H, HD]), ALU.mult)\
                   .then_inc(s_o, 1)

        def v_mixed_out(dve, own, c, r):
            i = 4 * c + r
            await_(dve, passed["vector"], s_m2, 5 * i + 3)
            dve.tensor_tensor(y2[:, :, :], m2[:, :].rearrange("p (g d) -> p g d", g=G),
                              t.b_o[:, :].unsqueeze(1).broadcast_to([P, G, D]), ALU.add).then_inc(s_m2_read, 1)
            await_(dve, passed["vector"], s_m2_read, 5 * i + 4)
            rows = lambda j: y2[:, j, :]
            v_stats(dve, own, s_vec2, rows, stats2, mv2, s_var2)
            own(v_scale(dve, s_rstd2, 3 * i + 1, rows, y2, mv2, rstd2))
            dve.wait_ge(s_vec2, own.value())
            own(dve.tensor_tensor(tiles(c, r), tiles(c, r), y2[:, :, :], ALU.add))
            await_(dve, passed["vector"], s_vec2, own.value())
            rows = lambda j: t.x[:, 16 * c + 4 * r + j, :]
            v_stats(dve, own, s_vec2, rows, stats2, mv2, s_var2)
            v_scale(dve, s_rstd2, 3 * i + 2, rows, o, mv2, rstd2).then_inc(s_xn2, 1)

        def v_last(dve, own, c, r):
            i = 4 * c + r
            await_(dve, passed["vector"], s_m2, 5 * i + 5)
            rows = lambda j: m2[:, j * P:(j + 1) * P]
            v_stats(dve, own, s_vec2, rows, stats2, mv2, s_var2)
            v_scale(dve, s_rstd2, 3 * i + 3, rows, y2, mv2, rstd2).then_inc(s_m2_read, 1)
            await_(dve, passed["vector"], s_m2_read, 5 * i + 6)
            dve.tensor_tensor(tiles(c, r), tiles(c, r), y2[:, :, :], ALU.add).then_inc(s_x2, 1)

        def v_group(dve, c, r, one, two):
            i, i2, c2 = 4 * c + r, 4 * (c - 1) + r, c - 1
            slot, slot2 = c % 2, (c - 1) % 2
            own1, own2 = Ticks(s_vec1, STEPS1 * i), Ticks(s_vec2, STEPS2 * i2)
            if one:
                v_norm1(dve, own1, c, r, 1)
            if two:
                v_queries(dve, own2, i2)
            if one:
                v_gates(dve, own1, i)
            for e in range(E):
                if two:
                    if e < 4:
                        v_logits(dve, own2, i2, slot2, e)
                    if e == 4:
                        v_positions(dve, own2, i2)
                        for n in range(0, 4):
                            v_kink(dve, own2, n)
                    if e == 5:
                        for n in range(4, NPOS):
                            v_kink(dve, own2, n)
                        v_softmax(dve, own2, i2)
                    if e == 6:
                        v_weight_sums(dve, own2, i2)
                    if e >= 6:
                        for j in range(2 * (e - 6), 2 * (e - 6) + 2):
                            v_values(dve, own2, i2, slot2, j)
                if one:
                    v_expert(dve, own1, i, e)
            if one:
                v_experts_out(dve, own1, c, r)
            if two:
                v_mixed_out(dve, own2, c2, r)
            if one:
                v_norm1(dve, own1, c, r, 2)
                v_keys_values(dve, own1, c, r, slot)
            if two:
                v_last(dve, own2, c2, r)
            assert not one or own1.n == STEPS1, own1.n
            assert not two or own2.n == STEPS2, own2.n

        def a_copy(act, dst, bank, s_fill, fill, s_read):
            await_(act, passed["scalar"], s_fill, fill)
            act.activation(dst, bank, ACT.Copy).then_inc(s_read, 1)

        def a_group(act, c, r, one, two):
            i, i2 = 4 * c + r, 4 * (c - 1) + r
            if one:
                a_copy(act, xn1_t[:, :], m1[:, :], s_m1, 7 * i + 1, s_m1_read)
                await_(act, passed["scalar"], s_gated, i + 1)
                act.activation(gexp[:, :, :], shifted[:, :, :], ACT.Exp).then_inc(s_gexp, 1)
                a_copy(act, mask_t[:, :], m1[0:E, :], s_m1, 7 * i + 3, s_m1_read)
            for k in range(E * F):
                if one:
                    act.wait_ge(s_y, 32 * i + k + 1)
                    await_(act, passed["scalar"], s_h, 32 * i + k + 1)
                    act.activation(hidden[:, k % 4, :], h_bank[k % 2][:, :], ACT.Relu, bias=t.b1[:, k:k + 1])\
                       .then_inc(s_relu, 1)
                if two and k == 16:
                    await_(act, passed["scalar"], s_lg, i2 + 1)
                    act.activation(pos[:, :, :, :], logits[:, :, :, :], ACT.Tanh, scale=0.5 * SCALE).then_inc(s_tanh, 1)
                if two and k == 25:
                    await_(act, passed["scalar"], s_shifted, i2 + 1)
                    act.activation(acc[:, :, :, :], acc[:, :, :, :], ACT.Exp).then_inc(s_p, 1)
            if two:
                a_copy(act, o_t[:, :], m2[:, :], s_m2, 5 * i2 + 2, s_m2_read)
            if one:
                a_copy(act, xn1_t2[:, :], m1[:, :], s_m1, 7 * i + 5, s_m1_read)
            if two:
                a_copy(act, o_t[:, :], m2[:, :], s_m2, 5 * i2 + 4, s_m2_read)
                for k in range(K2):
                    act.wait_ge(s_y2, 8 * i2 + k + 1)
                    await_(act, passed["scalar"], s_g, 12 * i2 + 5 + k)
                    act.activation(hidden2[:, k % 4, :], g_bank[k % 2][:, :], ACT.Relu, bias=t.b_in[:, k:k + 1])\
                       .then_inc(s_g_read, 1)
                await_(act, passed["scalar"], s_y2, 8 * i2 + 12)
                act.activation(z_t[:, :], y2_bank[:, :], ACT.Identity, bias=t.b_out[:, 0:1]).then_inc(s_y2_read, 1)

        def p_rstd(pool, m, r, s_var, s_shift, s_rstd, number):
            await_(pool, passed["pool"], s_var, number)
            pool.tensor_scalar(r[:, :], m[:, :, 1], EPS, None, ALU.add).then_inc(s_shift, 1)
            await_(pool, passed["pool"], s_shift, number)
            pool.tensor_tensor(r[:, :], r[:, :], t.minus_half[:, :], ALU.pow).then_inc(s_rstd, 1)

        def p_group(pool, c, r, one, two):
            i, i2 = 4 * c + r, 4 * (c - 1) + r
            norm1 = lambda n: p_rstd(pool, mv1, rstd1, s_var1, s_shift1, s_rstd1, 3 * i + n)
            norm2 = lambda n: p_rstd(pool, mv2, rstd2, s_var2, s_shift2, s_rstd2, 3 * i2 + n)
            if two:
                pool.tensor_copy(xs[:, :], kept[:, r, :]).then_inc(s_xs, 1)
            if one:
                norm1(1)
                norm1(2)
            if two:
                norm2(1)
                norm2(2)
            if one:
                norm1(3)
                if two:
                    pool.wait_ge(s_xs, i2 + 1)
                await_(pool, passed["pool"], s_m1_read, 7 * i + 6)
                pool.tensor_copy(kept[:, r, :], xn1_t2[:, :]).then_inc(s_keep, 1)
            if two:
                norm2(3)

        def d_group(sp, c, r, one, two):
            i, i2 = 4 * c + r, 4 * (c - 1) + r
            if one:
                await_(sp, passed["sync"], s_m1_read, 7 * i + 4)
                await_(sp, passed["sync"], s_mask_in, 16 * i + 16)
                sp.dma_start(mask_scratch, mask_t[:, :]).then_inc(s_mask_out, 16)
                await_(sp, passed["sync"], s_y_read, 8 * i + 1)
                await_(sp, passed["sync"], s_mask_out, 16 * i + 16)
                src = mask_scratch.rearrange("(o e) n -> o e n", o=1).broadcast_to([P, E, N])
                sp.dma_start(mask_all[:, :, :], src).then_inc(s_mask_in, 16)
            if two:
                await_(sp, passed["sync"], s_x2, i2 + 1)
                sp.dma_start(x_out[:, c - 1, bass.ds(4 * r, G), :], tiles(c - 1, r)).then_inc(s_out, 16)

        def all_groups(eng, group):
            with eng.Fori(0, R) as r:
                group(eng, 0, r, True, False)
            with eng.Fori(1, C) as c:
                with eng.Fori(0, R) as r:
                    group(eng, c, r, True, True)
            with eng.Fori(0, R) as r:
                group(eng, C, r, False, True)

        with nc.Block() as block:
            @block.tensor
            def _(pe):
                pe.sem_inc(s_y, 4)
                pe.sem_inc(s_y2, 4)
                all_groups(pe, pe_group)

            @block.vector
            def _(dve):
                dve.sem_inc(s_y_read, 1)
                all_groups(dve, v_group)

            @block.scalar
            def _(act):
                for s, n in ((s_m1_read, 1), (s_m2_read, 1), (s_relu, 2), (s_g_read, 2), (s_y2_read, 1)):
                    act.sem_inc(s, n)
                all_groups(act, a_group)

            @block.gpsimd
            def _(pool):
                all_groups(pool, p_group)

            @block.sync
            def _(sp):
                sp.sem_inc(s_mask_in, 16)
                all_groups(sp, d_group)
                sp.wait_ge(s_out, 16 * C * R)


def build(nc, a, out):
    with ExitStack() as ctx:
        class t:
            pass

        def sb(name, shape, dt=F32):
            return ctx.enter_context(nc.sbuf_tensor(name, shape, dt))

        def sem(name):
            return ctx.enter_context(nc.semaphore(name))

        t.x = sb("x", [P, T, D])
        t.ident, t.ones, t.ident16 = sb("ident", [P, P]), sb("ones", [P, P]), sb("ident16", [P, P], BF16)
        t.w_at, t.b_at = sb("w_at", [P, 3 * D]), sb("b_at", [P, 3 * D])
        t.w_kink, t.b_kink = sb("w_kink", [P, 2 * NPOS * H]), sb("b_kink", [P, 2 * NPOS * H])
        t.w_o, t.b_o = sb("w_o", [P, D]), sb("b_o", [P, D])
        t.w_gate, t.w1, t.w2 = sb("w_gate", [P, E]), sb("w1", [P, E, HID]), sb("w2", [P, E * F, D])
        t.b1, t.b2 = sb("b1", [P, E * F]), sb("b2", [P, E])
        t.w_in, t.b_in = sb("w_in", [P, M2 * J2]), sb("b_in", [P, K2])
        t.w_out, t.b_out = sb("w_out", [P, K2, D]), sb("b_out", [P, 1])
        t.minus_half = sb("minus_half", [P, C])
        t.first_x_loaded, t.rest_x_loaded = sem("first_x_loaded"), sem("rest_x_loaded")
        with ExitStack() as first:
            def sb0(name, shape, dt=F32):
                return first.enter_context(nc.sbuf_tensor(name, shape, dt))

            t.w_qkv, t.w_proj = sb0("w_qkv", [P, 3 * D]), sb0("w_proj", [P, D])
            t.causal = sb0("causal", [P, N])
            t.q_stack, t.k_stack = sb0("q_stack", [P, PAIRS, N], BF16), sb0("k_stack", [P, PAIRS, N], BF16)
            t.v_ext = sb0("v_ext", [P, NQ, H, 32])
            load_and_prepare(nc, a, t, sem)
            causal_attention(nc, a, t, sem)
        experts_and_mixing(nc, a, t, sem, out)


_INS = [
    'L0_attn_batch', 'L0_attn_W_qkv', 'L0_attn_u_qkv', 'L0_attn_sigma_qkv',
    'L0_attn_W_proj', 'L0_attn_u_proj', 'L0_attn_sigma_proj', 'L0_ffn_W_gate',
    'L0_ffn_W1', 'L0_ffn_b1', 'L0_ffn_W2', 'L0_ffn_b2',
    'L1_attn_Wq', 'L1_attn_bq', 'L1_attn_Wk', 'L1_attn_bk',
    'L1_attn_Wv', 'L1_attn_bv', 'L1_attn_Wo', 'L1_attn_bo',
    'L1_attn_pos_emb', 'L1_ffn_Win', 'L1_ffn_bin_', 'L1_ffn_W1',
    'L1_ffn_b1', 'L1_ffn_W2', 'L1_ffn_b2', 'L1_ffn_Wout',
    'L1_ffn_bout',
]
_OUT = (S, N, D)


def kernel(**inputs):
    import numpy as _np
    import concourse.bacc as _bacc
    from concourse import mybir as _mybir
    from concourse.bass_utils import run_bass_kernel_spmd as _run

    nc = _bacc.Bacc("TRN2", target_bir_lowering=False, num_devices=1)
    arrays, a = {}, {}
    for name in _INS:
        v = _np.ascontiguousarray(inputs[name])
        arrays[f"in_{name}_dram"] = v
        a[name] = nc.dram_tensor(f"in_{name}_dram", v.shape, _mybir.dt.from_np(v.dtype), kind="ExternalInput").ap()
    out = nc.dram_tensor("out_dram", _OUT, _mybir.dt.float32, kind="ExternalOutput").ap()
    build(nc, a, out)
    r = _run(nc, [arrays], core_ids=[0])
    return r.results[0]["out_dram"]
```

```python
import concourse.bass as bass
from concourse import mybir
from contextlib import ExitStack

F32 = mybir.dt.float32
BF16 = mybir.dt.bfloat16
ALU = mybir.AluOpType
ACT = mybir.ActivationFunctionType
AX = mybir.AxisListType

P = 128
S, N, D = 16, 512, 128
C = N // P
T = S * C
H, HD = 16, 8
SCALE = HD ** -0.5
EPS = 1e-5
E, HID = 8, 512
F = HID // P
PARTS = 6
KS = PARTS * HD
MR = 3
NPOS = S
M2, J2 = 64, 16
K2 = M2 * J2 // P
NEG = -3.0e38
LOWEST = -3.4028e38


class Ticks:

    def __init__(self, sem, base=0):
        self.sem, self.base, self.n = sem, base, 0

    def __call__(self, instruction, by=1):
        instruction.then_inc(self.sem, by)
        self.n += by

    def value(self):
        return self.base + self.n


def await_(eng, passed, sem, value):
    eng.wait_ge(sem, value)
    eng.sem_inc(passed, 1)


def load_and_prepare(nc, a, t, sem):
    x_in = a["L0_attn_batch"].rearrange("s (c p) d -> s p c d", p=P)
    x_sb = t.x[:, :, :].rearrange("p (c s) d -> p c s d", s=S)
    s_norm, s_attn, s_ffn = sem("norm_weights_loaded"), sem("attn_weights_loaded"), sem("ffn_weights_loaded")
    s_pool, s_vec, s_pe, s_act = sem("pool_step"), sem("vector_step"), sem("tensor_step"), sem("scalar_step")
    norm_loads, attn_loads, ffn_loads = [], [], []

    def row(v, n):
        return v.rearrange("(o n) -> o n", o=1).broadcast_to([P, n])

    with ExitStack() as ctx:
        def sb(name, shape, dt=F32):
            return ctx.enter_context(nc.sbuf_tensor(name, shape, dt))

        def ps(name):
            return ctx.enter_context(nc.psum_tensor(name, [P, 512], F32))

        u_row, up_row = sb("u_row", [P, 384]), sb("up_row", [P, D])
        sigma, norms, junk = sb("sigma", [P, 2]), sb("norms", [P, 8]), sb("junk", [P, 384])
        wu, wu_rep = sb("wu", [P, 2]), sb("wu_rep", [P, 2, P])
        b1_rows, b2_rows = sb("b1_rows", [E * F, P]), sb("b2_rows", [E, D])
        wq_t, pe_rep, kink = sb("wq_t", [P, P]), sb("pe_rep", [P, NPOS + 2]), sb("kink", [P, 2 * NPOS])
        blocks, bq_col, bq_rep = sb("blocks", [P, 2 * NPOS, H]), sb("bq_col", [P, 1]), sb("bq_rep", [P, P])
        head_of = sb("head_of", [P, H])
        win, wout = sb("win", [P, M2]), sb("wout", [M2, D])
        w1_row, b1_row, bin_row = sb("w1_row", [P, M2 * J2]), sb("b1_row", [1, M2 * J2]), sb("bin_row", [1, M2])
        w2_in, w2_spread = sb("w2_in", [M2, J2]), sb("w2_spread", [M2, M2, J2])
        b2_col, bout_col = sb("b2_col", [M2, 1]), sb("bout_col", [P, 1])
        pa, pb, pc, pd, pe2 = ps("pa"), ps("pb"), ps("pc"), ps("pd"), ps("pe2")
        junk2, junk3, s_mid = sb("junk2", [P, 2]), sb("junk3", [1, M2 * J2]), sem("kink_step")
        half = sb("half", [P, 2])

        norm_loads += [
            (t.w_qkv[:, :], a["L0_attn_W_qkv"]), (t.w_proj[:, :], a["L0_attn_W_proj"]),
            (u_row[:, :], row(a["L0_attn_u_qkv"], 384)), (up_row[:, :], row(a["L0_attn_u_proj"], D)),
            (sigma[:, 0:1], row(a["L0_attn_sigma_qkv"], 1)), (sigma[:, 1:2], row(a["L0_attn_sigma_proj"], 1)),
        ]
        attn_loads += [(t.w_at[:, i * D:(i + 1) * D], a["L1_attn_" + n]) for i, n in enumerate(["Wq", "Wk", "Wv"])]
        attn_loads += [(t.b_at[:, i * D:(i + 1) * D], row(a["L1_attn_" + n], D)) for i, n in enumerate(["bq", "bk", "bv"])]
        attn_loads += [
            (t.w_o[:, :], a["L1_attn_Wo"]), (t.b_o[:, :], row(a["L1_attn_bo"], D)),
            (bq_col[:, :], a["L1_attn_bq"].rearrange("(n o) -> n o", o=1)),
        ]
        attn_loads += [(pe_rep[HD * h:HD * h + HD, :], a["L1_attn_pos_emb"][0, :, 0:NPOS + 2]) for h in range(H)]
        ffn_loads += [
            (t.w_gate[:, :], a["L0_ffn_W_gate"]),
            (t.w1[:, :, :], a["L0_ffn_W1"].rearrange("e d h -> d e h")),
            (t.w2[:, :, :], a["L0_ffn_W2"].rearrange("e (f p) d -> p (e f) d", p=P)),
            (b1_rows[:, :], a["L0_ffn_b1"].rearrange("e (f p) -> (e f) p", p=P)),
            (b2_rows[:, :], a["L0_ffn_b2"]),
            (win[:, :], a["L1_ffn_Win"]), (wout[:, :], a["L1_ffn_Wout"]),
            (w1_row[:, :], row(a["L1_ffn_W1"].rearrange("m j -> (m j)"), M2 * J2)),
            (b1_row[:, :], a["L1_ffn_b1"].rearrange("m j -> (m j)").rearrange("(o n) -> o n", o=1)),
            (bin_row[:, :], a["L1_ffn_bin_"].rearrange("(o n) -> o n", o=1)),
            (w2_in[:, :], a["L1_ffn_W2"]), (b2_col[:, :], a["L1_ffn_b2"].rearrange("(n o) -> n o", o=1)),
            (bout_col[:, :], a["L1_ffn_bout"].rearrange("(n o) -> n o", o=1)),
        ]

        with nc.Block() as block:
            @block.sync
            def _(sp):
                for dst, src in norm_loads:
                    sp.dma_start(dst, src).then_inc(s_norm, 16)
                sp.dma_start(x_sb[:, :, 0, :], x_in[0]).then_inc(t.first_x_loaded, 16)
                for dst, src in attn_loads:
                    sp.dma_start(dst, src).then_inc(s_attn, 16)
                for s in range(1, S):
                    sp.dma_start(x_sb[:, :, s, :], x_in[s]).then_inc(t.rest_x_loaded, 16)

            @block.gpsimd
            def _(pool):
                done = Ticks(s_pool)
                done(pool.memset(t.ones[:, :], 1.0))
                done(pool.memset(t.ident[:, :], 0.0))
                done(pool.memset(t.causal[:, :], 0.0))
                done(pool.memset(head_of[:, :], 1.0))
                pool.wait_ge(s_pool, done.value())
                done(pool.affine_select(out=t.ident[:, :], in_=t.ident[:, :], compare_op=ALU.not_equal, fill=1.0,
                                        base=0, pattern=[[-1, P]], channel_multiplier=1))
                last = t.causal[:, N - P:N]
                done(pool.affine_select(out=last, in_=last, compare_op=ALU.is_ge, fill=NEG,
                                        base=0, pattern=[[-1, P]], channel_multiplier=1))
                done(pool.affine_select(out=head_of[:, :], in_=head_of[:, :], compare_op=ALU.is_ge, fill=0.0,
                                        base=0, pattern=[[-HD, H]], channel_multiplier=1))
                pool.wait_ge(s_pool, done.value())
                done(pool.affine_select(out=head_of[:, :], in_=head_of[:, :], compare_op=ALU.is_ge, fill=0.0,
                                        base=HD - 1, pattern=[[HD, H]], channel_multiplier=-1))
                assert done.n == 8
                done(pool.tensor_copy(t.ident16[:, :], t.ident[:, :]))
                done(pool.memset(t.k_stack[:, :, :], 1.0))
                done(pool.memset(t.v_ext[:, :, :, :], 0.0))
                pool.wait_ge(s_pool, done.value())
                pool.memset(t.v_ext[:, :, :, HD:HD + 1], 1.0)
                pool.memset(t.minus_half[:, :], -0.5)
                done(pool.memset(half[:, :], 0.5))
                pool.wait_ge(s_ffn, 16 * len(ffn_loads))
                done(pool.affine_select(out=w2_spread[:, :, :],
                                        in_=w2_in[:, :].unsqueeze(1).broadcast_to([M2, M2, J2]),
                                        compare_op=ALU.is_equal, fill=0.0,
                                        base=0, pattern=[[-1, M2], [0, J2]], channel_multiplier=1))
                assert done.n == 13
                pool.wait_ge(s_pool, done.value())
                pool.wait_ge(s_vec, 6)
                done(pool.tensor_tensor(norms[:, 4:6], norms[:, 2:4], half[:, :], ALU.pow))
                assert done.n == 14

            @block.scalar
            def _(act):
                for dst, src in ffn_loads:
                    act.dma_start(dst, src).then_inc(s_ffn, 16)
                act.wait_ge(s_pe, 3)
                act.activation(junk[:, 0:384], pa[:, 0:384], ACT.Square, accum_out=norms[:, 0:1]).then_inc(s_act, 1)
                act.wait_ge(s_act, 1)
                act.activation(junk[:, 0:D], pb[:, 0:D], ACT.Square, accum_out=norms[:, 1:2]).then_inc(s_act, 1)

            @block.tensor
            def _(pe):
                done = Ticks(s_pe)
                pe.wait_ge(s_vec, 4)
                done(pe.matmul(pa[:, 0:384], wu_rep[:, 0, :], t.w_qkv[:, :], start=True, stop=True))
                done(pe.matmul(pb[:, 0:D], wu_rep[:, 1, :], t.w_proj[:, :], start=True, stop=True))
                done(pe.matmul(pc[:, 0:2], t.ones[:, :], junk2[:, 0:2], start=True, stop=True))
                pe.wait_ge(s_pool, 8)
                pe.wait_ge(s_attn, 16 * len(attn_loads))
                done(pe.transpose(pd[:, 0:P], t.w_at[:, 0:D], t.ident[:, :]))
                pe.wait_ge(s_vec, 11)
                done(pe.matmul(pa[:, :], wq_t[:, :], blocks[:, :, :].rearrange("p n h -> p (n h)"), start=True, stop=True))
                done(pe.matmul(pb[:, :], bq_rep[:, :], blocks[:, :, :].rearrange("p n h -> p (n h)"), start=True, stop=True))
                pe.wait_ge(s_ffn, 16 * len(ffn_loads))
                done(pe.transpose(pd[:, 128:128 + E * F], b1_rows[:, :], t.ident[0:E * F, 0:E * F]))
                done(pe.transpose(pd[:, 192:192 + E], b2_rows[:, :], t.ident[0:E, 0:E]))
                done(pe.matmul(pd[:, 224:225], wout[:, :], b2_col[:, :], start=True, stop=True))
                pe.wait_ge(s_vec, 14)
                for k in range(K2):
                    mm = pe.matmul(pd[:, 240 + k:241 + k], b1_row[:, k * P:(k + 1) * P], t.ones[0:1, 0:1],
                                   start=True, stop=True)
                done(mm)
                pe.wait_ge(s_pool, 13)
                for k in range(K2):
                    dst = (pc, pe2)[k // 4]
                    mm = pe.matmul(dst[:, (k % 4) * P:(k % 4 + 1) * P],
                                   w2_spread[:, k * 8:(k + 1) * 8, :].rearrange("m a j -> m (a j)"), wout[:, :],
                                   start=True, stop=True)
                done(mm)
                assert done.n == 11

            @block.vector
            def _(dve):
                done = Ticks(s_vec)
                dve.wait_ge(s_norm, 16 * len(norm_loads))
                dve.wait_ge(s_pool, 1)
                dve.tensor_tensor_reduce(junk[:, 0:384], t.w_qkv[:, :], u_row[:, :], 1.0, 0.0, ALU.mult, ALU.add,
                                         wu[:, 0:1]).then_inc(s_vec, 1)
                dve.tensor_tensor_reduce(up_row[:, :], t.w_proj[:, :], up_row[:, :], 1.0, 0.0, ALU.mult, ALU.add,
                                         wu[:, 1:2]).then_inc(s_vec, 1)
                dve.wait_ge(s_vec, 2)
                dve.tensor_tensor(junk2[:, :], wu[:, :], wu[:, :], ALU.mult)
                dve.tensor_scalar(wu_rep[:, 0, :], t.ones[:, :], wu[:, 0:1], None, ALU.mult).then_inc(s_vec, 1)
                dve.tensor_scalar(wu_rep[:, 1, :], t.ones[:, :], wu[:, 1:2], None, ALU.mult).then_inc(s_vec, 1)
                done.n = 4
                dve.wait_ge(s_act, 2)
                done(dve.reciprocal(norms[:, 6:8], norms[:, 0:2]))
                dve.wait_ge(s_vec, done.value())
                done(dve.tensor_tensor(norms[:, 2:4], pc[:, 0:2], norms[:, 6:8], ALU.mult))
                dve.wait_ge(s_pool, 14)
                done(dve.tensor_tensor(sigma[:, :], norms[:, 4:6], sigma[:, :], ALU.mult))
                dve.wait_ge(s_vec, done.value())
                dve.tensor_scalar(t.w_qkv[:, :], t.w_qkv[:, :], sigma[:, 0:1], None, ALU.mult)
                done(dve.tensor_scalar(t.w_proj[:, :], t.w_proj[:, :], sigma[:, 1:2], None, ALU.mult))
                dve.wait_ge(s_attn, 16 * len(attn_loads))
                tmp = junk[:, 0:NPOS]
                mid = Ticks(s_mid)
                mid(dve.scalar_tensor_tensor(tmp, pe_rep[:, 1:NPOS + 1], -2.0, pe_rep[:, 0:NPOS], ALU.mult, ALU.add))
                mid(dve.tensor_tensor(kink[:, 0:1], pe_rep[:, 1:2], pe_rep[:, 0:1], ALU.subtract))
                for k in range(NPOS):
                    col = kink[:, 2 * NPOS - 1 - k:2 * NPOS - k]
                    mid(dve.tensor_scalar(col, pe_rep[:, k:k + 1], float(k + 1), None, ALU.mult))
                dve.wait_ge(s_mid, mid.value())
                mid(dve.tensor_tensor(kink[:, 1:NPOS], tmp[:, 0:NPOS - 1], pe_rep[:, 2:NPOS + 1], ALU.add))
                for k in range(NPOS):
                    col = kink[:, 2 * NPOS - 1 - k:2 * NPOS - k]
                    mid(dve.scalar_tensor_tensor(col, pe_rep[:, k + 1:k + 2], float(-k), col, ALU.mult, ALU.add))
                dve.wait_ge(s_mid, mid.value())
                dve.wait_ge(s_pool, 8)
                done(dve.tensor_tensor(blocks[:, :, :], kink[:, :].unsqueeze(2).broadcast_to([P, 2 * NPOS, H]),
                                       head_of[:, :].unsqueeze(1).broadcast_to([P, 2 * NPOS, H]), ALU.mult))
                done(dve.tensor_scalar(bq_rep[:, :], t.ones[:, :], bq_col[:, 0:1], None, ALU.mult))
                dve.wait_ge(s_pe, 4)
                done(dve.tensor_copy(wq_t[:, :], pd[:, 0:P]))
                assert done.n == 11
                dve.wait_ge(s_pe, 6)
                done(dve.tensor_copy(t.w_kink[:, :], pa[:, :]))
                done(dve.tensor_copy(t.b_kink[:, :], pb[:, :]))
                dve.wait_ge(s_ffn, 16 * len(ffn_loads))
                inner = junk3[:, :].rearrange("p (m j) -> p m j", j=J2)
                mid(dve.tensor_tensor(inner, bin_row[:, :].unsqueeze(2).broadcast_to([1, M2, J2]),
                                      w1_row[0:1, :].rearrange("p (m j) -> p m j", j=J2), ALU.mult))
                dve.wait_ge(s_mid, mid.value())
                done(dve.tensor_tensor(b1_row[:, :], junk3[:, :], b1_row[:, :], ALU.add))
                assert done.n == 14
                dve.tensor_tensor(t.w_in[:, :].rearrange("p (m j) -> p m j", j=J2),
                                  win[:, :].unsqueeze(2).broadcast_to([P, M2, J2]),
                                  w1_row[:, :].rearrange("p (m j) -> p m j", j=J2), ALU.mult)
                dve.wait_ge(s_pe, 10)
                dve.tensor_copy(t.b1[:, :], pd[:, 128:128 + E * F])
                dve.tensor_copy(t.b2[:, :], pd[:, 192:192 + E])
                dve.tensor_tensor(t.b_out[:, :], pd[:, 224:225], bout_col[:, :], ALU.add)
                dve.tensor_copy(t.b_in[:, :], pd[:, 240:240 + K2])
                dve.wait_ge(s_pe, 11)
                dve.tensor_copy(t.w_out[:, 0:4, :], pc[:, :].rearrange("p (k d) -> p k d", d=D))
                dve.tensor_copy(t.w_out[:, 4:8, :], pe2[:, :].rearrange("p (k d) -> p k d", d=D)).then_inc(s_vec, 1)


NQ = 4
PAIRS = H // 2
Q_ORDER = [3, 2, 1, 0]
STEPS_BEFORE, STEPS_FIRST, STEPS_ROW = 12, 33, 38


def causal_attention(nc, a, t, sem):
    scratch = {k: nc.dram_tensor("stack_" + k, [H, PARTS, HD, N], BF16, kind="Internal").ap() for k in "qk"}
    part_of = {"q": [0, 0, 0, 1, 1, 2], "k": [0, 1, 2, 0, 1, 0]}
    x_t = t.x[:, :, :].rearrange("p (c s) d -> p c s d", s=S)

    s_scores, s_tile_max = sem("scores_for_maxima"), sem("tile_maxima")
    s_mparts, s_mt, s_mt_copied = sem("max_parts_ready"), sem("max_parts_turned"), sem("max_rows_copied")
    s_mrow = [sem("max_rows_in_stack_even"), sem("max_rows_in_stack_odd")]
    s_st, s_exp, s_masked = sem("scores_turned"), sem("exp_done"), sem("diagonal_masked")
    s_av, s_vext = sem("values_product"), [sem("values_placed_0"), sem("values_placed_1")]
    s_o_copied, s_o_turned, s_o_norm = sem("outputs_copied"), sem("outputs_turned"), sem("outputs_normalised")
    s_misc, s_misc_read = sem("misc_bank_filled"), sem("misc_bank_read")
    s_vec, s_pool, s_row_done = sem("vector_step0"), sem("pool_step0"), sem("batch_row_done")
    s_xn = sem("rows_normalised")
    s_var, s_shifted, s_rstd = ({k: sem(name + k) for k in ("in", "out")}
                                for name in ("variances_", "variances_shifted_", "inverse_deviations_"))
    s_parts = {k: sem("all_parts_" + k) for k in "qk"}
    s_written, s_half = sem("stacks_written"), [sem("stack_half_0"), sem("stack_half_1")]
    passed = {k: sem("passed_" + k) for k in ("vector", "scalar", "pool", "sync")}

    def fill_in(b, piece, first=False):
        return (piece + 1) if first else 6 * b + piece - 1

    def fill_out(b, piece, last=False):
        return 6 * b + piece + (5 if last else 9)

    with ExitStack() as ctx:
        def sb(name, shape, dt=F32):
            return ctx.enter_context(nc.sbuf_tensor(name, shape, dt))

        banks = [ctx.enter_context(nc.psum_tensor(f"bank{i}", [P, 512], F32)) for i in range(7)]
        max_bank = ctx.enter_context(nc.psum_tensor("max_bank", [P, 1024], BF16))
        s_bank, st_bank, o_bank, turn_bank, misc = banks[0:2], banks[2:4], banks[4], banks[5], banks[6]
        junk = sb("scores_junk", [P, 2, N])
        mx, mres = sb("maxima", [P, 2, 2, NQ]), sb("max_rest", [P, 2, NQ])
        mparts = sb("max_parts", [P, 2, 2, MR, NQ], BF16)
        mrows = sb("max_rows", [2 * MR * NQ, 2, P], BF16)
        probs = sb("probs", [P, NQ, 2, N])
        outs, attn = sb("outs", [P, N]), sb("attn", [P, NQ, D])
        attn_t, rden = sb("attn_t", [P, N]), sb("rden", [P, NQ, 4])
        xn, xn_t = sb("xn", [P, NQ, D]), sb("xn_t", [P, N])
        stats, mv, rstd = sb("stats", [P, NQ, 6]), sb("mv", [P, NQ, 2]), sb("rstd", [P, NQ])
        stats2, mv2, rstd2, y = sb("stats2", [P, NQ, 6]), sb("mv2", [P, NQ, 2]), sb("rstd2", [P, NQ]), sb("y", [P, NQ, D])
        parts = {k: sb("parts_" + k, [P, MR, N], BF16) for k in "qk"}
        rest = {k: sb("rest_" + k, [P, N]) for k in "qk"}
        v_next = sb("v_next", [P, NQ, D])

        def ahead(b, u):
            return (b, u + 2) if u + 2 < PAIRS else (b + 1, u + 2 - PAIRS)

        def pe_scores(pe, b, u, i):
            qt = Q_ORDER[i]
            if i == 0 and u % 4 == 0:
                pe.wait_ge(s_half[u // 4], 64 * b + 64)
            for e in range(2):
                pe.wait_ge(s_tile_max, 64 * b + 8 * u + 2 * i + e + 7)
                pe.matmul(s_bank[e][:, 0:(qt + 1) * P], t.q_stack[64 * e:64 * e + KS, u, qt * P:(qt + 1) * P],
                          t.k_stack[64 * e:64 * e + KS, u, 0:(qt + 1) * P], start=True, stop=True).then_inc(s_scores, 1)

        def pe_turn_max(pe, b, u):
            pe.wait_ge(s_mparts, 8 * b + u + 1)
            pe.wait_ge(s_mt_copied, 8 * b + u + 1)
            pe.transpose(max_bank[0:2 * MR * NQ, 0:P], mparts[:, u % 2, :, :, :].rearrange("p e r q -> p (e r q)"),
                         t.ident16[:, :]).then_inc(s_mt, 1)

        def pe_scores_turned(pe, b, u, kt):
            if kt == 0:
                pe.wait_ge(s_mrow[u % 2], 128 * b + 32 * (u // 2) + 64)
            for e in range(2):
                pe.wait_ge(s_exp, 64 * b + 8 * u + 2 * kt + e + 7)
                pe.matmul(st_bank[e][:, 0:N - kt * P], t.k_stack[64 * e:64 * e + KS + MR, u, kt * P:(kt + 1) * P],
                          t.q_stack[64 * e:64 * e + KS + MR, u, kt * P:N], start=True, stop=True).then_inc(s_st, 1)

        def pe_values(pe, b, u, kt):
            if kt == 0 and u % 4 == 0:
                pe.wait_ge(s_vext[u // 4], b + 1)
            if kt == 0 and u % 2 == 0:
                pe.wait_ge(s_o_copied, 4 * b + u // 2 + 1)
            pe.wait_ge(s_masked, 32 * b + 4 * u + kt + 1)
            for e in range(2):
                g = 2 * (u % 2) + e
                mm = pe.matmul(o_bank[32 * g:32 * g + 32, kt * P:N], t.v_ext[:, kt, 2 * u + e, :],
                               probs[:, kt, e, 0:N - kt * P], start=(kt == 0), stop=(kt == NQ - 1),
                               skip_group_check=True)
            mm.then_inc(s_av, 1)

        def pe_turn_outputs(pe, b, w):
            pe.wait_ge(s_o_copied, 4 * b + w + 2)
            pe.wait_ge(s_o_norm, 4 * b + w + 1)
            for qt in range(NQ):
                mm = pe.transpose(turn_bank[:, qt * P:(qt + 1) * P], outs[:, qt * P:(qt + 1) * P], t.ident[:, :])
            mm.then_inc(s_o_turned, 1)

        def pe_project_in(pe, b, piece, first=False):
            pe.wait_ge(s_misc_read, fill_in(b, piece, first))
            if piece == 0:
                pe.wait_ge(s_xn, b + 1)
                for c in range(NQ):
                    mm = pe.transpose(misc[:, c * P:(c + 1) * P], xn[:, c, :], t.ident[:, :])
            elif piece < 3:
                mm = pe.matmul(misc[:, :], t.w_qkv[:, (piece - 1) * D:piece * D], xn_t[:, :], start=True, stop=True)
            else:
                for c in range(NQ):
                    mm = pe.matmul(misc[:, c * P:(c + 1) * P], xn_t[:, c * P:(c + 1) * P], t.w_qkv[:, 2 * D:3 * D],
                                   start=True, stop=True)
            mm.then_inc(s_misc, 1)

        def pe_project_out(pe, b, piece, last=False):
            if piece == 0:
                pe.wait_ge(s_o_norm, 4 * b + 5)
            pe.wait_ge(s_misc_read, fill_out(b, piece, last))
            for c in range(NQ):
                tile = misc[:, c * P:(c + 1) * P]
                if piece == 0:
                    mm = pe.transpose(tile, attn[:, c, :], t.ident[:, :])
                else:
                    mm = pe.matmul(tile, attn_t[:, c * P:(c + 1) * P], t.w_proj[:, :], start=True, stop=True)
            mm.then_inc(s_misc, 1)

        def pe_row(pe, b, first=False, last=False):
            for u in range(PAIRS):
                more = not (last and u + 2 >= PAIRS)
                if not (last and u == PAIRS - 1):
                    pe_turn_max(pe, *((b, u + 1) if u + 1 < PAIRS else (b + 1, 0)))
                for kt in range(NQ):
                    pe_scores_turned(pe, b, u, kt)
                    if more:
                        pe_scores(pe, *ahead(b, u), kt)
                    if kt >= 2:
                        pe_values(pe, b, u, kt - 2)
                    elif u >= 1:
                        pe_values(pe, b, u - 1, kt + 2)
                    elif not first:
                        pe_values(pe, b - 1, PAIRS - 1, kt + 2)
                    if kt == 3 and u % 2 == 0 and u >= 2:
                        pe_turn_outputs(pe, b, u // 2 - 1)
                    if kt == 3 and u == 0 and not first:
                        pe_turn_outputs(pe, b - 1, 3)
                    if u == 1 and kt in (1, 3) and not first:
                        pe_project_out(pe, b - 1, kt // 2)
                if not last and 1 <= u <= 4:
                    pe_project_in(pe, b + 1, u - 1)

        def v_maxima(dve, b, u, i):
            width = (Q_ORDER[i] + 1) * P
            for e in range(2):
                await_(dve, passed["vector"], s_scores, 64 * b + 8 * u + 2 * i + e + 1)
                dve.tensor_tensor_reduce(junk[:, e, 0:width], s_bank[e][:, 0:width], t.causal[:, N - width:N], 1.0, LOWEST,
                                         ALU.add, ALU.max, mx[:, u % 2, e, Q_ORDER[i]:Q_ORDER[i] + 1]).then_inc(s_tile_max, 1)

        def v_split_maxima(dve, own, b, u):
            m, p = mx[:, u % 2, :, :], mparts[:, u % 2, :, :, :]
            dve.wait_ge(s_tile_max, 64 * b + 8 * u + 16)
            own(dve.tensor_scalar(p[:, :, 0, :], m, -1.0, None, ALU.mult))
            dve.wait_ge(s_vec, own.value())
            own(dve.scalar_tensor_tensor(mres[:, :, :], m, -1.0, p[:, :, 0, :], ALU.mult, ALU.subtract))
            dve.wait_ge(s_vec, own.value())
            own(dve.tensor_copy(p[:, :, 1, :], mres[:, :, :]))
            dve.wait_ge(s_vec, own.value())
            dve.tensor_tensor(p[:, :, 2, :], mres[:, :, :], p[:, :, 1, :], ALU.subtract).then_inc(s_mparts, 1)

        def v_norm_outputs(dve, own, b, w):
            await_(dve, passed["vector"], s_o_turned, 4 * b + w + 2)
            tb = turn_bank[:, :].rearrange("p (q g r) -> p q g r", q=NQ, g=4)
            own(dve.reciprocal(rden[:, :, :], tb[:, :, :, HD]))
            dve.wait_ge(s_vec, own.value())
            out = attn[:, :, 32 * w:32 * w + 32].rearrange("p q (g d) -> p q g d", d=HD)
            dve.tensor_tensor(out, tb[:, :, :, 0:HD], rden[:, :, :].unsqueeze(3).broadcast_to([P, NQ, 4, HD]),
                              ALU.mult).then_inc(s_o_norm, 1)

        def v_stats(dve, own, rows, st, m, which):
            for c in range(NQ):
                own(dve.bn_stats(st[:, c, :], rows(c)))
            await_(dve, passed["vector"], s_vec, own.value())
            for c in range(NQ):
                ins = dve.bn_aggr(m[:, c, :], st[:, c, :])
            ins.then_inc(s_var[which], 1)

        def v_norm_in(dve, b):
            await_(dve, passed["vector"], s_rstd["in"], b + 1)
            for c in range(NQ):
                ins = dve.tensor_scalar(xn[:, c, :], x_t[:, c, b, :], mv[:, c, 0:1], rstd[:, c:c + 1],
                                        ALU.subtract, ALU.mult)
            ins.then_inc(s_xn, 1)

        def v_first_part(dve, own, b, k, first=False):
            fill = fill_in(b, 1 + "qk".index(k), first)
            await_(dve, passed["vector"], s_misc, fill)
            own(dve.tensor_copy(parts[k][:, 0, :], misc[:, :]))
            dve.wait_ge(s_vec, own.value())
            dve.tensor_tensor(rest[k][:, :], misc[:, :], parts[k][:, 0, :], ALU.subtract).then_inc(s_misc_read, 1)

        def v_values(dve, b, first=False):
            await_(dve, passed["vector"], s_misc, fill_in(b, 3, first))
            dve.tensor_copy(v_next[:, :, :], misc[:, :].rearrange("p (c d) -> p c d", d=D)).then_inc(s_misc_read, 1)

        def v_place_values(dve, b, half, first=False):
            if half == 0:
                dve.wait_ge(s_misc_read, fill_in(b, 3, first) + 1)
            await_(dve, passed["vector"], s_av, 32 * b + 4 if half else (4 if first else 32 * b - 12))
            for c in range(NQ):
                ins = dve.tensor_copy(t.v_ext[:, c, 8 * half:8 * half + 8, 0:HD],
                                      v_next[:, c, 64 * half:64 * half + 64].rearrange("p (h d) -> p h d", d=HD))
            ins.then_inc(s_vext[half], 1)

        def v_out_stats(dve, own, b, last=False):
            await_(dve, passed["vector"], s_misc, fill_out(b, 1, last))
            v_stats(dve, own, lambda c: misc[:, c * P:(c + 1) * P], stats2, mv2, "out")

        def v_out_add(dve, b, last=False):
            await_(dve, passed["vector"], s_rstd["out"], b + 1)
            for c in range(NQ):
                ins = dve.tensor_scalar(y[:, c, :], misc[:, c * P:(c + 1) * P], mv2[:, c, 0:1], rstd2[:, c:c + 1],
                                        ALU.subtract, ALU.mult)
            ins.then_inc(s_misc_read, 1)
            await_(dve, passed["vector"], s_misc_read, fill_out(b, 1, last) + 1)
            dve.tensor_tensor(x_t[:, :, b, :], x_t[:, :, b, :], y[:, :, :], ALU.add).then_inc(s_row_done, 1)

        def v_row(dve, b, first=False, last=False):
            own = Ticks(s_vec, STEPS_BEFORE if first else STEPS_BEFORE + STEPS_FIRST - STEPS_ROW + STEPS_ROW * b)
            for u in range(PAIRS):
                if u == 0 and not last:
                    v_stats(dve, own, lambda c: x_t[:, c, b + 1, :], stats, mv, "in")
                if not last and u in (3, 4):
                    v_first_part(dve, own, b + 1, "qk"[u - 3])
                if not last and u == 5:
                    v_values(dve, b + 1)
                if not last and u == 6:
                    v_place_values(dve, b + 1, 0)
                if not first and u == 2:
                    v_place_values(dve, b, 1)
                if not (last and u + 2 >= PAIRS):
                    for i in range(NQ):
                        v_maxima(dve, *ahead(b, u), i)
                    v_split_maxima(dve, own, *ahead(b, u))
                if u == 0 and not last:
                    v_norm_in(dve, b + 1)
                if u == 0 and not first:
                    v_norm_outputs(dve, own, b - 1, 3)
                if u in (2, 4, 6):
                    v_norm_outputs(dve, own, b, u // 2 - 1)
                if not first and u == 1:
                    v_out_stats(dve, own, b - 1)
                    v_out_add(dve, b - 1)
            assert last or own.n == (STEPS_FIRST if first else STEPS_ROW), own.n
            return own

        def a_copy_max(act, b, u):
            act.wait_ge(s_mrow[u % 2], 128 * b + 32 * (u // 2) + 32 if u >= 2 else 128 * b + 32)
            await_(act, passed["scalar"], s_mt, 8 * b + u + 1)
            act.activation(mrows[:, u % 2, :], max_bank[0:2 * MR * NQ, 0:P], ACT.Copy).then_inc(s_mt_copied, 1)

        def a_exp(act, b, u, kt):
            width = N - kt * P
            act.wait_ge(s_av, 32 * b + 4 * u + kt + 1)
            for e in range(2):
                await_(act, passed["scalar"], s_st, 64 * b + 8 * u + 2 * kt + e + 1)
                act.activation(probs[:, kt, e, 0:width], st_bank[e][:, 0:width], ACT.Exp, scale=SCALE)\
                   .then_inc(s_exp, 1)

        def a_copy_outputs(act, b, w):
            act.wait_ge(s_o_turned, 4 * b + w + 1)
            await_(act, passed["scalar"], s_av, 32 * b + 8 * w + 12)
            act.activation(outs[:, :], o_bank[:, :], ACT.Copy).then_inc(s_o_copied, 1)

        def a_copy_misc(act, dst, fill):
            await_(act, passed["scalar"], s_misc, fill)
            act.activation(dst[:, :], misc[:, :], ACT.Copy).then_inc(s_misc_read, 1)

        def a_row(act, b, first=False, last=False):
            for u in range(PAIRS):
                if not (last and u == PAIRS - 1):
                    a_copy_max(act, *((b, u + 1) if u + 1 < PAIRS else (b + 1, 0)))
                for kt in range(NQ):
                    a_exp(act, b, u, kt)
                    if kt == 1 and u % 2 == 0 and u >= 2:
                        a_copy_outputs(act, b, u // 2 - 1)
                    if kt == 1 and u == 0 and not first:
                        a_copy_outputs(act, b - 1, 3)
                    if kt == 2 and u == 1 and not first:
                        a_copy_misc(act, attn_t, fill_out(b - 1, 0))
                if u == 1 and not last:
                    a_copy_misc(act, xn_t, fill_in(b + 1, 0))

        def p_mask(pool, b, u, kt):
            await_(pool, passed["pool"], s_exp, 64 * b + 8 * u + 2 * kt + 10)
            diagonal = probs[:, kt, :, 0:P]
            pool.affine_select(out=diagonal, in_=diagonal, compare_op=ALU.is_ge, fill=0.0, base=0,
                               pattern=[[0, 2], [1, P]], channel_multiplier=-1).then_inc(s_masked, 1)

        def p_rstd(pool, m, r, which, b):
            await_(pool, passed["pool"], s_var[which], b + 1)
            pool.tensor_scalar(r[:, :], m[:, :, 1], EPS, None, ALU.add).then_inc(s_shifted[which], 1)
            await_(pool, passed["pool"], s_shifted[which], b + 1)
            pool.tensor_tensor(r[:, :], r[:, :], t.minus_half[:, :], ALU.pow).then_inc(s_rstd[which], 1)

        def p_parts(pool, b, k, first=False):
            fill = fill_in(b, 1 + "qk".index(k), first)
            await_(pool, passed["pool"], s_misc_read, fill + 1)
            pool.tensor_copy(parts[k][:, 1, :], rest[k][:, :]).then_inc(s_pool, 1)
            await_(pool, passed["pool"], s_pool, 2 * b + "qk".index(k) + 1)
            pool.tensor_tensor(parts[k][:, 2, :], rest[k][:, :], parts[k][:, 1, :], ALU.subtract).then_inc(s_parts[k], 1)

        def p_row(pool, b, first=False, last=False):
            for u in range(PAIRS):
                for kt in range(NQ):
                    p_mask(pool, b, u, kt)
                    if kt == 1 and not last:
                        if u == 0:
                            p_rstd(pool, mv, rstd, "in", b + 1)
                        if u in (3, 4):
                            p_parts(pool, b + 1, "qk"[u - 3])
                if u == 1 and not first:
                    p_rstd(pool, mv2, rstd2, "out", b - 1)

        def d_max_rows(sp, b, u):
            await_(sp, passed["sync"], s_mt_copied, 8 * b + u + 2)
            for e in range(2):
                lo = 64 * e + KS
                sp.dma_start(t.q_stack[lo:lo + MR, u, :], mrows[MR * NQ * e:MR * NQ * (e + 1), u % 2, :])\
                  .then_inc(s_mrow[u % 2], 16)

        def d_write(sp, b, k):
            await_(sp, passed["sync"], s_parts[k], b + 1)
            for r in range(PARTS):
                sp.dma_start(scratch[k][:, r, :, :], parts[k][:, part_of[k][r], :]).then_inc(s_written, 16)

        def d_load(sp, half):
            for k, stack in (("q", t.q_stack), ("k", t.k_stack)):
                src = scratch[k].rearrange("(u e) r d n -> e (r d) u n", e=2)
                for e in range(2):
                    sp.dma_start(stack[64 * e:64 * e + KS, 4 * half:4 * half + 4, :], src[e][:, 4 * half:4 * half + 4, :])\
                      .then_inc(s_half[half], 16)

        def d_row(sp, b, first=False, last=False):
            for u in range(PAIRS):
                if not (last and u == PAIRS - 1):
                    d_max_rows(sp, *((b, u + 1) if u + 1 < PAIRS else (b + 1, 0)))
                if u == 0:
                    await_(sp, passed["sync"], s_exp, 64 * b + 8)
                    d_load(sp, 1)
                if u == 3 and not last:
                    await_(sp, passed["sync"], s_half[1], 64 * b + 64)
                    d_write(sp, b + 1, "q")
                if u == 4 and not last:
                    d_write(sp, b + 1, "k")
                if u == 5 and not last:
                    await_(sp, passed["sync"], s_written, 192 * b + 384)
                    await_(sp, passed["sync"], s_st, 64 * b + 32)
                    d_load(sp, 0)

        def all_rows(eng, row):
            row(eng, 0, first=True)
            with eng.Fori(1, S - 1) as b:
                row(eng, b)
            return row(eng, S - 1, last=True)

        with nc.Block() as block:
            @block.tensor
            def _(pe):
                pe.sem_inc(s_av, 4)
                pe.sem_inc(s_o_turned, 1)
                for piece in range(4):
                    pe_project_in(pe, 0, piece, first=True)
                for u in range(2):
                    for i in range(NQ):
                        pe_scores(pe, 0, u, i)
                    if u == 0:
                        pe_turn_max(pe, 0, 0)
                all_rows(pe, pe_row)
                for kt in (2, 3):
                    pe_values(pe, S - 1, PAIRS - 1, kt)
                pe_turn_outputs(pe, S - 1, 3)
                for piece in range(2):
                    pe_project_out(pe, S - 1, piece, last=True)

            @block.vector
            def _(dve):
                dve.sem_inc(s_tile_max, 8)
                dve.sem_inc(s_o_norm, 1)
                dve.sem_inc(s_misc_read, 1)
                own = Ticks(s_vec)
                dve.wait_ge(t.first_x_loaded, 16)
                v_stats(dve, own, lambda c: x_t[:, c, 0, :], stats, mv, "in")
                v_norm_in(dve, 0)
                v_first_part(dve, own, 0, "q", first=True)
                v_first_part(dve, own, 0, "k", first=True)
                v_values(dve, 0, first=True)
                v_place_values(dve, 0, 0, first=True)
                v_place_values(dve, 0, 1, first=True)
                for u in range(2):
                    for i in range(NQ):
                        v_maxima(dve, 0, u, i)
                    v_split_maxima(dve, own, 0, u)
                assert own.n == STEPS_BEFORE, own.n
                dve.wait_ge(t.rest_x_loaded, 16 * (S - 1))
                own = all_rows(dve, v_row)
                v_norm_outputs(dve, own, S - 1, 3)
                v_out_stats(dve, own, S - 1, last=True)
                v_out_add(dve, S - 1, last=True)

            @block.scalar
            def _(act):
                act.sem_inc(s_exp, 8)
                act.sem_inc(s_mt_copied, 1)
                act.sem_inc(s_o_copied, 1)
                a_copy_misc(act, xn_t, fill_in(0, 0, first=True))
                a_copy_max(act, 0, 0)
                all_rows(act, a_row)
                a_copy_outputs(act, S - 1, 3)
                a_copy_misc(act, attn_t, fill_out(S - 1, 0, last=True))

            @block.gpsimd
            def _(pool):
                p_rstd(pool, mv, rstd, "in", 0)
                p_parts(pool, 0, "q", first=True)
                p_parts(pool, 0, "k", first=True)
                all_rows(pool, p_row)
                p_rstd(pool, mv2, rstd2, "out", S - 1)

            @block.sync
            def _(sp):
                sp.sem_inc(s_mrow[0], 32)
                sp.sem_inc(s_mrow[1], 32)
                d_write(sp, 0, "q")
                d_write(sp, 0, "k")
                sp.wait_ge(s_written, 192)
                d_load(sp, 0)
                d_max_rows(sp, 0, 0)
                all_rows(sp, d_row)


R = S // C
G = 4
GROUPS = C * R
STEPS_E, STEPS_P, STEPS_S, STEPS_M, STEPS_Q = 6, 9, 13, 57, 24


def masked(value, bits):
    return value & bits if isinstance(value, int) else (value & bits).with_bounds(min_val=0, max_val=bits)


def experts_and_mixing(nc, a, t, sem, out):
    x_out = out.rearrange("s (c p) d -> p c s d", p=P)
    mask_scratch = nc.dram_tensor("mask_scratch", [E, N], F32, kind="Internal").ap()

    s_vec_e, s_vec_p, s_vec_s = sem("vector_step_experts"), sem("vector_step_experts_end"), sem("vector_step_gates")
    s_vec_m, s_vec_q = sem("vector_step_weights"), sem("vector_step_values")
    s_var1, s_shift1, s_rstd1, s_xn1 = sem("variances1"), sem("shifted1"), sem("inverse_dev1"), sem("rows_normalised1")
    s_var2, s_shift2, s_rstd2, s_xn2 = sem("variances2"), sem("shifted2"), sem("inverse_dev2"), sem("rows_normalised2")
    s_m1, s_m1_read = sem("bank_m1_filled"), sem("bank_m1_read")
    s_m2, s_m2_read = sem("bank_m2_filled"), sem("bank_m2_read")
    s_gated, s_gexp, s_mask = sem("gates_shifted"), sem("gates_exp"), sem("mask_ready")
    s_mask_out, s_mask_lo, s_mask_hi = sem("mask_written"), sem("mask_spread_low"), sem("mask_spread_high")
    s_xt = sem("expert_rows_ready")
    s_h, s_relu, s_y, s_y_read = sem("hidden_ready"), sem("relu_done"), sem("expert_product"), sem("expert_read")
    s_acc = sem("experts_summed")
    s_g, s_g_read, s_y2, s_y2_read = sem("bank_g_filled"), sem("bank_g_read"), sem("inner_product"), sem("inner_read")
    s_keep, s_xs = sem("rows_kept"), sem("rows_recalled")
    s_kv = sem("keys_values_ready")
    s_lg, s_tanh, s_shifted, s_p = sem("logits_ready"), sem("gates_tanh"), sem("logits_shifted"), sem("weights_exp")
    s_o, s_x2 = sem("mixed_ready"), sem("x_after_last")
    s_out = sem("rows_written")
    passed = {k: sem("passed1_" + k) for k in ("vector", "scalar", "pool", "sync")}

    with ExitStack() as ctx:
        def sb(name, shape, dt=F32):
            return ctx.enter_context(nc.sbuf_tensor(name, shape, dt))

        banks = [ctx.enter_context(nc.psum_tensor(f"rest_bank{i}", [P, 512], F32)) for i in range(8)]
        h_bank, y_bank, m1, g_bank, y2_bank, m2 = banks[0:2], banks[2], banks[3], banks[4:6], banks[6], banks[7]
        xn1, xn1_t, xn1_t2 = sb("xn1", [P, G, D]), sb("xn1_t", [P, N]), sb("xn1_t2", [P, N])
        stats1, mv1, rstd1 = sb("stats1", [P, G, 6]), sb("mv1", [P, G, 2]), sb("rstd1", [P, G])
        stats2, mv2, rstd2 = sb("stats2b", [P, G, 6]), sb("mv2b", [P, G, 2]), sb("rstd2b", [P, G])
        gate, top, shifted, keep = sb("gate", [P, G, E]), sb("top", [P, G, 8]), sb("shifted", [P, G, E]), sb("keep", [P, G, E])
        gexp, gsum, mask_t = sb("gexp", [P, G, E]), sb("gsum", [P, G]), sb("mask_t", [E, N])
        mask_all = sb("mask_all", [P, E, N])
        hidden, term, total = sb("hidden", [P, 4, N]), sb("term", [P, N]), sb("total", [P, N])
        y1 = sb("y1", [P, G, D])
        kv = sb("kv", [P, 2 * S, 2 * D])
        kept, xs = sb("kept", [P, R, N]), sb("xs", [P, N])
        q = sb("q", [P, G, D])
        kinks = sb("kinks", [P, 2 * NPOS, G, H])
        prod = sb("prod", [P, S, D])
        logits, pos, acc = sb("logits", [P, S, G, H]), sb("pos", [P, S, G, H]), sb("acc", [P, S, G, H])
        kterm = logits
        peak, wsum = sb("peak", [P, G * H]), sb("wsum", [P, G * H])
        o, o_t, y2 = sb("o", [P, G, D]), sb("o_t", [P, N]), sb("y2", [P, G, D])
        hidden2 = sb("hidden2", [P, 4, N])
        z_t = o_t

        def tiles(g):
            return t.x[:, bass.ds(G * g, G), :]

        def row(g):
            return lambda j: t.x[:, G * g + j, :]

        def special(i, values, otherwise):
            return values[i] if isinstance(i, int) and i in values else otherwise

        def before_m1(i):
            return special(i, {-1: -4, GROUPS: 7 * GROUPS - 4}, 7 * i - 1)

        def before_var1(i):
            return special(i, {-1: -2, GROUPS: 3 * GROUPS - 2}, 3 * i - 1)

        def before_xn1(i):
            return special(i, {-1: -1, GROUPS: 2 * GROUPS - 1}, 2 * i)

        def before_m2(i):
            return special(i, {R: 0}, 5 * (i - R) - 4)

        def before_g(i):
            return special(i, {R: 0}, 12 * (i - R) - 8)

        def pe_turn(pe, i, fill, number):
            pe.wait_ge(s_m1_read, before_m1(i) + fill)
            pe.wait_ge(s_xn1, before_xn1(i) + number)
            for j in range(G):
                mm = pe.transpose(m1[:, j * P:(j + 1) * P], xn1[:, j, :], t.ident[:, :])
            mm.then_inc(s_m1, 1)

        def pe_gates(pe, i):
            pe.wait_ge(s_m1_read, before_m1(i) + 6)
            for j in range(G):
                mm = pe.matmul(m1[:, j * E:(j + 1) * E], xn1_t2[:, j * P:(j + 1) * P], t.w_gate[:, :], start=True, stop=True)
            mm.then_inc(s_m1, 1)

        def pe_mask(pe, i):
            pe.wait_ge(s_m1_read, before_m1(i) + 7)
            pe.wait_ge(s_mask, i + 2)
            for j in range(G):
                mm = pe.transpose(m1[0:E, j * P:(j + 1) * P], gexp[:, j, :], t.ident[:, :])
            mm.then_inc(s_m1, 1)

        def pe_hidden(pe, i, k):
            if k == 0:
                pe.wait_ge(s_xt, i + 1)
            pe.wait_ge(s_relu, 32 * i + k + 1)
            pe.matmul(h_bank[k % 2][:, :], t.w1[:, k // F, (k % F) * P:(k % F + 1) * P], xn1_t[:, :],
                      start=True, stop=True).then_inc(s_h, 1)

        def pe_expert(pe, i, k):
            if k % F == 0:
                pe.wait_ge(s_y_read, 8 * i + k // F + 1)
            pe.wait_ge(s_relu, 32 * i + k + 3)
            pe.matmul(y_bank[:, :], t.w2[:, k, :], hidden[:, k % 4, :], start=(k % F == 0), stop=(k % F == F - 1))\
              .then_inc(s_y, 1)

        def pe_experts_out(pe, i):
            pe.wait_ge(s_m1_read, before_m1(i) + 1)
            pe.wait_ge(s_acc, i)
            for j in range(G):
                mm = pe.transpose(m1[:, j * P:(j + 1) * P], total[:, j * P:(j + 1) * P], t.ident[:, :])
            mm.then_inc(s_m1, 1)

        def pe_keys_values(pe, i, half):
            pe.wait_ge(s_m1_read, before_m1(i) + 3 + half)
            for j in range(2):
                g = 2 * half + j
                mm = pe.matmul(m1[:, j * 2 * D:(j + 1) * 2 * D], xn1_t2[:, g * P:(g + 1) * P], t.w_at[:, D:3 * D],
                               start=True, stop=True)
            mm.then_inc(s_m1, 1)

        def pe_queries(pe, i):
            pe.wait_ge(s_xs, i - R + 1)
            pe.wait_ge(s_m2_read, before_m2(i) + 1)
            for j in range(G):
                mm = pe.matmul(m2[:, j * P:(j + 1) * P], xs[:, j * P:(j + 1) * P], t.w_at[:, 0:D], start=True, stop=True)
            mm.then_inc(s_m2, 1)

        def pe_kinks(pe, i, j):
            pe.wait_ge(s_g_read, before_g(i) + j + 1)
            pe.matmul(g_bank[j % 2][:, :], xs[:, j * P:(j + 1) * P], t.w_kink[:, :], start=True, stop=True)\
              .then_inc(s_g, 1)

        def pe_turn_mixed(pe, i, m):
            pe.wait_ge(s_o, i - R)
            pe.wait_ge(s_m2_read, m + 2)
            for j in range(G):
                mm = pe.transpose(m2[:, j * P:(j + 1) * P], o[:, j, :], t.ident[:, :])
            mm.then_inc(s_m2, 1)

        def pe_project(pe, i, m):
            pe.wait_ge(s_m2_read, m + 3)
            for j in range(G):
                mm = pe.matmul(m2[:, j * P:(j + 1) * P], o_t[:, j * P:(j + 1) * P], t.w_o[:, :], start=True, stop=True)
            mm.then_inc(s_m2, 1)

        def pe_turn_last(pe, i, m):
            pe.wait_ge(s_xn2, i - R)
            pe.wait_ge(s_m2_read, m + 4)
            for j in range(G):
                mm = pe.transpose(m2[:, j * P:(j + 1) * P], o[:, j, :], t.ident[:, :])
            mm.then_inc(s_m2, 1)

        def pe_inner(pe, i, m, g, k):
            if k == 0:
                pe.wait_ge(s_m2_read, m + 5)
            pe.wait_ge(s_g_read, g + k + 5)
            pe.matmul(g_bank[k % 2][:, :], t.w_in[:, k * P:(k + 1) * P], o_t[:, :], start=True, stop=True)\
              .then_inc(s_g, 1)

        def pe_outer(pe, i, g, k):
            if k == 0:
                pe.wait_ge(s_y2_read, i - R)
            pe.wait_ge(s_g_read, g + k + 7)
            pe.matmul(y2_bank[:, :], t.w_out[:, k, :], hidden2[:, k % 4, :],
                      start=(k == 0), stop=(k == K2 - 1)).then_inc(s_y2, 1)

        def pe_turn_result(pe, i):
            pe.wait_ge(s_y2_read, i - R + 1)
            for j in range(G):
                mm = pe.transpose(m2[:, j * P:(j + 1) * P], z_t[:, j * P:(j + 1) * P], t.ident[:, :])
            mm.then_inc(s_m2, 1)

        def pe_step(pe, i, experts, end, gates, attend, finish):
            m = before_m2(i) - (0 if attend else 1) if finish else None
            g = before_g(i) - (0 if attend else G) if finish else None
            for k in range(E * F + 2):
                if end:
                    if k == 2:
                        pe_experts_out(pe, i)
                    if k == 6:
                        pe_turn(pe, i, 2, 1)
                    if k in (8, 9):
                        pe_keys_values(pe, i, k - 8)
                if attend:
                    if k == 4:
                        pe_queries(pe, i)
                    if k in (4, 5, 10, 12):
                        pe_kinks(pe, i, (4, 5, 10, 12).index(k))
                if finish:
                    if k == 11:
                        pe_turn_mixed(pe, i, m)
                    if k == 13:
                        pe_project(pe, i, m)
                    if k == 18:
                        pe_turn_last(pe, i, m)
                    if 19 <= k < 19 + K2:
                        pe_inner(pe, i, m, g, k - 19)
                    if 21 <= k < 21 + K2:
                        pe_outer(pe, i, g, k - 21)
                    if k == 31:
                        pe_turn_result(pe, i)
                if gates:
                    if k == 22:
                        pe_turn(pe, i, 5, 2)
                    if k == 24:
                        pe_gates(pe, i)
                    if k == 30:
                        pe_mask(pe, i)
                if experts:
                    if k < E * F:
                        pe_hidden(pe, i, k)
                    if k >= 2:
                        pe_expert(pe, i, k - 2)

        def v_stats(dve, own, s_vec, rows, st, m, s_var):
            for j in range(G):
                own(dve.bn_stats(st[:, j, :], rows(j)))
            await_(dve, passed["vector"], s_vec, own.value())
            for j in range(G):
                ins = dve.bn_aggr(m[:, j, :], st[:, j, :])
            ins.then_inc(s_var, 1)

        def v_scale(dve, s_rstd, number, rows, dst, m, r):
            await_(dve, passed["vector"], s_rstd, number)
            for j in range(G):
                ins = dve.tensor_scalar(dst[:, j, :], rows(j), m[:, j, 0:1], r[:, j:j + 1], ALU.subtract, ALU.mult)
            return ins

        def v_stats1(dve, own, rows):
            v_stats(dve, own, own.sem, rows, stats1, mv1, s_var1)

        def v_scale1(dve, i, number, rows, dst):
            return v_scale(dve, s_rstd1, before_var1(i) + number, rows, dst, mv1, rstd1)

        def v_gates(dve, own, i):
            await_(dve, passed["vector"], s_m1, before_m1(i) + 6)
            dve.tensor_copy(gate[:, :, :], m1[:, 0:G * E].rearrange("p (g e) -> p g e", e=E)).then_inc(s_m1_read, 1)
            await_(dve, passed["vector"], s_m1_read, before_m1(i) + 7)
            for j in range(G):
                own(dve.max(top[:, j, :], gate[:, j, :]))
            await_(dve, passed["vector"], s_vec_s, own.value())
            dve.tensor_tensor(shifted[:, :, :], gate[:, :, :], top[:, :, 0:1].broadcast_to([P, G, E]), ALU.subtract)\
               .then_inc(s_gated, 1)
            own(dve.tensor_tensor(keep[:, :, :], gate[:, :, :], top[:, :, 1:2].broadcast_to([P, G, E]), ALU.is_ge))
            dve.wait_ge(s_vec_s, own.value())

        def v_mask(dve, own, i):
            await_(dve, passed["vector"], s_gexp, i + 2)
            own(dve.tensor_tensor(gexp[:, :, :], gexp[:, :, :], keep[:, :, :], ALU.mult))
            dve.wait_ge(s_vec_s, own.value())
            own(dve.tensor_reduce(gsum[:, :], gexp[:, :, :], AX.X, ALU.add))
            dve.wait_ge(s_vec_s, own.value())
            own(dve.reciprocal(gsum[:, :], gsum[:, :]))
            dve.wait_ge(s_vec_s, own.value())
            own(dve.tensor_scalar(gsum[:, :], gsum[:, :], 1.0 / E, None, ALU.mult))
            dve.wait_ge(s_vec_s, own.value())
            dve.tensor_tensor(gexp[:, :, :], gexp[:, :, :], gsum[:, :].unsqueeze(2).broadcast_to([P, G, E]), ALU.mult)\
               .then_inc(s_mask, 1)

        def v_expert(dve, own, i, e):
            if e == 0:
                dve.wait_ge(s_mask_lo, 16 * i + 16)
            if e == E // 2:
                dve.wait_ge(s_mask_hi, 16 * i + 16)
            await_(dve, passed["vector"], s_y, 32 * i + 4 * e + 8)
            dst = total if e == 0 else term
            dve.scalar_tensor_tensor(dst[:, :], y_bank[:, :], t.b2[:, e:e + 1], mask_all[:, e, :], ALU.add, ALU.mult)\
               .then_inc(s_y_read, 1)
            if e >= 1:
                dve.wait_ge(s_y_read, 8 * i + e + 2)
                if e == E - 1:
                    dve.tensor_tensor(total[:, :], total[:, :], term[:, :], ALU.add).then_inc(s_acc, 1)
                else:
                    own(dve.tensor_tensor(total[:, :], total[:, :], term[:, :], ALU.add))
                    dve.wait_ge(s_vec_e, own.value())

        def v_experts_stats(dve, own, i):
            await_(dve, passed["vector"], s_m1, before_m1(i) + 1)
            v_stats1(dve, own, lambda j: m1[:, j * P:(j + 1) * P])

        def v_experts_add(dve, own, i):
            v_scale1(dve, i, 1, lambda j: m1[:, j * P:(j + 1) * P], y1).then_inc(s_m1_read, 1)
            await_(dve, passed["vector"], s_m1_read, before_m1(i) + 2)
            own(dve.tensor_tensor(tiles(i - 1), tiles(i - 1), y1[:, :, :], ALU.add))
            await_(dve, passed["vector"], s_vec_p, own.value())
            v_stats1(dve, own, row(i - 1))

        def v_keys_values(dve, i, half):
            await_(dve, passed["vector"], s_m1, before_m1(i) + 3 + half)
            dve.tensor_tensor(kv[:, bass.ds(G * masked(i - 1, 2 * R - 1) + 2 * half, 2), :],
                              m1[:, :].rearrange("p (g d) -> p g d", g=2),
                              t.b_at[:, D:3 * D].unsqueeze(1).broadcast_to([P, 2, 2 * D]), ALU.add)\
               .then_inc(s_m1_read, 1)

        def v_queries(dve, i):
            await_(dve, passed["vector"], s_m2, before_m2(i) + 1)
            dve.tensor_tensor(q[:, :, :], m2[:, :].rearrange("p (g d) -> p g d", g=G),
                              t.b_at[:, 0:D].unsqueeze(1).broadcast_to([P, G, D]), ALU.add).then_inc(s_m2_read, 1)

        def v_kink_heights(dve, i, j):
            await_(dve, passed["vector"], s_g, before_g(i) + j + 1)
            dve.tensor_tensor(kinks[:, :, j, :], g_bank[j % 2][:, :].rearrange("p (n h) -> p n h", h=H),
                              t.b_kink[:, :].rearrange("p (n h) -> p n h", h=H), ALU.add).then_inc(s_g_read, 1)

        def v_logits(dve, own, i, j):
            if j == 0:
                dve.wait_ge(s_m2_read, before_m2(i) + 2)
            keys = kv[:, bass.ds(G * masked(i - R, R), S), 0:D]
            own(dve.tensor_tensor(prod[:, :, :], q[:, j, :].unsqueeze(1).broadcast_to([P, S, D]), keys, ALU.mult))
            dve.wait_ge(s_vec_m, own.value())
            ins = dve.tensor_reduce(logits[:, :, j, :], prod[:, :, :].rearrange("p t (h d) -> p t h d", d=HD),
                                    AX.X, ALU.add)
            if j == G - 1:
                ins.then_inc(s_lg, 1)
                dve.wait_ge(s_lg, i - R + 1)
            else:
                own(ins)
                dve.wait_ge(s_vec_m, own.value())

        def v_positions(dve, own, i):
            await_(dve, passed["vector"], s_tanh, i - R + 1)
            flat = pos[:, :, :, :].rearrange("p t g h -> p t (g h)")
            own(dve.tensor_scalar(flat, flat, 0.5, 0.5, ALU.mult, ALU.add))
            dve.wait_ge(s_vec_m, own.value())
            for k in range(S - 2, -1, -1):
                own(dve.tensor_tensor(flat[:, k, :], flat[:, k, :], flat[:, k + 1, :], ALU.add))
                dve.wait_ge(s_vec_m, own.value())
            dve.wait_ge(s_g_read, before_g(i) + 6)
            own(dve.scalar_tensor_tensor(acc[:, :, :, :].rearrange("p t g h -> p (t g h)"),
                                         logits[:, :, :, :].rearrange("p t g h -> p (t g h)"), SCALE,
                                         kinks[:, NPOS:, :, :].rearrange("p t g h -> p (t g h)"), ALU.mult, ALU.add))
            dve.wait_ge(s_vec_m, own.value())

        def v_kink(dve, own, n):
            keys = S - n
            f = lambda x: x[:, 0:keys, :, :].rearrange("p t g h -> p t (g h)")
            height = kinks[:, n, :, :].rearrange("p g h -> p (g h)").unsqueeze(1).broadcast_to([P, keys, G * H])
            own(dve.scalar_tensor_tensor(f(kterm), f(pos), float(n), height, ALU.max, ALU.mult))
            dve.wait_ge(s_vec_m, own.value())
            own(dve.tensor_tensor(f(acc), f(acc), f(kterm), ALU.add))
            dve.wait_ge(s_vec_m, own.value())

        def v_softmax(dve, own, i):
            by_key = lambda x: x[:, :, :, :].rearrange("p t g h -> p (g h) t")
            flat = lambda x: x[:, :, :, :].rearrange("p t g h -> p t (g h)")
            own(dve.tensor_reduce(peak[:, :], by_key(acc), AX.X, ALU.max))
            dve.wait_ge(s_vec_m, own.value())
            dve.tensor_tensor(flat(acc), flat(acc), peak[:, :].unsqueeze(1).broadcast_to([P, S, G * H]), ALU.subtract)\
               .then_inc(s_shifted, 1)

        def v_weight_sums(dve, own, i):
            by_key = lambda x: x[:, :, :, :].rearrange("p t g h -> p (g h) t")
            await_(dve, passed["vector"], s_p, i - R)
            own(dve.tensor_reduce(wsum[:, :], by_key(acc), AX.X, ALU.add))
            dve.wait_ge(s_vec_q, own.value())
            own(dve.reciprocal(wsum[:, :], wsum[:, :]))
            dve.wait_ge(s_vec_q, own.value())

        def v_values(dve, own, i, j):
            values = kv[:, bass.ds(G * masked(i - R - 1, R), S), D:2 * D].rearrange("p t (h d) -> p t h d", d=HD)
            weights = acc[:, :, j, :].unsqueeze(3).broadcast_to([P, S, H, HD])
            own(dve.tensor_tensor(prod[:, :, :].rearrange("p t (h d) -> p t h d", d=HD), weights, values, ALU.mult))
            dve.wait_ge(s_vec_q, own.value())
            own(dve.tensor_reduce(o[:, j, :], prod[:, :, :].rearrange("p t c -> p c t"), AX.X, ALU.add))
            dve.wait_ge(s_vec_q, own.value())
            if j == G - 1:
                heads = o[:, :, :].rearrange("p g (h d) -> p (g h) d", d=HD)
                dve.tensor_tensor(heads, heads, wsum[:, :].unsqueeze(2).broadcast_to([P, G * H, HD]), ALU.mult)\
                   .then_inc(s_o, 1)

        def v_stats2(dve, own, rows):
            v_stats(dve, own, own.sem, rows, stats2, mv2, s_var2)

        def v_scale2(dve, i, number, rows, dst):
            return v_scale(dve, s_rstd2, 3 * (i - R - 1) + number, rows, dst, mv2, rstd2)

        def v_mixed_stats(dve, own, i, m):
            await_(dve, passed["vector"], s_m2, m + 3)
            dve.tensor_tensor(y2[:, :, :], m2[:, :].rearrange("p (g d) -> p g d", g=G),
                              t.b_o[:, :].unsqueeze(1).broadcast_to([P, G, D]), ALU.add).then_inc(s_m2_read, 1)
            await_(dve, passed["vector"], s_m2_read, m + 4)
            v_stats2(dve, own, lambda j: y2[:, j, :])

        def v_mixed_add(dve, own, i):
            g = i - R - 1
            own(v_scale2(dve, i, 1, lambda j: y2[:, j, :], y2))
            dve.wait_ge(s_vec_q, own.value())
            own(dve.tensor_tensor(tiles(g), tiles(g), y2[:, :, :], ALU.add))
            await_(dve, passed["vector"], s_vec_q, own.value())
            v_stats2(dve, own, row(g))

        def v_last_add(dve, i, m):
            g = i - R - 1
            v_scale2(dve, i, 3, lambda j: m2[:, j * P:(j + 1) * P], y2).then_inc(s_m2_read, 1)
            await_(dve, passed["vector"], s_m2_read, m + 6)
            dve.tensor_tensor(tiles(g), tiles(g), y2[:, :, :], ALU.add).then_inc(s_x2, 1)

        def v_step(dve, i, experts, end, gates, attend, finish):
            own_e, own_p, own_s = Ticks(s_vec_e, STEPS_E * i), Ticks(s_vec_p, STEPS_P * (i - 1)), Ticks(s_vec_s, STEPS_S * (i + 1))
            own_m, own_q = Ticks(s_vec_m, STEPS_M * (i - R)), Ticks(s_vec_q, STEPS_Q * (i - R - 1))
            m = before_m2(i) - (0 if attend else 1) if finish else None
            for e in range(E):
                if e == 0:
                    if end:
                        v_experts_stats(dve, own_p, i)
                    if finish:
                        v_weight_sums(dve, own_q, i)
                        v_values(dve, own_q, i, 0)
                    if end:
                        v_experts_add(dve, own_p, i)
                    if finish:
                        v_values(dve, own_q, i, 1)
                    if end:
                        v_scale1(dve, i, 2, row(i - 1), xn1).then_inc(s_xn1, 1)
                if e == 1:
                    if finish:
                        v_values(dve, own_q, i, 2)
                    if attend:
                        v_queries(dve, i)
                        v_kink_heights(dve, i, 0)
                        v_kink_heights(dve, i, 1)
                    if end:
                        v_keys_values(dve, i, 0)
                    if finish:
                        v_values(dve, own_q, i, 3)
                    if end:
                        v_keys_values(dve, i, 1)
                        await_(dve, passed["vector"], s_m1_read, before_m1(i) + 5)
                if e == 2 and attend:
                    v_logits(dve, own_m, i, 0)
                    v_kink_heights(dve, i, 2)
                    v_logits(dve, own_m, i, 1)
                    v_kink_heights(dve, i, 3)
                if e == 3:
                    if finish:
                        v_mixed_stats(dve, own_q, i, m)
                    if attend:
                        v_logits(dve, own_m, i, 2)
                    if finish:
                        v_mixed_add(dve, own_q, i)
                    if attend:
                        v_logits(dve, own_m, i, 3)
                    if finish:
                        v_scale2(dve, i, 2, row(i - R - 1), o).then_inc(s_xn2, 1)
                if e == 4:
                    if gates:
                        v_stats1(dve, own_s, row(i + 1))
                    if attend:
                        v_positions(dve, own_m, i)
                    if gates:
                        v_scale1(dve, i, 3, row(i + 1), xn1).then_inc(s_xn1, 1)
                if e == 6 and gates:
                    v_gates(dve, own_s, i)
                if attend:
                    for n in {4: range(0, 3), 5: range(3, 9), 6: range(9, NPOS)}.get(e, ()):
                        v_kink(dve, own_m, n)
                if e == 6 and gates:
                    v_mask(dve, own_s, i)
                if e == 7:
                    if attend:
                        v_softmax(dve, own_m, i)
                    if finish:
                        await_(dve, passed["vector"], s_m2, m + 5)
                        v_stats2(dve, own_q, lambda j: m2[:, j * P:(j + 1) * P])
                        v_last_add(dve, i, m)
                if experts:
                    v_expert(dve, own_e, i, e)
            assert not experts or own_e.n == STEPS_E, own_e.n
            assert not end or own_p.n == STEPS_P, own_p.n
            assert not gates or own_s.n == STEPS_S, own_s.n
            assert not attend or own_m.n == STEPS_M, own_m.n
            assert not finish or own_q.n == STEPS_Q, own_q.n

        def a_copy(act, dst, bank, s_fill, fill, s_read):
            await_(act, passed["scalar"], s_fill, fill)
            act.activation(dst, bank, ACT.Copy).then_inc(s_read, 1)

        def a_expert_rows(act, i):
            if not (isinstance(i, int) and i == 0):
                await_(act, passed["scalar"], s_h, 32 * i)
            act.activation(xn1_t[:, :], xn1_t2[:, :], ACT.Copy).then_inc(s_xt, 1)
            await_(act, passed["scalar"], s_xt, i + 1)

        def a_inner(act, i, g, k):
            q = 8 * (i - R - 1)
            act.wait_ge(s_y2, q + k + 1)
            await_(act, passed["scalar"], s_g, g + 5 + k)
            act.activation(hidden2[:, k % 4, :], g_bank[k % 2][:, :], ACT.Relu, bias=t.b_in[:, k:k + 1])\
               .then_inc(s_g_read, 1)

        def a_step(act, i, experts, end, gates, attend, finish):
            m = before_m2(i) - (0 if attend else 1) if finish else None
            g = before_g(i) - (0 if attend else G) if finish else None
            if experts:
                a_expert_rows(act, i)
            for k in range(E * F):
                if k == 6 and end:
                    a_copy(act, xn1_t2[:, :], m1[:, :], s_m1, before_m1(i) + 2, s_m1_read)
                if k == 12 and finish:
                    a_copy(act, o_t[:, :], m2[:, :], s_m2, m + 2, s_m2_read)
                if k == 18 and finish:
                    a_copy(act, o_t[:, :], m2[:, :], s_m2, m + 4, s_m2_read)
                if k == 18 and attend:
                    await_(act, passed["scalar"], s_lg, i - R + 1)
                    act.activation(pos[:, :, :, :], logits[:, :, :, :], ACT.Tanh, scale=0.5 * SCALE).then_inc(s_tanh, 1)
                if 19 <= k < 19 + K2 and finish:
                    a_inner(act, i, g, k - 19)
                if k == 22 and gates:
                    if end:
                        await_(act, passed["scalar"], s_keep, i)
                    a_copy(act, xn1_t2[:, :], m1[:, :], s_m1, before_m1(i) + 5, s_m1_read)
                if k == 28 and gates:
                    await_(act, passed["scalar"], s_gated, i + 2)
                    act.activation(gexp[:, :, :], shifted[:, :, :], ACT.Exp).then_inc(s_gexp, 1)
                if k == 30 and finish:
                    await_(act, passed["scalar"], s_y2, 8 * (i - R - 1) + 12)
                    act.activation(z_t[:, :], y2_bank[:, :], ACT.Identity, bias=t.b_out[:, 0:1]).then_inc(s_y2_read, 1)
                if k == 31 and gates:
                    a_copy(act, mask_t[:, :], m1[0:E, :], s_m1, before_m1(i) + 7, s_m1_read)
                if experts:
                    act.wait_ge(s_y, 32 * i + k + 1)
                    await_(act, passed["scalar"], s_h, 32 * i + k + 1)
                    act.activation(hidden[:, k % 4, :], h_bank[k % 2][:, :], ACT.Relu, bias=t.b1[:, k:k + 1])\
                       .then_inc(s_relu, 1)
            if attend:
                await_(act, passed["scalar"], s_shifted, i - R + 1)
                act.activation(acc[:, :, :, :], acc[:, :, :, :], ACT.Exp).then_inc(s_p, 1)

        def p_rstd(pool, m, r, s_var, s_shift, s_rstd, number):
            await_(pool, passed["pool"], s_var, number)
            pool.tensor_scalar(r[:, :], m[:, :, 1], EPS, None, ALU.add).then_inc(s_shift, 1)
            await_(pool, passed["pool"], s_shift, number)
            pool.tensor_tensor(r[:, :], r[:, :], t.minus_half[:, :], ALU.pow).then_inc(s_rstd, 1)

        def p_step(pool, i, experts, end, gates, attend, finish):
            norm1 = lambda n: p_rstd(pool, mv1, rstd1, s_var1, s_shift1, s_rstd1, before_var1(i) + n)
            norm2 = lambda n: p_rstd(pool, mv2, rstd2, s_var2, s_shift2, s_rstd2, 3 * (i - R - 1) + n)
            if attend:
                pool.tensor_copy(xs[:, :], kept[:, masked(i - R, R - 1), :]).then_inc(s_xs, 1)
            if end:
                norm1(1)
                norm1(2)
                await_(pool, passed["pool"], s_m1_read, before_m1(i) + 3)
                pool.tensor_copy(kept[:, masked(i - 1, R - 1), :], xn1_t2[:, :]).then_inc(s_keep, 1)
            if finish:
                norm2(1)
                norm2(2)
            if gates:
                norm1(3)
            if finish:
                norm2(3)

        def d_mask(sp, g):
            first = isinstance(g, int) and g == 0
            await_(sp, passed["sync"], s_m1_read, 4 if first else 7 * g)
            if not first:
                sp.wait_ge(s_mask_lo, 16 * g)
                await_(sp, passed["sync"], s_mask_hi, 16 * g)
            sp.dma_start(mask_scratch, mask_t[:, :]).then_inc(s_mask_out, 16)
            src = mask_scratch.rearrange("(o e) n -> o e n", o=1).broadcast_to([P, E, N])
            if not first:
                await_(sp, passed["sync"], s_y_read, 8 * g - 3)
            await_(sp, passed["sync"], s_mask_out, 16 * g + 16)
            sp.dma_start(mask_all[:, 0:E // 2, :], src[:, 0:E // 2, :]).then_inc(s_mask_lo, 16)
            if not first:
                await_(sp, passed["sync"], s_y_read, 8 * g + 1)
            sp.dma_start(mask_all[:, E // 2:E, :], src[:, E // 2:E, :]).then_inc(s_mask_hi, 16)

        def d_out(sp, c, r):
            g = R * c + r
            await_(sp, passed["sync"], s_x2, g + 1)
            sp.dma_start(x_out[:, c, bass.ds(G * r, G), :], tiles(g)).then_inc(s_out, 16)

        def d_all(sp):
            d_mask(sp, 0)
            with sp.Fori(1, R + 2) as g:
                d_mask(sp, g)
            with sp.Fori(0, 2) as c:
                with sp.Fori(0, R) as r:
                    d_mask(sp, R * c + r + R + 2)
                    d_out(sp, c, r)
            with sp.Fori(0, 2) as r:
                d_mask(sp, R * 2 + r + R + 2)
                d_out(sp, 2, r)
            with sp.Fori(2, R) as r:
                d_out(sp, 2, r)
            with sp.Fori(0, R) as r:
                d_out(sp, 3, r)

        def all_steps(eng, step):
            step(eng, -1, False, False, True, False, False)
            step(eng, 0, True, False, True, False, False)
            with eng.Fori(1, R) as i:
                step(eng, i, True, True, True, False, False)
            step(eng, R, True, True, True, True, False)
            with eng.Fori(R + 1, GROUPS - 1) as i:
                step(eng, i, True, True, True, True, True)
            step(eng, GROUPS - 1, True, True, False, True, True)
            step(eng, GROUPS, False, True, False, True, True)
            with eng.Fori(GROUPS + 1, GROUPS + R) as i:
                step(eng, i, False, False, False, True, True)
            step(eng, GROUPS + R, False, False, False, False, True)

        with nc.Block() as block:
            @block.tensor
            def _(pe):
                pe.sem_inc(s_y, 4)
                pe.sem_inc(s_y2, 4)
                all_steps(pe, pe_step)

            @block.vector
            def _(dve):
                dve.sem_inc(s_y_read, 1)
                all_steps(dve, v_step)

            @block.scalar
            def _(act):
                for s, n in ((s_m1_read, 1), (s_m2_read, 1), (s_relu, 2), (s_g_read, 2), (s_y2_read, 1)):
                    act.sem_inc(s, n)
                all_steps(act, a_step)

            @block.gpsimd
            def _(pool):
                all_steps(pool, p_step)

            @block.sync
            def _(sp):
                d_all(sp)
                sp.wait_ge(s_out, 16 * C * R)


def build(nc, a, out):
    with ExitStack() as ctx:
        class t:
            pass

        def sb(name, shape, dt=F32):
            return ctx.enter_context(nc.sbuf_tensor(name, shape, dt))

        def sem(name):
            return ctx.enter_context(nc.semaphore(name))

        t.x = sb("x", [P, T, D])
        t.ident, t.ones, t.ident16 = sb("ident", [P, P]), sb("ones", [P, P]), sb("ident16", [P, P], BF16)
        t.w_at, t.b_at = sb("w_at", [P, 3 * D]), sb("b_at", [P, 3 * D])
        t.w_kink, t.b_kink = sb("w_kink", [P, 2 * NPOS * H]), sb("b_kink", [P, 2 * NPOS * H])
        t.w_o, t.b_o = sb("w_o", [P, D]), sb("b_o", [P, D])
        t.w_gate, t.w1, t.w2 = sb("w_gate", [P, E]), sb("w1", [P, E, HID]), sb("w2", [P, E * F, D])
        t.b1, t.b2 = sb("b1", [P, E * F]), sb("b2", [P, E])
        t.w_in, t.b_in = sb("w_in", [P, M2 * J2]), sb("b_in", [P, K2])
        t.w_out, t.b_out = sb("w_out", [P, K2, D]), sb("b_out", [P, 1])
        t.minus_half = sb("minus_half", [P, C])
        t.first_x_loaded, t.rest_x_loaded = sem("first_x_loaded"), sem("rest_x_loaded")
        with ExitStack() as first:
            def sb0(name, shape, dt=F32):
                return first.enter_context(nc.sbuf_tensor(name, shape, dt))

            t.w_qkv, t.w_proj = sb0("w_qkv", [P, 3 * D]), sb0("w_proj", [P, D])
            t.causal = sb0("causal", [P, N])
            t.q_stack, t.k_stack = sb0("q_stack", [P, PAIRS, N], BF16), sb0("k_stack", [P, PAIRS, N], BF16)
            t.v_ext = sb0("v_ext", [P, NQ, H, 32])
            load_and_prepare(nc, a, t, sem)
            causal_attention(nc, a, t, sem)
        experts_and_mixing(nc, a, t, sem, out)


_INS = [
    'L0_attn_batch', 'L0_attn_W_qkv', 'L0_attn_u_qkv', 'L0_attn_sigma_qkv',
    'L0_attn_W_proj', 'L0_attn_u_proj', 'L0_attn_sigma_proj', 'L0_ffn_W_gate',
    'L0_ffn_W1', 'L0_ffn_b1', 'L0_ffn_W2', 'L0_ffn_b2',
    'L1_attn_Wq', 'L1_attn_bq', 'L1_attn_Wk', 'L1_attn_bk',
    'L1_attn_Wv', 'L1_attn_bv', 'L1_attn_Wo', 'L1_attn_bo',
    'L1_attn_pos_emb', 'L1_ffn_Win', 'L1_ffn_bin_', 'L1_ffn_W1',
    'L1_ffn_b1', 'L1_ffn_W2', 'L1_ffn_b2', 'L1_ffn_Wout',
    'L1_ffn_bout',
]
_OUT = (S, N, D)


def kernel(**inputs):
    import numpy as _np
    import concourse.bacc as _bacc
    from concourse import mybir as _mybir
    from concourse.bass_utils import run_bass_kernel_spmd as _run

    nc = _bacc.Bacc("TRN2", target_bir_lowering=False, num_devices=1)
    arrays, a = {}, {}
    for name in _INS:
        v = _np.ascontiguousarray(inputs[name])
        arrays[f"in_{name}_dram"] = v
        a[name] = nc.dram_tensor(f"in_{name}_dram", v.shape, _mybir.dt.from_np(v.dtype), kind="ExternalInput").ap()
    out = nc.dram_tensor("out_dram", _OUT, _mybir.dt.float32, kind="ExternalOutput").ap()
    build(nc, a, out)
    r = _run(nc, [arrays], core_ids=[0])
    return r.results[0]["out_dram"]
```

```python
import concourse.bass as bass
from concourse import mybir
from contextlib import ExitStack

F32 = mybir.dt.float32
BF16 = mybir.dt.bfloat16
ALU = mybir.AluOpType
ACT = mybir.ActivationFunctionType
AX = mybir.AxisListType

P = 128
S, N, D = 16, 512, 128
C = N // P
T = S * C
H, HD = 16, 8
SCALE = HD ** -0.5
EPS = 1e-5
E, HID = 8, 512
F = HID // P
PARTS = 6
KS = PARTS * HD
MR = 3
NPOS = S
M2, J2 = 64, 16
K2 = M2 * J2 // P
NEG = -3.0e38
LOWEST = -3.4028e38


class Ticks:

    def __init__(self, sem, base=0):
        self.sem, self.base, self.n = sem, base, 0

    def __call__(self, instruction, by=1):
        instruction.then_inc(self.sem, by)
        self.n += by

    def value(self):
        return self.base + self.n


def await_(eng, passed, sem, value):
    eng.wait_ge(sem, value)
    eng.sem_inc(passed, 1)


def load_and_prepare(nc, a, t, sem):
    x_in = a["L0_attn_batch"].rearrange("s (c p) d -> s p c d", p=P)
    x_sb = t.x[:, :, :].rearrange("p (c s) d -> p c s d", s=S)
    s_norm, s_attn, s_ffn = sem("norm_weights_loaded"), sem("attn_weights_loaded"), sem("ffn_weights_loaded")
    s_pool, s_vec, s_pe, s_act = sem("pool_step"), sem("vector_step"), sem("tensor_step"), sem("scalar_step")
    norm_loads, attn_loads, ffn_loads = [], [], []

    def row(v, n):
        return v.rearrange("(o n) -> o n", o=1).broadcast_to([P, n])

    with ExitStack() as ctx:
        def sb(name, shape, dt=F32):
            return ctx.enter_context(nc.sbuf_tensor(name, shape, dt))

        def ps(name):
            return ctx.enter_context(nc.psum_tensor(name, [P, 512], F32))

        u_row, up_row = sb("u_row", [P, 384]), sb("up_row", [P, D])
        sigma, norms, junk = sb("sigma", [P, 2]), sb("norms", [P, 8]), sb("junk", [P, 384])
        wu, wu_rep = sb("wu", [P, 2]), sb("wu_rep", [P, 2, P])
        b1_rows, b2_rows = sb("b1_rows", [E * F, P]), sb("b2_rows", [E, D])
        wq_t, pe_rep, kink = sb("wq_t", [P, P]), sb("pe_rep", [P, NPOS + 2]), sb("kink", [P, 2 * NPOS])
        blocks, bq_col, bq_rep = sb("blocks", [P, 2 * NPOS, H]), sb("bq_col", [P, 1]), sb("bq_rep", [P, P])
        head_of = sb("head_of", [P, H])
        wout, bin_col = sb("wout", [P, D]), sb("bin_col", [P, 1])
        w1_in, b1_in, w2_in = sb("w1_in", [P, J2]), sb("b1_in", [P, J2]), sb("w2_in", [P, J2])
        b2_col, bout_col = sb("b2_col", [M2, 1]), sb("bout_col", [P, 1])
        pa, pb, pc, pd = ps("pa"), ps("pb"), ps("pc"), ps("pd")
        junk2, s_mid = sb("junk2", [P, 2]), sem("kink_step")
        half = sb("half", [P, 2])

        norm_loads += [
            (t.w_qkv[:, :], a["L0_attn_W_qkv"]), (t.w_proj[:, :], a["L0_attn_W_proj"]),
            (u_row[:, :], row(a["L0_attn_u_qkv"], 384)), (up_row[:, :], row(a["L0_attn_u_proj"], D)),
            (sigma[:, 0:1], row(a["L0_attn_sigma_qkv"], 1)), (sigma[:, 1:2], row(a["L0_attn_sigma_proj"], 1)),
        ]
        attn_loads += [(t.w_at[:, i * D:(i + 1) * D], a["L1_attn_" + n]) for i, n in enumerate(["Wq", "Wk", "Wv"])]
        attn_loads += [(t.b_at[:, i * D:(i + 1) * D], row(a["L1_attn_" + n], D)) for i, n in enumerate(["bq", "bk", "bv"])]
        attn_loads += [
            (t.w_o[:, :], a["L1_attn_Wo"]), (t.b_o[:, :], row(a["L1_attn_bo"], D)),
            (bq_col[:, :], a["L1_attn_bq"].rearrange("(n o) -> n o", o=1)),
        ]
        attn_loads += [(pe_rep[:, :], a["L1_attn_pos_emb"][:, :, 0:NPOS + 2].broadcast_to([H, HD, NPOS + 2]))]
        ffn_loads += [
            (t.w_gate[:, :], a["L0_ffn_W_gate"]),
            (b1_rows[:, :], a["L0_ffn_b1"].rearrange("e (f p) -> (e f) p", p=P)),
            (b2_rows[:, :], a["L0_ffn_b2"]),
            (b2_col[:, :], a["L1_ffn_b2"].rearrange("(n o) -> n o", o=1)),
            (bout_col[:, :], a["L1_ffn_bout"].rearrange("(n o) -> n o", o=1)),
        ]

        for odd in range(2):
            half_of = slice(M2 * odd, M2 * odd + M2)
            ffn_loads += [
                (t.w_in[:, half_of], a["L1_ffn_Win"]), (wout[half_of, :], a["L1_ffn_Wout"]),
                (w1_in[half_of, :], a["L1_ffn_W1"]), (b1_in[half_of, :], a["L1_ffn_b1"]),
                (w2_in[half_of, :], a["L1_ffn_W2"]),
                (bin_col[half_of, :], a["L1_ffn_bin_"].rearrange("(n o) -> n o", o=1)),
            ]

        with nc.Block() as block:
            @block.sync
            def _(sp):
                for dst, src in norm_loads:
                    sp.dma_start(dst, src).then_inc(s_norm, 16)
                sp.dma_start(x_sb[:, :, 0, :], x_in[0]).then_inc(t.first_x_loaded, 16)
                for dst, src in attn_loads:
                    sp.dma_start(dst, src).then_inc(s_attn, 16)
                for s in range(1, S):
                    sp.dma_start(x_sb[:, :, s, :], x_in[s]).then_inc(t.rest_x_loaded, 16)

            @block.gpsimd
            def _(pool):
                done = Ticks(s_pool)
                done(pool.memset(t.ones[:, :], 1.0))
                done(pool.memset(t.ident[:, :], 0.0))
                done(pool.memset(t.causal[:, :], 0.0))
                done(pool.memset(head_of[:, :], 1.0))
                pool.wait_ge(s_pool, done.value())
                done(pool.affine_select(out=t.ident[:, :], in_=t.ident[:, :], compare_op=ALU.not_equal, fill=1.0,
                                        base=0, pattern=[[-1, P]], channel_multiplier=1))
                last = t.causal[:, N - P:N]
                done(pool.affine_select(out=last, in_=last, compare_op=ALU.is_ge, fill=NEG,
                                        base=0, pattern=[[-1, P]], channel_multiplier=1))
                done(pool.affine_select(out=head_of[:, :], in_=head_of[:, :], compare_op=ALU.is_ge, fill=0.0,
                                        base=0, pattern=[[-HD, H]], channel_multiplier=1))
                pool.wait_ge(s_pool, done.value())
                done(pool.affine_select(out=head_of[:, :], in_=head_of[:, :], compare_op=ALU.is_ge, fill=0.0,
                                        base=HD - 1, pattern=[[HD, H]], channel_multiplier=-1))
                assert done.n == 8
                done(pool.tensor_copy(t.ident16[:, :], t.ident[:, :]))
                done(pool.memset(t.k_stack[:, :, :], 1.0))
                done(pool.memset(t.v_ext[:, :, :, :], 0.0))
                pool.wait_ge(s_pool, done.value())
                pool.memset(t.v_ext[:, :, :, HD:HD + 1], 1.0)
                pool.memset(t.minus_half[:, :], -0.5)
                done(pool.memset(half[:, :], 0.5))
                assert done.n == 12
                pool.wait_ge(s_pool, done.value())
                pool.wait_ge(s_vec, 6)
                done(pool.tensor_tensor(norms[:, 4:6], norms[:, 2:4], half[:, :], ALU.pow))
                assert done.n == 13

            @block.scalar
            def _(act):
                for dst, src in ffn_loads:
                    act.dma_start(dst, src).then_inc(s_ffn, 16)
                act.wait_ge(s_pe, 3)
                act.activation(junk[:, 0:384], pa[:, 0:384], ACT.Square, accum_out=norms[:, 0:1]).then_inc(s_act, 1)
                act.wait_ge(s_act, 1)
                act.activation(junk[:, 0:D], pb[:, 0:D], ACT.Square, accum_out=norms[:, 1:2]).then_inc(s_act, 1)

            @block.tensor
            def _(pe):
                done = Ticks(s_pe)
                pe.wait_ge(s_vec, 4)
                done(pe.matmul(pa[:, 0:384], wu_rep[:, 0, :], t.w_qkv[:, :], start=True, stop=True))
                done(pe.matmul(pb[:, 0:D], wu_rep[:, 1, :], t.w_proj[:, :], start=True, stop=True))
                done(pe.matmul(pc[:, 0:2], t.ones[:, :], junk2[:, 0:2], start=True, stop=True))
                pe.wait_ge(s_pool, 8)
                pe.wait_ge(s_attn, 16 * len(attn_loads))
                done(pe.transpose(pd[:, 0:P], t.w_at[:, 0:D], t.ident[:, :]))
                pe.wait_ge(s_vec, 11)
                done(pe.matmul(pa[:, :], wq_t[:, :], blocks[:, :, :].rearrange("p n h -> p (n h)"), start=True, stop=True))
                done(pe.matmul(pb[:, :], bq_rep[:, :], blocks[:, :, :].rearrange("p n h -> p (n h)"), start=True, stop=True))
                pe.wait_ge(s_ffn, 16 * len(ffn_loads))
                done(pe.transpose(pd[:, 128:128 + E * F], b1_rows[:, :], t.ident[0:E * F, 0:E * F]))
                done(pe.transpose(pd[:, 192:192 + E], b2_rows[:, :], t.ident[0:E, 0:E]))
                done(pe.matmul(pd[:, 224:225], wout[0:M2, :], b2_col[:, :], start=True, stop=True))
                assert done.n == 9

            @block.vector
            def _(dve):
                done = Ticks(s_vec)
                dve.wait_ge(s_norm, 16 * len(norm_loads))
                dve.wait_ge(s_pool, 1)
                dve.tensor_tensor_reduce(junk[:, 0:384], t.w_qkv[:, :], u_row[:, :], 1.0, 0.0, ALU.mult, ALU.add,
                                         wu[:, 0:1]).then_inc(s_vec, 1)
                dve.tensor_tensor_reduce(up_row[:, :], t.w_proj[:, :], up_row[:, :], 1.0, 0.0, ALU.mult, ALU.add,
                                         wu[:, 1:2]).then_inc(s_vec, 1)
                dve.wait_ge(s_vec, 2)
                dve.tensor_tensor(junk2[:, :], wu[:, :], wu[:, :], ALU.mult)
                dve.tensor_scalar(wu_rep[:, 0, :], t.ones[:, :], wu[:, 0:1], None, ALU.mult).then_inc(s_vec, 1)
                dve.tensor_scalar(wu_rep[:, 1, :], t.ones[:, :], wu[:, 1:2], None, ALU.mult).then_inc(s_vec, 1)
                done.n = 4
                dve.wait_ge(s_act, 2)
                done(dve.reciprocal(norms[:, 6:8], norms[:, 0:2]))
                dve.wait_ge(s_vec, done.value())
                done(dve.tensor_tensor(norms[:, 2:4], pc[:, 0:2], norms[:, 6:8], ALU.mult))
                dve.wait_ge(s_pool, 13)
                done(dve.tensor_tensor(sigma[:, :], norms[:, 4:6], sigma[:, :], ALU.mult))
                dve.wait_ge(s_vec, done.value())
                dve.tensor_scalar(t.w_qkv[:, :], t.w_qkv[:, :], sigma[:, 0:1], None, ALU.mult)
                done(dve.tensor_scalar(t.w_proj[:, :], t.w_proj[:, :], sigma[:, 1:2], None, ALU.mult))
                dve.wait_ge(s_attn, 16 * len(attn_loads))
                tmp = junk[:, 0:NPOS]
                mid = Ticks(s_mid)
                mid(dve.scalar_tensor_tensor(tmp, pe_rep[:, 1:NPOS + 1], -2.0, pe_rep[:, 0:NPOS], ALU.mult, ALU.add))
                mid(dve.tensor_tensor(kink[:, 0:1], pe_rep[:, 1:2], pe_rep[:, 0:1], ALU.subtract))
                for k in range(NPOS):
                    col = kink[:, 2 * NPOS - 1 - k:2 * NPOS - k]
                    mid(dve.tensor_scalar(col, pe_rep[:, k:k + 1], float(k + 1), None, ALU.mult))
                dve.wait_ge(s_mid, mid.value())
                mid(dve.tensor_tensor(kink[:, 1:NPOS], tmp[:, 0:NPOS - 1], pe_rep[:, 2:NPOS + 1], ALU.add))
                for k in range(NPOS):
                    col = kink[:, 2 * NPOS - 1 - k:2 * NPOS - k]
                    mid(dve.scalar_tensor_tensor(col, pe_rep[:, k + 1:k + 2], float(-k), col, ALU.mult, ALU.add))
                dve.wait_ge(s_mid, mid.value())
                dve.wait_ge(s_pool, 8)
                done(dve.tensor_tensor(blocks[:, :, :], kink[:, :].unsqueeze(2).broadcast_to([P, 2 * NPOS, H]),
                                       head_of[:, :].unsqueeze(1).broadcast_to([P, 2 * NPOS, H]), ALU.mult))
                done(dve.tensor_scalar(bq_rep[:, :], t.ones[:, :], bq_col[:, 0:1], None, ALU.mult))
                dve.wait_ge(s_pe, 4)
                done(dve.tensor_copy(wq_t[:, :], pd[:, 0:P]))
                assert done.n == 11
                dve.wait_ge(s_pe, 6)
                done(dve.tensor_copy(t.w_kink[:, :], pa[:, :]))
                done(dve.tensor_copy(t.b_kink[:, :], pb[:, :]))
                dve.wait_ge(s_ffn, 16 * len(ffn_loads))
                for odd in range(2):
                    half_of = slice(M2 * odd, M2 * odd + M2)
                    by_j = lambda v: v[half_of, :].rearrange("m (k two) -> m k two", two=2)[:, :, odd]
                    dve.tensor_copy(t.s_in[half_of, :], by_j(w1_in))
                    dve.scalar_tensor_tensor(t.b_in[half_of, :], by_j(w1_in), bin_col[half_of, 0:1], by_j(b1_in),
                                             ALU.mult, ALU.add)
                    dve.tensor_tensor(t.w_out[half_of, :, :], wout[half_of, :].unsqueeze(1).broadcast_to([M2, K2, D]),
                                      by_j(w2_in).unsqueeze(2).broadcast_to([M2, K2, D]), ALU.mult)
                dve.wait_ge(s_pe, 9)
                dve.tensor_copy(t.b1[:, :], pd[:, 128:128 + E * F])
                dve.tensor_copy(t.b2[:, :], pd[:, 192:192 + E])
                dve.tensor_tensor(t.b_out[:, :], pd[:, 224:225], bout_col[:, :], ALU.add).then_inc(s_vec, 1)


NQ = 4
PAIRS = H // 2
Q_ORDER = [3, 2, 1, 0]
STEPS_BEFORE, STEPS_FIRST, STEPS_ROW = 12, 33, 38


def causal_attention(nc, a, t, sem):
    scratch = {k: nc.dram_tensor("stack_" + k, [H, PARTS, HD, N], BF16, kind="Internal").ap() for k in "qk"}
    part_of = {"q": [0, 0, 0, 1, 1, 2], "k": [0, 1, 2, 0, 1, 0]}
    x_t = t.x[:, :, :].rearrange("p (c s) d -> p c s d", s=S)

    s_scores, s_tile_max = sem("scores_for_maxima"), sem("tile_maxima")
    s_mparts, s_mt, s_mt_copied = sem("max_parts_ready"), sem("max_parts_turned"), sem("max_rows_copied")
    s_mrow = [sem("max_rows_in_stack_even"), sem("max_rows_in_stack_odd")]
    s_st, s_exp, s_masked = sem("scores_turned"), sem("exp_done"), sem("diagonal_masked")
    s_av, s_vext = sem("values_product"), [sem("values_placed_0"), sem("values_placed_1")]
    s_o_copied, s_o_turned, s_o_norm = sem("outputs_copied"), sem("outputs_turned"), sem("outputs_normalised")
    s_misc, s_misc_read = sem("misc_bank_filled"), sem("misc_bank_read")
    s_vec, s_pool, s_row_done = sem("vector_step0"), sem("pool_step0"), sem("batch_row_done")
    s_xn = sem("rows_normalised")
    s_var, s_shifted, s_rstd = ({k: sem(name + k) for k in ("in", "out")}
                                for name in ("variances_", "variances_shifted_", "inverse_deviations_"))
    s_parts = {k: sem("all_parts_" + k) for k in "qk"}
    s_written, s_half = sem("stacks_written"), [sem("stack_half_0"), sem("stack_half_1")]
    passed = {k: sem("passed_" + k) for k in ("vector", "scalar", "pool", "sync")}

    def fill_in(b, piece, first=False):
        return (piece + 1) if first else 6 * b + piece - 1

    def fill_out(b, piece, last=False):
        return 6 * b + piece + (5 if last else 9)

    with ExitStack() as ctx:
        def sb(name, shape, dt=F32):
            return ctx.enter_context(nc.sbuf_tensor(name, shape, dt))

        banks = [ctx.enter_context(nc.psum_tensor(f"bank{i}", [P, 512], F32)) for i in range(7)]
        max_bank = ctx.enter_context(nc.psum_tensor("max_bank", [P, 1024], BF16))
        s_bank, st_bank, o_bank, turn_bank, misc = banks[0:2], banks[2:4], banks[4], banks[5], banks[6]
        junk = sb("scores_junk", [P, 2, N])
        mx, mres = sb("maxima", [P, 2, 2, NQ]), sb("max_rest", [P, 2, NQ])
        mparts = sb("max_parts", [P, 2, 2, MR, NQ], BF16)
        mrows = sb("max_rows", [2 * MR * NQ, 2, P], BF16)
        probs = sb("probs", [P, NQ, 2, N])
        outs, attn = sb("outs", [P, N]), sb("attn", [P, NQ, D])
        attn_t, rden = sb("attn_t", [P, N]), sb("rden", [P, NQ, 4])
        xn, xn_t = sb("xn", [P, NQ, D]), sb("xn_t", [P, N])
        stats, mv, rstd = sb("stats", [P, NQ, 6]), sb("mv", [P, NQ, 2]), sb("rstd", [P, NQ])
        stats2, mv2, rstd2, y = sb("stats2", [P, NQ, 6]), sb("mv2", [P, NQ, 2]), sb("rstd2", [P, NQ]), sb("y", [P, NQ, D])
        parts = {k: sb("parts_" + k, [P, MR, N], BF16) for k in "qk"}
        rest = {k: sb("rest_" + k, [P, N]) for k in "qk"}
        v_next = sb("v_next", [P, NQ, D])

        def ahead(b, u):
            return (b, u + 2) if u + 2 < PAIRS else (b + 1, u + 2 - PAIRS)

        def pe_scores(pe, b, u, i):
            qt = Q_ORDER[i]
            if i == 0 and u % 4 == 0:
                pe.wait_ge(s_half[u // 4], 64 * b + 64)
            for e in range(2):
                pe.wait_ge(s_tile_max, 64 * b + 8 * u + 2 * i + e + 7)
                pe.matmul(s_bank[e][:, 0:(qt + 1) * P], t.q_stack[64 * e:64 * e + KS, u, qt * P:(qt + 1) * P],
                          t.k_stack[64 * e:64 * e + KS, u, 0:(qt + 1) * P], start=True, stop=True).then_inc(s_scores, 1)

        def pe_turn_max(pe, b, u):
            pe.wait_ge(s_mparts, 8 * b + u + 1)
            pe.wait_ge(s_mt_copied, 8 * b + u + 1)
            pe.transpose(max_bank[0:2 * MR * NQ, 0:P], mparts[:, u % 2, :, :, :].rearrange("p e r q -> p (e r q)"),
                         t.ident16[:, :]).then_inc(s_mt, 1)

        def pe_scores_turned(pe, b, u, kt):
            if kt == 0:
                pe.wait_ge(s_mrow[u % 2], 128 * b + 32 * (u // 2) + 64)
            for e in range(2):
                pe.wait_ge(s_exp, 64 * b + 8 * u + 2 * kt + e + 7)
                pe.matmul(st_bank[e][:, 0:N - kt * P], t.k_stack[64 * e:64 * e + KS + MR, u, kt * P:(kt + 1) * P],
                          t.q_stack[64 * e:64 * e + KS + MR, u, kt * P:N], start=True, stop=True).then_inc(s_st, 1)

        def pe_values(pe, b, u, kt):
            if kt == 0 and u % 4 == 0:
                pe.wait_ge(s_vext[u // 4], b + 1)
            if kt == 0 and u % 2 == 0:
                pe.wait_ge(s_o_copied, 4 * b + u // 2 + 1)
            pe.wait_ge(s_masked, 32 * b + 4 * u + kt + 1)
            for e in range(2):
                g = 2 * (u % 2) + e
                mm = pe.matmul(o_bank[32 * g:32 * g + 32, kt * P:N], t.v_ext[:, kt, 2 * u + e, :],
                               probs[:, kt, e, 0:N - kt * P], start=(kt == 0), stop=(kt == NQ - 1),
                               skip_group_check=True)
            mm.then_inc(s_av, 1)

        def pe_turn_outputs(pe, b, w):
            pe.wait_ge(s_o_copied, 4 * b + w + 2)
            pe.wait_ge(s_o_norm, 4 * b + w + 1)
            for qt in range(NQ):
                mm = pe.transpose(turn_bank[:, qt * P:(qt + 1) * P], outs[:, qt * P:(qt + 1) * P], t.ident[:, :])
            mm.then_inc(s_o_turned, 1)

        def pe_project_in(pe, b, piece, first=False):
            pe.wait_ge(s_misc_read, fill_in(b, piece, first))
            if piece == 0:
                pe.wait_ge(s_xn, b + 1)
                for c in range(NQ):
                    mm = pe.transpose(misc[:, c * P:(c + 1) * P], xn[:, c, :], t.ident[:, :])
            elif piece < 3:
                mm = pe.matmul(misc[:, :], t.w_qkv[:, (piece - 1) * D:piece * D], xn_t[:, :], start=True, stop=True)
            else:
                for c in range(NQ):
                    mm = pe.matmul(misc[:, c * P:(c + 1) * P], xn_t[:, c * P:(c + 1) * P], t.w_qkv[:, 2 * D:3 * D],
                                   start=True, stop=True)
            mm.then_inc(s_misc, 1)

        def pe_project_out(pe, b, piece, last=False):
            if piece == 0:
                pe.wait_ge(s_o_norm, 4 * b + 5)
            pe.wait_ge(s_misc_read, fill_out(b, piece, last))
            for c in range(NQ):
                tile = misc[:, c * P:(c + 1) * P]
                if piece == 0:
                    mm = pe.transpose(tile, attn[:, c, :], t.ident[:, :])
                else:
                    mm = pe.matmul(tile, attn_t[:, c * P:(c + 1) * P], t.w_proj[:, :], start=True, stop=True)
            mm.then_inc(s_misc, 1)

        def pe_row(pe, b, first=False, last=False):
            for u in range(PAIRS):
                more = not (last and u + 2 >= PAIRS)
                if not (last and u == PAIRS - 1):
                    pe_turn_max(pe, *((b, u + 1) if u + 1 < PAIRS else (b + 1, 0)))
                for kt in range(NQ):
                    pe_scores_turned(pe, b, u, kt)
                    if more:
                        pe_scores(pe, *ahead(b, u), kt)
                    if kt >= 2:
                        pe_values(pe, b, u, kt - 2)
                    elif u >= 1:
                        pe_values(pe, b, u - 1, kt + 2)
                    elif not first:
                        pe_values(pe, b - 1, PAIRS - 1, kt + 2)
                    if kt == 3 and u % 2 == 0 and u >= 2:
                        pe_turn_outputs(pe, b, u // 2 - 1)
                    if kt == 3 and u == 0 and not first:
                        pe_turn_outputs(pe, b - 1, 3)
                    if u == 1 and kt in (1, 3) and not first:
                        pe_project_out(pe, b - 1, kt // 2)
                if not last and 1 <= u <= 4:
                    pe_project_in(pe, b + 1, u - 1)

        def v_maxima(dve, b, u, i):
            width = (Q_ORDER[i] + 1) * P
            for e in range(2):
                await_(dve, passed["vector"], s_scores, 64 * b + 8 * u + 2 * i + e + 1)
                dve.tensor_tensor_reduce(junk[:, e, 0:width], s_bank[e][:, 0:width], t.causal[:, N - width:N], 1.0, LOWEST,
                                         ALU.add, ALU.max, mx[:, u % 2, e, Q_ORDER[i]:Q_ORDER[i] + 1]).then_inc(s_tile_max, 1)

        def v_split_maxima(dve, own, b, u):
            m, p = mx[:, u % 2, :, :], mparts[:, u % 2, :, :, :]
            dve.wait_ge(s_tile_max, 64 * b + 8 * u + 16)
            own(dve.tensor_scalar(p[:, :, 0, :], m, -1.0, None, ALU.mult))
            dve.wait_ge(s_vec, own.value())
            own(dve.scalar_tensor_tensor(mres[:, :, :], m, -1.0, p[:, :, 0, :], ALU.mult, ALU.subtract))
            dve.wait_ge(s_vec, own.value())
            own(dve.tensor_copy(p[:, :, 1, :], mres[:, :, :]))
            dve.wait_ge(s_vec, own.value())
            dve.tensor_tensor(p[:, :, 2, :], mres[:, :, :], p[:, :, 1, :], ALU.subtract).then_inc(s_mparts, 1)

        def v_norm_outputs(dve, own, b, w):
            dve.wait_ge(s_o_turned, 4 * b + w + 2)
            tb = turn_bank[:, :].rearrange("p (q g r) -> p q g r", q=NQ, g=4)
            own(dve.reciprocal(rden[:, :, :], tb[:, :, :, HD]))
            dve.wait_ge(s_vec, own.value())
            out = attn[:, :, 32 * w:32 * w + 32].rearrange("p q (g d) -> p q g d", d=HD)
            dve.tensor_tensor(out, tb[:, :, :, 0:HD], rden[:, :, :].unsqueeze(3).broadcast_to([P, NQ, 4, HD]),
                              ALU.mult).then_inc(s_o_norm, 1)

        def v_stats(dve, own, rows, st, m, which):
            for c in range(NQ):
                own(dve.bn_stats(st[:, c, :], rows(c)))
            await_(dve, passed["vector"], s_vec, own.value())
            for c in range(NQ):
                ins = dve.bn_aggr(m[:, c, :], st[:, c, :])
            ins.then_inc(s_var[which], 1)

        def v_norm_in(dve, b):
            dve.wait_ge(s_rstd["in"], b + 1)
            for c in range(NQ):
                ins = dve.tensor_scalar(xn[:, c, :], x_t[:, c, b, :], mv[:, c, 0:1], rstd[:, c:c + 1],
                                        ALU.subtract, ALU.mult)
            ins.then_inc(s_xn, 1)

        def v_first_part(dve, own, b, k, first=False):
            fill = fill_in(b, 1 + "qk".index(k), first)
            dve.wait_ge(s_misc, fill)
            own(dve.tensor_copy(parts[k][:, 0, :], misc[:, :]))
            dve.wait_ge(s_vec, own.value())
            dve.tensor_tensor(rest[k][:, :], misc[:, :], parts[k][:, 0, :], ALU.subtract).then_inc(s_misc_read, 1)

        def v_values(dve, b, first=False):
            dve.wait_ge(s_misc, fill_in(b, 3, first))
            dve.tensor_copy(v_next[:, :, :], misc[:, :].rearrange("p (c d) -> p c d", d=D)).then_inc(s_misc_read, 1)

        def v_place_values(dve, b, half, first=False):
            if half == 0:
                dve.wait_ge(s_misc_read, fill_in(b, 3, first) + 1)
            dve.wait_ge(s_av, 32 * b + 4 if half else (4 if first else 32 * b - 12))
            for c in range(NQ):
                ins = dve.tensor_copy(t.v_ext[:, c, 8 * half:8 * half + 8, 0:HD],
                                      v_next[:, c, 64 * half:64 * half + 64].rearrange("p (h d) -> p h d", d=HD))
            ins.then_inc(s_vext[half], 1)

        def v_out_stats(dve, own, b, last=False):
            dve.wait_ge(s_misc, fill_out(b, 1, last))
            v_stats(dve, own, lambda c: misc[:, c * P:(c + 1) * P], stats2, mv2, "out")

        def v_out_add(dve, b, last=False):
            dve.wait_ge(s_rstd["out"], b + 1)
            for c in range(NQ):
                ins = dve.tensor_scalar(y[:, c, :], misc[:, c * P:(c + 1) * P], mv2[:, c, 0:1], rstd2[:, c:c + 1],
                                        ALU.subtract, ALU.mult)
            ins.then_inc(s_misc_read, 1)
            dve.wait_ge(s_misc_read, fill_out(b, 1, last) + 1)
            dve.tensor_tensor(x_t[:, :, b, :], x_t[:, :, b, :], y[:, :, :], ALU.add).then_inc(s_row_done, 1)

        def v_row(dve, b, first=False, last=False):
            own = Ticks(s_vec, STEPS_BEFORE if first else STEPS_BEFORE + STEPS_FIRST - STEPS_ROW + STEPS_ROW * b)
            for u in range(PAIRS):
                if u == 0 and not last:
                    v_stats(dve, own, lambda c: x_t[:, c, b + 1, :], stats, mv, "in")
                if not last and u in (3, 4):
                    v_first_part(dve, own, b + 1, "qk"[u - 3])
                if not last and u == 5:
                    v_values(dve, b + 1)
                if not last and u == 6:
                    v_place_values(dve, b + 1, 0)
                if not first and u == 2:
                    v_place_values(dve, b, 1)
                if not (last and u + 2 >= PAIRS):
                    for i in range(NQ):
                        v_maxima(dve, *ahead(b, u), i)
                    v_split_maxima(dve, own, *ahead(b, u))
                if u == 0 and not last:
                    v_norm_in(dve, b + 1)
                if u == 0 and not first:
                    v_norm_outputs(dve, own, b - 1, 3)
                if u in (2, 4, 6):
                    v_norm_outputs(dve, own, b, u // 2 - 1)
                if not first and u == 1:
                    v_out_stats(dve, own, b - 1)
                    v_out_add(dve, b - 1)
            assert last or own.n == (STEPS_FIRST if first else STEPS_ROW), own.n
            return own

        def a_copy_max(act, b, u):
            act.wait_ge(s_mrow[u % 2], 128 * b + 32 * (u // 2) + 32 if u >= 2 else 128 * b + 32)
            await_(act, passed["scalar"], s_mt, 8 * b + u + 1)
            act.activation(mrows[:, u % 2, :], max_bank[0:2 * MR * NQ, 0:P], ACT.Copy).then_inc(s_mt_copied, 1)

        def a_exp(act, b, u, kt):
            width = N - kt * P
            act.wait_ge(s_av, 32 * b + 4 * u + kt + 1)
            for e in range(2):
                await_(act, passed["scalar"], s_st, 64 * b + 8 * u + 2 * kt + e + 1)
                act.activation(probs[:, kt, e, 0:width], st_bank[e][:, 0:width], ACT.Exp, scale=SCALE)\
                   .then_inc(s_exp, 1)

        def a_copy_outputs(act, b, w):
            act.wait_ge(s_o_turned, 4 * b + w + 1)
            await_(act, passed["scalar"], s_av, 32 * b + 8 * w + 12)
            act.activation(outs[:, :], o_bank[:, :], ACT.Copy).then_inc(s_o_copied, 1)

        def a_copy_misc(act, dst, fill):
            await_(act, passed["scalar"], s_misc, fill)
            act.activation(dst[:, :], misc[:, :], ACT.Copy).then_inc(s_misc_read, 1)

        def a_row(act, b, first=False, last=False):
            for u in range(PAIRS):
                if not (last and u == PAIRS - 1):
                    a_copy_max(act, *((b, u + 1) if u + 1 < PAIRS else (b + 1, 0)))
                for kt in range(NQ):
                    a_exp(act, b, u, kt)
                    if kt == 1 and u % 2 == 0 and u >= 2:
                        a_copy_outputs(act, b, u // 2 - 1)
                    if kt == 1 and u == 0 and not first:
                        a_copy_outputs(act, b - 1, 3)
                    if kt == 2 and u == 1 and not first:
                        a_copy_misc(act, attn_t, fill_out(b - 1, 0))
                if u == 1 and not last:
                    a_copy_misc(act, xn_t, fill_in(b + 1, 0))
                if first:
                    act.dma_start(t.w1[:, u, :], a["L0_ffn_W1"][u]).then_inc(t.experts_loaded, 16)
                    act.dma_start(t.w2[:, F * u:F * u + F, :], a["L0_ffn_W2"][u].rearrange("(f p) d -> p f d", p=P))\
                      .then_inc(t.experts_loaded, 16)

        def p_mask(pool, b, u, kt):
            await_(pool, passed["pool"], s_exp, 64 * b + 8 * u + 2 * kt + 10)
            diagonal = probs[:, kt, :, 0:P]
            pool.affine_select(out=diagonal, in_=diagonal, compare_op=ALU.is_ge, fill=0.0, base=0,
                               pattern=[[0, 2], [1, P]], channel_multiplier=-1).then_inc(s_masked, 1)

        def p_rstd(pool, m, r, which, b):
            await_(pool, passed["pool"], s_var[which], b + 1)
            pool.tensor_scalar(r[:, :], m[:, :, 1], EPS, None, ALU.add).then_inc(s_shifted[which], 1)
            await_(pool, passed["pool"], s_shifted[which], b + 1)
            pool.tensor_tensor(r[:, :], r[:, :], t.minus_half[:, :], ALU.pow).then_inc(s_rstd[which], 1)

        def p_parts(pool, b, k, first=False):
            fill = fill_in(b, 1 + "qk".index(k), first)
            await_(pool, passed["pool"], s_misc_read, fill + 1)
            pool.tensor_copy(parts[k][:, 1, :], rest[k][:, :]).then_inc(s_pool, 1)
            await_(pool, passed["pool"], s_pool, 2 * b + "qk".index(k) + 1)
            pool.tensor_tensor(parts[k][:, 2, :], rest[k][:, :], parts[k][:, 1, :], ALU.subtract).then_inc(s_parts[k], 1)

        def p_row(pool, b, first=False, last=False):
            for u in range(PAIRS):
                for kt in range(NQ):
                    p_mask(pool, b, u, kt)
                    if kt == 1 and not last:
                        if u == 0:
                            p_rstd(pool, mv, rstd, "in", b + 1)
                        if u in (3, 4):
                            p_parts(pool, b + 1, "qk"[u - 3])
                if u == 1 and not first:
                    p_rstd(pool, mv2, rstd2, "out", b - 1)

        def d_max_rows(sp, b, u):
            await_(sp, passed["sync"], s_mt_copied, 8 * b + u + 2)
            for e in range(2):
                lo = 64 * e + KS
                sp.dma_start(t.q_stack[lo:lo + MR, u, :], mrows[MR * NQ * e:MR * NQ * (e + 1), u % 2, :])\
                  .then_inc(s_mrow[u % 2], 16)

        def d_write(sp, b, k):
            await_(sp, passed["sync"], s_parts[k], b + 1)
            for r in range(PARTS):
                sp.dma_start(scratch[k][:, r, :, :], parts[k][:, part_of[k][r], :]).then_inc(s_written, 16)

        def d_load(sp, half):
            for k, stack in (("q", t.q_stack), ("k", t.k_stack)):
                src = scratch[k].rearrange("(u e) r d n -> e (r d) u n", e=2)
                for e in range(2):
                    sp.dma_start(stack[64 * e:64 * e + KS, 4 * half:4 * half + 4, :], src[e][:, 4 * half:4 * half + 4, :])\
                      .then_inc(s_half[half], 16)

        def d_row(sp, b, first=False, last=False):
            for u in range(PAIRS):
                if not (last and u == PAIRS - 1):
                    d_max_rows(sp, *((b, u + 1) if u + 1 < PAIRS else (b + 1, 0)))
                if u == 0:
                    await_(sp, passed["sync"], s_exp, 64 * b + 8)
                    d_load(sp, 1)
                if u == 3 and not last:
                    await_(sp, passed["sync"], s_half[1], 64 * b + 64)
                    d_write(sp, b + 1, "q")
                if u == 4 and not last:
                    d_write(sp, b + 1, "k")
                if u == 5 and not last:
                    await_(sp, passed["sync"], s_written, 192 * b + 384)
                    await_(sp, passed["sync"], s_st, 64 * b + 32)
                    d_load(sp, 0)

        def all_rows(eng, row):
            row(eng, 0, first=True)
            with eng.Fori(1, S - 1) as b:
                row(eng, b)
            return row(eng, S - 1, last=True)

        with nc.Block() as block:
            @block.tensor
            def _(pe):
                pe.sem_inc(s_av, 4)
                pe.sem_inc(s_o_turned, 1)
                for piece in range(4):
                    pe_project_in(pe, 0, piece, first=True)
                for u in range(2):
                    for i in range(NQ):
                        pe_scores(pe, 0, u, i)
                    if u == 0:
                        pe_turn_max(pe, 0, 0)
                all_rows(pe, pe_row)
                for kt in (2, 3):
                    pe_values(pe, S - 1, PAIRS - 1, kt)
                pe_turn_outputs(pe, S - 1, 3)
                for piece in range(2):
                    pe_project_out(pe, S - 1, piece, last=True)

            @block.vector
            def _(dve):
                dve.sem_inc(s_tile_max, 8)
                dve.sem_inc(s_o_norm, 1)
                dve.sem_inc(s_misc_read, 1)
                own = Ticks(s_vec)
                dve.wait_ge(t.first_x_loaded, 16)
                v_stats(dve, own, lambda c: x_t[:, c, 0, :], stats, mv, "in")
                v_norm_in(dve, 0)
                v_first_part(dve, own, 0, "q", first=True)
                v_first_part(dve, own, 0, "k", first=True)
                v_values(dve, 0, first=True)
                v_place_values(dve, 0, 0, first=True)
                v_place_values(dve, 0, 1, first=True)
                for u in range(2):
                    for i in range(NQ):
                        v_maxima(dve, 0, u, i)
                    v_split_maxima(dve, own, 0, u)
                assert own.n == STEPS_BEFORE, own.n
                dve.wait_ge(t.rest_x_loaded, 16 * (S - 1))
                own = all_rows(dve, v_row)
                v_norm_outputs(dve, own, S - 1, 3)
                v_out_stats(dve, own, S - 1, last=True)
                v_out_add(dve, S - 1, last=True)

            @block.scalar
            def _(act):
                act.sem_inc(s_exp, 8)
                act.sem_inc(s_mt_copied, 1)
                act.sem_inc(s_o_copied, 1)
                a_copy_misc(act, xn_t, fill_in(0, 0, first=True))
                a_copy_max(act, 0, 0)
                all_rows(act, a_row)
                a_copy_outputs(act, S - 1, 3)
                a_copy_misc(act, attn_t, fill_out(S - 1, 0, last=True))

            @block.gpsimd
            def _(pool):
                p_rstd(pool, mv, rstd, "in", 0)
                p_parts(pool, 0, "q", first=True)
                p_parts(pool, 0, "k", first=True)
                all_rows(pool, p_row)
                p_rstd(pool, mv2, rstd2, "out", S - 1)

            @block.sync
            def _(sp):
                sp.sem_inc(s_mrow[0], 32)
                sp.sem_inc(s_mrow[1], 32)
                d_write(sp, 0, "q")
                d_write(sp, 0, "k")
                sp.wait_ge(s_written, 192)
                d_load(sp, 0)
                d_max_rows(sp, 0, 0)
                all_rows(sp, d_row)


R = S // C
G = 4
INNER_AT = 22
GROUPS = C * R
HALVED = (1,)
STEPS_E, STEPS_P, STEPS_S, STEPS_M, STEPS_Q = 6, 9, 13, 56, 16 + len(HALVED)


def masked(value, bits):
    return value & bits if isinstance(value, int) else (value & bits).with_bounds(min_val=0, max_val=bits)


def experts_and_mixing(nc, a, t, sem, out):
    x_out = out.rearrange("s (c p) d -> p c s d", p=P)
    mask_scratch = nc.dram_tensor("mask_scratch", [E, N], F32, kind="Internal").ap()

    s_vec_e, s_vec_p, s_vec_s = sem("vector_step_experts"), sem("vector_step_experts_end"), sem("vector_step_gates")
    s_vec_m, s_vec_q = sem("vector_step_weights"), sem("vector_step_values")
    s_var1, s_shift1, s_rstd1, s_xn1 = sem("variances1"), sem("shifted1"), sem("inverse_dev1"), sem("rows_normalised1")
    s_var2, s_shift2, s_rstd2, s_xn2 = sem("variances2"), sem("shifted2"), sem("inverse_dev2"), sem("rows_normalised2")
    s_m1, s_m1_read = sem("bank_m1_filled"), sem("bank_m1_read")
    s_m2, s_m2_read = sem("bank_m2_filled"), sem("bank_m2_read")
    s_gated, s_gexp, s_mask = sem("gates_shifted"), sem("gates_exp"), sem("mask_ready")
    s_mask_out, s_mask_lo, s_mask_hi = sem("mask_written"), sem("mask_spread_low"), sem("mask_spread_high")
    s_xt = sem("expert_rows_ready")
    s_h, s_relu, s_y, s_y_read = sem("hidden_ready"), sem("relu_done"), sem("expert_product"), sem("expert_read")
    s_acc = sem("experts_summed")
    s_k, s_k_read = sem("kinks_product"), sem("kinks_read")
    s_in, s_relu2 = sem("inner_product"), sem("inner_relu_done")
    s_y2, s_y2_read = sem("outer_product"), sem("outer_read")
    s_keep, s_xs = sem("rows_kept"), sem("rows_recalled")
    s_lg, s_tanh, s_shifted, s_p = sem("logits_ready"), sem("gates_tanh"), sem("logits_shifted"), sem("weights_exp")
    s_vprod, s_vsum = sem("weighted_values"), sem("weighted_values_summed")
    s_mixed_scaled = sem("projection_normalised")
    s_mixed, s_x2 = sem("mixture_copied"), sem("x_after_last")
    s_out = sem("rows_written")
    passed = {k: sem("passed1_" + k) for k in ("vector", "scalar", "pool", "sync")}

    with ExitStack() as ctx:
        def sb(name, shape, dt=F32):
            return ctx.enter_context(nc.sbuf_tensor(name, shape, dt))

        banks = [ctx.enter_context(nc.psum_tensor(f"rest_bank{i}", [P, 512], F32)) for i in range(8)]
        h_bank, y_bank, m1, k_bank, y2_bank, m2 = banks[0:2], banks[2:4], banks[4], banks[5], banks[6], banks[7]
        xn1, xn1_t, xn1_t2 = sb("xn1", [P, G, D]), sb("xn1_t", [P, N]), sb("xn1_t2", [P, N])
        stats1, mv1, rstd1 = sb("stats1", [P, G, 6]), sb("mv1", [P, G, 2]), sb("rstd1", [P, G])
        shift1, shift2 = sb("mean_shift1", [P, G]), sb("mean_shift2", [P, G])
        stats2, mv2, rstd2 = sb("stats2b", [P, G, 6]), sb("mv2b", [P, G, 2]), sb("rstd2b", [P, G])
        gate, top, shifted, keep = sb("gate", [P, G, E]), sb("top", [P, G, 8]), sb("shifted", [P, G, E]), sb("keep", [P, G, E])
        gexp, gsum, mask_t = sb("gexp", [P, G, E]), sb("gsum", [P, G]), sb("mask_t", [E, N])
        mask_all = sb("mask_all", [P, E, N])
        hidden, term, total = sb("hidden", [P, 4, N]), sb("term", [P, N]), sb("total", [P, N])
        y1 = sb("y1", [P, G, D])
        kv = sb("kv", [P, 2 * S, 2 * D])
        kept, xs = sb("kept", [P, R, N]), sb("xs", [P, N])
        q = sb("q", [P, G, D])
        kinks = sb("kinks", [P, 2 * NPOS, G, H])
        prod = sb("prod", [P, S, D])
        logits, pos, acc = sb("logits", [P, S, G, H]), sb("pos", [P, S, G, H]), sb("acc", [P, S, G, H])
        kterm = logits
        peak, wsum = sb("peak", [P, G * H]), sb("wsum", [P, G * H])
        o, o_t, y2 = sb("o", [P, G, D]), sb("o_t", [P, N]), sb("y2", [P, G, D])
        hidden2 = sb("hidden2", [P, 4, N])
        spare = hidden2[:, :, :].rearrange("p k n -> p (k n)").rearrange("p (t c) -> p t c", c=D)
        weighted = [spare, prod[:, :, :], spare, spare]
        kterms = [kterm[:, :, :, :].rearrange("p t g h -> p (t g h)")]
        kterms += [prod[:, :, :].rearrange("p t c -> p (t c)")[:, n * S * G * H:(n + 1) * S * G * H] for n in range(2)]
        z_t = o_t

        def tiles(g):
            return t.x[:, bass.ds(G * g, G), :]

        def row(g):
            return lambda j: t.x[:, G * g + j, :]

        def special(i, values, otherwise):
            return values[i] if isinstance(i, int) and i in values else otherwise

        def before_m1(i):
            return special(i, {-1: -4, GROUPS: 7 * GROUPS - 4}, 7 * i - 1)

        def before_var1(i):
            return special(i, {-1: -2, GROUPS: 3 * GROUPS - 2}, 3 * i - 1)

        def before_xn1(i):
            return special(i, {-1: -1, GROUPS: 2 * GROUPS - 1}, 2 * i)

        def before_m2(i):
            return special(i, {R: 0}, 4 * (i - R) - 3)

        def pe_turn(pe, i, fill, number):
            pe.wait_ge(s_m1_read, before_m1(i) + fill)
            pe.wait_ge(s_xn1, before_xn1(i) + number)
            for j in range(G):
                mm = pe.transpose(m1[:, j * P:(j + 1) * P], xn1[:, j, :], t.ident[:, :])
            mm.then_inc(s_m1, 1)

        def pe_gates(pe, i):
            pe.wait_ge(s_m1_read, before_m1(i) + 6)
            for j in range(G):
                mm = pe.matmul(m1[:, j * E:(j + 1) * E], xn1_t2[:, j * P:(j + 1) * P], t.w_gate[:, :], start=True, stop=True)
            mm.then_inc(s_m1, 1)

        def pe_mask(pe, i):
            pe.wait_ge(s_m1_read, before_m1(i) + 7)
            pe.wait_ge(s_mask, i + 2)
            for j in range(G):
                mm = pe.transpose(m1[0:E, j * P:(j + 1) * P], gexp[:, j, :], t.ident[:, :])
            mm.then_inc(s_m1, 1)

        def pe_hidden(pe, i, k):
            if k == 0:
                pe.wait_ge(s_xt, i + 1)
            pe.wait_ge(s_relu, 32 * i + k + 1)
            pe.matmul(h_bank[k % 2][:, :], t.w1[:, k // F, (k % F) * P:(k % F + 1) * P], xn1_t[:, :],
                      start=True, stop=True).then_inc(s_h, 1)

        def pe_expert(pe, i, k):
            if k % F == 0:
                pe.wait_ge(s_y_read, 8 * i + k // F + 1)
            pe.wait_ge(s_relu, 32 * i + k + 3)
            pe.matmul(y_bank[k // F % 2][:, :], t.w2[:, k, :], hidden[:, k % 4, :], start=(k % F == 0), stop=(k % F == F - 1))\
              .then_inc(s_y, 1)

        def pe_experts_out(pe, i):
            pe.wait_ge(s_m1_read, before_m1(i) + 1)
            pe.wait_ge(s_acc, i)
            for j in range(G):
                mm = pe.transpose(m1[:, j * P:(j + 1) * P], total[:, j * P:(j + 1) * P], t.ident[:, :])
            mm.then_inc(s_m1, 1)

        def pe_keys_values(pe, i, half):
            pe.wait_ge(s_m1_read, before_m1(i) + 3 + half)
            for j in range(2):
                g = 2 * half + j
                mm = pe.matmul(m1[:, j * 2 * D:(j + 1) * 2 * D], xn1_t2[:, g * P:(g + 1) * P], t.w_at[:, D:3 * D],
                               start=True, stop=True)
            mm.then_inc(s_m1, 1)

        def pe_queries(pe, i):
            pe.wait_ge(s_xs, i - R + 1)
            pe.wait_ge(s_m2_read, before_m2(i) + 1)
            for j in range(G):
                mm = pe.matmul(m2[:, j * P:(j + 1) * P], xs[:, j * P:(j + 1) * P], t.w_at[:, 0:D], start=True, stop=True)
            mm.then_inc(s_m2, 1)

        def pe_kinks(pe, i, j):
            pe.wait_ge(s_k_read, 4 * (i - R) + j + 1)
            pe.matmul(k_bank[:, :], xs[:, j * P:(j + 1) * P], t.w_kink[:, :], start=True, stop=True).then_inc(s_k, 1)

        def pe_mix(pe, i, j):
            if j == 0:
                pe.wait_ge(s_y2_read, i - R)
            pe.wait_ge(s_vprod, 4 * (i - R - 1) + j + 1)
            keys = S // 2 if j in HALVED else S
            for k in range(keys):
                mm = pe.matmul(y2_bank[:, j * P:(j + 1) * P], weighted[j][:, k, :], t.ident[:, :],
                               start=(k == 0), stop=(k == keys - 1))
            mm.then_inc(s_vsum, 1)

        def pe_project(pe, i, m):
            pe.wait_ge(s_m2_read, m + 2)
            pe.wait_ge(s_mixed, i - R)
            for j in range(G):
                mm = pe.matmul(m2[:, j * P:(j + 1) * P], o_t[:, j * P:(j + 1) * P], t.w_o[:, :], start=True, stop=True)
            mm.then_inc(s_m2, 1)

        def pe_turn_last(pe, i, m):
            pe.wait_ge(s_xn2, i - R)
            pe.wait_ge(s_m2_read, m + 3)
            for j in range(G):
                mm = pe.transpose(m2[:, j * P:(j + 1) * P], o[:, j, :], t.ident[:, :])
            mm.then_inc(s_m2, 1)

        def pe_inner(pe, m):
            pe.wait_ge(s_m2_read, m + 4)
            pe.matmul(m2[:, :], t.w_in[:, :], o_t[:, :], start=True, stop=True).then_inc(s_in, 1)

        def pe_outer(pe, i, k):
            pe.wait_ge(s_relu2, K2 * (i - R - 1) + k + 1)
            pe.matmul(y2_bank[:, :], t.w_out[:, k, :], hidden2[:, k % 4, :],
                      start=(k == 0), stop=(k == K2 - 1)).then_inc(s_y2, 1)

        def pe_turn_result(pe, i):
            pe.wait_ge(s_y2_read, i - R + 1)
            for j in range(G):
                mm = pe.transpose(m2[:, j * P:(j + 1) * P], z_t[:, j * P:(j + 1) * P], t.ident[:, :])
            mm.then_inc(s_m2, 1)

        def pe_step(pe, i, experts, end, gates, attend, finish):
            m = before_m2(i) - (0 if attend else 1) if finish else None
            for k in range(E * F + 2):
                if attend:
                    if k == 3:
                        pe_queries(pe, i)
                    if k in (4, 6, 9, 14):
                        pe_kinks(pe, i, (4, 6, 9, 14).index(k))
                if end:
                    if k == 2:
                        pe_experts_out(pe, i)
                    if k == 7:
                        pe_turn(pe, i, 2, 1)
                    if k in (8, 9):
                        pe_keys_values(pe, i, k - 8)
                if gates:
                    if k == 13:
                        pe_turn(pe, i, 5, 2)
                    if k == 15:
                        pe_gates(pe, i)
                    if k == 30:
                        pe_mask(pe, i)
                if finish:
                    if k in (5, 7, 10, 13):
                        pe_mix(pe, i, (5, 7, 10, 13).index(k))
                    if k == 15:
                        pe_project(pe, i, m)
                    if k == 21:
                        pe_turn_last(pe, i, m)
                    if k == INNER_AT:
                        pe_inner(pe, m)
                    if INNER_AT + 2 <= k < INNER_AT + 2 + K2:
                        pe_outer(pe, i, k - INNER_AT - 2)
                    if k == 33:
                        pe_turn_result(pe, i)
                if experts:
                    if k < E * F:
                        pe_hidden(pe, i, k)
                    if k >= 2:
                        pe_expert(pe, i, k - 2)

        def v_stats(dve, own, rows, st, m, s_var, s_rstd, before):
            if not (isinstance(before, int) and before == 0):
                await_(dve, passed["vector"], s_rstd, before)
            for j in range(G):
                own(dve.bn_stats(st[:, j, :], rows(j)))
            await_(dve, passed["vector"], own.sem, own.value())
            for j in range(G):
                ins = dve.bn_aggr(m[:, j, :], st[:, j, :])
            ins.then_inc(s_var, 1)

        def v_stats1(dve, own, i, number, rows):
            v_stats(dve, own, rows, stats1, mv1, s_var1, s_rstd1, before_var1(i) + number - 1)

        def v_gates(dve, own, i):
            dve.wait_ge(s_m1, before_m1(i) + 6)
            dve.tensor_copy(gate[:, :, :], m1[:, 0:G * E].rearrange("p (g e) -> p g e", e=E)).then_inc(s_m1_read, 1)
            await_(dve, passed["vector"], s_m1_read, before_m1(i) + 7)
            for j in range(G):
                own(dve.max(top[:, j, :], gate[:, j, :]))
            dve.wait_ge(s_vec_s, own.value())
            dve.tensor_tensor(shifted[:, :, :], gate[:, :, :], top[:, :, 0:1].broadcast_to([P, G, E]), ALU.subtract)\
               .then_inc(s_gated, 1)
            own(dve.tensor_tensor(keep[:, :, :], gate[:, :, :], top[:, :, 1:2].broadcast_to([P, G, E]), ALU.is_ge))
            dve.wait_ge(s_vec_s, own.value())

        def v_mask(dve, own, i):
            dve.wait_ge(s_gexp, i + 2)
            own(dve.tensor_tensor(gexp[:, :, :], gexp[:, :, :], keep[:, :, :], ALU.mult))
            dve.wait_ge(s_vec_s, own.value())
            own(dve.tensor_reduce(gsum[:, :], gexp[:, :, :], AX.X, ALU.add))
            dve.wait_ge(s_vec_s, own.value())
            own(dve.reciprocal(gsum[:, :], gsum[:, :]))
            dve.wait_ge(s_vec_s, own.value())
            own(dve.tensor_scalar(gsum[:, :], gsum[:, :], 1.0 / E, None, ALU.mult))
            dve.wait_ge(s_vec_s, own.value())
            dve.tensor_tensor(gexp[:, :, :], gexp[:, :, :], gsum[:, :].unsqueeze(2).broadcast_to([P, G, E]), ALU.mult)\
               .then_inc(s_mask, 1)

        def v_expert(dve, own, i, e):
            if e == 0:
                dve.wait_ge(s_mask_lo, 16 * i + 16)
            if e == E // 2:
                dve.wait_ge(s_mask_hi, 16 * i + 16)
            dve.wait_ge(s_y, 32 * i + 4 * e + 8)
            dst = total if e == 0 else term
            dve.scalar_tensor_tensor(dst[:, :], y_bank[e % 2][:, :], t.b2[:, e:e + 1], mask_all[:, e, :], ALU.add, ALU.mult)\
               .then_inc(s_y_read, 1)
            if e >= 1:
                dve.wait_ge(s_y_read, 8 * i + e + 3)
                if e == E - 1:
                    dve.tensor_tensor(total[:, :], total[:, :], term[:, :], ALU.add).then_inc(s_acc, 1)
                else:
                    own(dve.tensor_tensor(total[:, :], total[:, :], term[:, :], ALU.add))
                    dve.wait_ge(s_vec_e, own.value())

        def v_experts_stats(dve, own, i):
            dve.wait_ge(s_m1, before_m1(i) + 1)
            v_stats1(dve, own, i, 1, lambda j: m1[:, j * P:(j + 1) * P])

        def v_experts_add(dve, own, i):
            dve.wait_ge(s_m1_read, before_m1(i) + 2)
            own(dve.tensor_tensor(tiles(i - 1), tiles(i - 1), y1[:, :, :], ALU.add))
            await_(dve, passed["vector"], s_vec_p, own.value())
            v_stats1(dve, own, i, 2, row(i - 1))

        def v_keys_values(dve, i, half):
            dve.wait_ge(s_m1, before_m1(i) + 3 + half)
            dve.tensor_tensor(kv[:, bass.ds(G * masked(i - 1, 2 * R - 1) + 2 * half, 2), :],
                              m1[:, :].rearrange("p (g d) -> p g d", g=2),
                              t.b_at[:, D:3 * D].unsqueeze(1).broadcast_to([P, 2, 2 * D]), ALU.add)\
               .then_inc(s_m1_read, 1)

        def v_queries(dve, i):
            dve.wait_ge(s_m2, before_m2(i) + 1)
            dve.tensor_tensor(q[:, :, :], m2[:, :].rearrange("p (g d) -> p g d", g=G),
                              t.b_at[:, 0:D].unsqueeze(1).broadcast_to([P, G, D]), ALU.add).then_inc(s_m2_read, 1)

        def v_kink_heights(dve, i, j):
            dve.wait_ge(s_k, 4 * (i - R) + j + 1)
            dve.tensor_tensor(kinks[:, :, j, :], k_bank[:, :].rearrange("p (n h) -> p n h", h=H),
                              t.b_kink[:, :].rearrange("p (n h) -> p n h", h=H), ALU.add).then_inc(s_k_read, 1)

        def v_logits(dve, own, i, j):
            if j == 0:
                dve.wait_ge(s_m2_read, before_m2(i) + 2)
            keys = kv[:, bass.ds(G * masked(i - R, R), S), 0:D]
            own(dve.tensor_tensor(prod[:, :, :], q[:, j, :].unsqueeze(1).broadcast_to([P, S, D]), keys, ALU.mult))
            dve.wait_ge(s_vec_m, own.value())
            ins = dve.tensor_reduce(logits[:, :, j, :], prod[:, :, :].rearrange("p t (h d) -> p t h d", d=HD),
                                    AX.X, ALU.add)
            if j == G - 1:
                ins.then_inc(s_lg, 1)
                dve.wait_ge(s_lg, i - R + 1)
            else:
                own(ins)
                dve.wait_ge(s_vec_m, own.value())

        def v_positions(dve, own, i):
            dve.wait_ge(s_tanh, 2 * (i - R) + 2)
            flat = pos[:, :, :, :].rearrange("p t g h -> p t (g h)")
            for k in range(S - 2, -1, -1):
                own(dve.tensor_tensor(flat[:, k, :], flat[:, k, :], flat[:, k + 1, :], ALU.add))
                dve.wait_ge(s_vec_m, own.value())
            dve.wait_ge(s_k_read, 4 * (i - R) + 5)
            own(dve.scalar_tensor_tensor(acc[:, :, :, :].rearrange("p t g h -> p (t g h)"),
                                         logits[:, :, :, :].rearrange("p t g h -> p (t g h)"), SCALE,
                                         kinks[:, NPOS:, :, :].rearrange("p t g h -> p (t g h)"), ALU.mult, ALU.add))
            dve.wait_ge(s_vec_m, own.value())

        def v_kink_term(dve, own, n):
            height = kinks[:, n, :, :].rearrange("p g h -> p (g h)").unsqueeze(1).broadcast_to([P, S - n, G * H])
            own(dve.scalar_tensor_tensor(kterms[n % 3][:, 0:(S - n) * G * H].rearrange("p (t g) -> p t g", g=G * H),
                                         pos[:, 0:S - n, :, :].rearrange("p t g h -> p t (g h)"), float(n), height,
                                         ALU.max, ALU.mult))

        def v_kink(dve, own, n):
            if n == 0:
                v_kink_term(dve, own, 0)
            written = own.value()
            if n + 1 < NPOS:
                v_kink_term(dve, own, n + 1)
            dve.wait_ge(s_vec_m, written)
            total_to = acc[:, 0:S - n, :, :].rearrange("p t g h -> p (t g h)")
            own(dve.tensor_tensor(total_to, total_to, kterms[n % 3][:, 0:(S - n) * G * H], ALU.add))

        def v_softmax(dve, own, i):
            by_key = lambda x: x[:, :, :, :].rearrange("p t g h -> p (g h) t")
            flat = lambda x: x[:, :, :, :].rearrange("p t g h -> p t (g h)")
            dve.wait_ge(s_vec_m, own.value())
            own(dve.tensor_reduce(peak[:, :], by_key(acc), AX.X, ALU.max))
            dve.wait_ge(s_vec_m, own.value())
            dve.tensor_tensor(flat(acc), flat(acc), peak[:, :].unsqueeze(1).broadcast_to([P, S, G * H]), ALU.subtract)\
               .then_inc(s_shifted, 1)

        def v_weight_sums(dve, own, i):
            by_key = lambda x: x[:, :, :, :].rearrange("p t g h -> p (g h) t")
            dve.wait_ge(s_p, i - R)
            own(dve.tensor_reduce(wsum[:, :], by_key(acc), AX.X, ALU.add))
            dve.wait_ge(s_vec_q, own.value())
            own(dve.reciprocal(wsum[:, :], wsum[:, :]))
            dve.wait_ge(s_vec_q, own.value())
            flat = acc[:, :, :, :].rearrange("p t g h -> p t (g h)")
            own(dve.tensor_tensor(flat, flat, wsum[:, :].unsqueeze(1).broadcast_to([P, S, G * H]), ALU.mult))
            dve.wait_ge(s_vec_q, own.value())

        def v_values(dve, own, i, j):
            values = kv[:, bass.ds(G * masked(i - R - 1, R), S), D:2 * D].rearrange("p t (h d) -> p t h d", d=HD)
            weights = acc[:, :, j, :].unsqueeze(3).broadcast_to([P, S, H, HD])
            if j != 1:
                dve.wait_ge(s_vsum, 4 * (i - R - 1) + (1, None, 2, 4)[j])
            ins = dve.tensor_tensor(weighted[j].rearrange("p t (h d) -> p t h d", d=HD), weights, values, ALU.mult)
            if j in HALVED:
                own(ins)
                dve.wait_ge(s_vec_q, own.value())
                ins = dve.tensor_tensor(weighted[j][:, 0:S // 2, :], weighted[j][:, 0:S // 2, :],
                                        weighted[j][:, S // 2:S, :], ALU.add)
            ins.then_inc(s_vprod, 1)

        def v_stats2(dve, own, i, number, rows):
            v_stats(dve, own, rows, stats2, mv2, s_var2, s_rstd2, 3 * (i - R - 1) + number)

        def v_mixed_stats(dve, own, i, m):
            dve.wait_ge(s_m2, m + 2)
            dve.tensor_tensor(y2[:, :, :], m2[:, :].rearrange("p (g d) -> p g d", g=G),
                              t.b_o[:, :].unsqueeze(1).broadcast_to([P, G, D]), ALU.add).then_inc(s_m2_read, 1)
            dve.wait_ge(s_m2_read, m + 3)
            v_stats2(dve, own, i, 1, lambda j: y2[:, j, :])

        def v_mixed_add(dve, own, i):
            g = i - R - 1
            dve.wait_ge(s_mixed_scaled, i - R)
            own(dve.tensor_tensor(tiles(g), tiles(g), y2[:, :, :], ALU.add))
            await_(dve, passed["vector"], s_vec_q, own.value())
            v_stats2(dve, own, i, 2, row(g))

        def v_last_add(dve, i, m):
            g = i - R - 1
            dve.wait_ge(s_m2_read, m + 5)
            dve.tensor_tensor(tiles(g), tiles(g), y2[:, :, :], ALU.add).then_inc(s_x2, 1)

        def v_step(dve, i, experts, end, gates, attend, finish):
            own_e, own_p, own_s = Ticks(s_vec_e, STEPS_E * i), Ticks(s_vec_p, STEPS_P * (i - 1)), Ticks(s_vec_s, STEPS_S * (i + 1))
            own_m, own_q = Ticks(s_vec_m, STEPS_M * (i - R)), Ticks(s_vec_q, STEPS_Q * (i - R - 1))
            m = before_m2(i) - (0 if attend else 1) if finish else None
            for e in range(E):
                if e == 0:
                    if end:
                        v_expert(dve, None, i - 1, E - 1)
                    if finish:
                        v_weight_sums(dve, own_q, i)
                    if end:
                        v_experts_stats(dve, own_p, i)
                    if finish:
                        v_values(dve, own_q, i, 0)
                    if attend:
                        v_queries(dve, i)
                    if finish:
                        v_values(dve, own_q, i, 1)
                    if end:
                        v_experts_add(dve, own_p, i)
                    if attend:
                        v_kink_heights(dve, i, 0)
                if e == 1:
                    if gates:
                        v_stats1(dve, own_s, i, 3, row(i + 1))
                    if attend:
                        v_kink_heights(dve, i, 1)
                if e == 2:
                    if finish:
                        v_values(dve, own_q, i, 2)
                    if end:
                        v_keys_values(dve, i, 0)
                        v_keys_values(dve, i, 1)
                        dve.wait_ge(s_m1_read, before_m1(i) + 5)
                    if finish:
                        dve.wait_ge(s_vsum, 4 * (i - R - 1) + 3)
                    if attend:
                        v_logits(dve, own_m, i, 0)
                if e == 3:
                    if finish:
                        v_values(dve, own_q, i, 3)
                    if attend:
                        v_kink_heights(dve, i, 2)
                        v_logits(dve, own_m, i, 1)
                        v_logits(dve, own_m, i, 2)
                if e == 4:
                    if finish:
                        v_mixed_stats(dve, own_q, i, m)
                    if attend:
                        v_kink_heights(dve, i, 3)
                        v_logits(dve, own_m, i, 3)
                    if finish:
                        v_mixed_add(dve, own_q, i)
                if e == 5:
                    if gates:
                        v_gates(dve, own_s, i)
                    if attend:
                        v_positions(dve, own_m, i)
                if e == 6 and gates:
                    v_mask(dve, own_s, i)
                if attend:
                    for n in {5: range(0, 2), 6: range(2, 7), 7: range(7, NPOS)}.get(e, ()):
                        v_kink(dve, own_m, n)
                if e == 7:
                    if attend:
                        v_softmax(dve, own_m, i)
                if experts and e >= 1:
                    v_expert(dve, own_e, i, e - 1)
                if e == 7 and finish:
                    dve.wait_ge(s_m2, m + 4)
                    v_stats2(dve, own_q, i, 3, lambda j: m2[:, j * P:(j + 1) * P])
                    v_last_add(dve, i, m)
            assert not experts or own_e.n == STEPS_E, own_e.n
            assert not end or own_p.n == STEPS_P, own_p.n
            assert not gates or own_s.n == STEPS_S, own_s.n
            assert not attend or own_m.n == STEPS_M, own_m.n
            assert not finish or own_q.n == STEPS_Q, own_q.n

        def a_copy(act, dst, bank, s_fill, fill, s_read):
            await_(act, passed["scalar"], s_fill, fill)
            act.activation(dst, bank, ACT.Copy).then_inc(s_read, 1)

        def a_scale(act, s_rstd, number, rows, dst, r, shift):
            await_(act, passed["scalar"], s_rstd, number)
            for j in range(G):
                ins = act.activation(dst[:, j, :], rows(j), ACT.Identity, scale=r[:, j:j + 1], bias=shift[:, j:j + 1])
            return ins

        def a_scale1(act, i, number, rows, dst):
            return a_scale(act, s_rstd1, before_var1(i) + number, rows, dst, rstd1, shift1)

        def a_scale2(act, i, number, rows, dst):
            return a_scale(act, s_rstd2, 3 * (i - R - 1) + number + 1, rows, dst, rstd2, shift2)

        def a_expert_rows(act, i):
            if not (isinstance(i, int) and i == 0):
                await_(act, passed["scalar"], s_h, 32 * i)
            act.activation(xn1_t[:, :], xn1_t2[:, :], ACT.Copy).then_inc(s_xt, 1)
            await_(act, passed["scalar"], s_xt, i + 1)

        def a_inner(act, i, k):
            if k == 0:
                act.wait_ge(s_in, i - R)
            await_(act, passed["scalar"], s_y2, K2 * (i - R - 1) + k + 1)
            act.activation(hidden2[:, k % 4, :], m2[:, :], ACT.Relu, scale=t.s_in[:, k:k + 1], bias=t.b_in[:, k:k + 1])\
               .then_inc(s_relu2, 1)

        def a_step(act, i, experts, end, gates, attend, finish):
            m = before_m2(i) - (0 if attend else 1) if finish else None
            if experts:
                a_expert_rows(act, i)
            for k in range(E * F):
                if k == 5 and end:
                    a_scale1(act, i, 1, lambda j: m1[:, j * P:(j + 1) * P], y1).then_inc(s_m1_read, 1)
                if k == 6 and end:
                    a_scale1(act, i, 2, row(i - 1), xn1).then_inc(s_xn1, 1)
                if k == 7 and end:
                    a_copy(act, xn1_t2[:, :], m1[:, :], s_m1, before_m1(i) + 2, s_m1_read)
                if k == 11 and gates:
                    a_scale1(act, i, 3, row(i + 1), xn1).then_inc(s_xn1, 1)
                if k == 13 and gates:
                    if end:
                        await_(act, passed["scalar"], s_keep, i)
                    a_copy(act, xn1_t2[:, :], m1[:, :], s_m1, before_m1(i) + 5, s_m1_read)
                if k == 14 and finish:
                    await_(act, passed["scalar"], s_vsum, 4 * (i - R) + 1)
                    act.activation(o_t[:, :], y2_bank[:, :], ACT.Copy).then_inc(s_mixed, 1)
                if k == 18 and finish:
                    a_scale2(act, i, 1, lambda j: y2[:, j, :], y2).then_inc(s_mixed_scaled, 1)
                if k == 19 and attend:
                    await_(act, passed["scalar"], s_lg, i - R + 1)
                    act.activation(pos[:, :, :, :], logits[:, :, :, :], ACT.Tanh, scale=0.5 * SCALE).then_inc(s_tanh, 1)
                    await_(act, passed["scalar"], s_tanh, 2 * (i - R) + 1)
                    act.activation(pos[:, :, :, :], pos[:, :, :, :], ACT.Copy, scale=0.5, bias=0.5).then_inc(s_tanh, 1)
                if k == 21 and finish:
                    a_scale2(act, i, 2, row(i - R - 1), o).then_inc(s_xn2, 1)
                    a_copy(act, o_t[:, :], m2[:, :], s_m2, m + 3, s_m2_read)
                if INNER_AT <= k < INNER_AT + K2 and finish:
                    a_inner(act, i, k - INNER_AT)
                if k == 24 and gates:
                    await_(act, passed["scalar"], s_gated, i + 2)
                    act.activation(gexp[:, :, :], shifted[:, :, :], ACT.Exp).then_inc(s_gexp, 1)
                if k == 30 and gates:
                    a_copy(act, mask_t[:, :], m1[0:E, :], s_m1, before_m1(i) + 7, s_m1_read)
                if k == 31 and finish:
                    await_(act, passed["scalar"], s_y2, 8 * (i - R - 1) + 12)
                    act.activation(z_t[:, :], y2_bank[:, :], ACT.Identity, bias=t.b_out[:, 0:1]).then_inc(s_y2_read, 1)
                if experts:
                    act.wait_ge(s_y, 32 * i + k + 1)
                    await_(act, passed["scalar"], s_h, 32 * i + k + 1)
                    act.activation(hidden[:, k % 4, :], h_bank[k % 2][:, :], ACT.Relu, bias=t.b1[:, k:k + 1])\
                       .then_inc(s_relu, 1)
            if attend:
                await_(act, passed["scalar"], s_shifted, i - R + 1)
                act.activation(acc[:, :, :, :], acc[:, :, :, :], ACT.Exp).then_inc(s_p, 1)
            if finish:
                a_scale2(act, i, 3, lambda j: m2[:, j * P:(j + 1) * P], y2).then_inc(s_m2_read, 1)

        def p_rstd(pool, m, r, nm, s_var, s_pool, s_rstd, number):
            await_(pool, passed["pool"], s_var, number)
            pool.tensor_scalar(nm[:, :], m[:, :, 0], -1.0, None, ALU.mult)
            pool.tensor_scalar(r[:, :], m[:, :, 1], EPS, None, ALU.add).then_inc(s_pool, 1)
            await_(pool, passed["pool"], s_pool, 2 * number - 1)
            pool.tensor_tensor(r[:, :], r[:, :], t.minus_half[:, :], ALU.pow).then_inc(s_pool, 1)
            await_(pool, passed["pool"], s_pool, 2 * number)
            pool.tensor_tensor(nm[:, :], nm[:, :], r[:, :], ALU.mult).then_inc(s_rstd, 1)

        def p_step(pool, i, experts, end, gates, attend, finish):
            norm1 = lambda n: p_rstd(pool, mv1, rstd1, shift1, s_var1, s_shift1, s_rstd1, before_var1(i) + n)
            norm2 = lambda n: p_rstd(pool, mv2, rstd2, shift2, s_var2, s_shift2, s_rstd2, 3 * (i - R - 1) + n)
            if attend:
                if not (isinstance(i, int) and i == R):
                    await_(pool, passed["pool"], s_k, 4 * (i - R))
                pool.tensor_copy(xs[:, :], kept[:, masked(i - R, R - 1), :]).then_inc(s_xs, 1)
            if end:
                await_(pool, passed["pool"], s_xn1, before_xn1(i))
                norm1(1)
                await_(pool, passed["pool"], s_m1_read, before_m1(i) + 2)
                norm1(2)
                await_(pool, passed["pool"], s_m1_read, before_m1(i) + 3)
                pool.tensor_copy(kept[:, masked(i - 1, R - 1), :], xn1_t2[:, :]).then_inc(s_keep, 1)
            if gates:
                if not (isinstance(i, int) and i < 0):
                    await_(pool, passed["pool"], s_xn1, before_xn1(i) + 1)
                norm1(3)
            if finish:
                await_(pool, passed["pool"], s_m2_read, before_m2(i) + 1)
                norm2(1)
                await_(pool, passed["pool"], s_mixed_scaled, i - R)
                norm2(2)
                await_(pool, passed["pool"], s_xn2, i - R)
                norm2(3)

        def d_mask(sp, g):
            first = isinstance(g, int) and g == 0
            await_(sp, passed["sync"], s_m1_read, 4 if first else 7 * g)
            if not first:
                sp.wait_ge(s_mask_lo, 16 * g)
                await_(sp, passed["sync"], s_mask_hi, 16 * g)
            sp.dma_start(mask_scratch, mask_t[:, :]).then_inc(s_mask_out, 16)
            src = mask_scratch.rearrange("(o e) n -> o e n", o=1).broadcast_to([P, E, N])
            if not first:
                await_(sp, passed["sync"], s_y_read, 8 * g - 2)
            await_(sp, passed["sync"], s_mask_out, 16 * g + 16)
            sp.dma_start(mask_all[:, 0:E // 2, :], src[:, 0:E // 2, :]).then_inc(s_mask_lo, 16)
            if not first:
                await_(sp, passed["sync"], s_y_read, 8 * g + 2)
            sp.dma_start(mask_all[:, E // 2:E, :], src[:, E // 2:E, :]).then_inc(s_mask_hi, 16)

        def d_out(sp, c, r):
            g = R * c + r
            await_(sp, passed["sync"], s_x2, g + 1)
            sp.dma_start(x_out[:, c, bass.ds(G * r, G), :], tiles(g)).then_inc(s_out, 16)

        def d_all(sp):
            d_mask(sp, 0)
            with sp.Fori(1, R + 2) as g:
                d_mask(sp, g)
            with sp.Fori(0, 2) as c:
                with sp.Fori(0, R) as r:
                    d_mask(sp, R * c + r + R + 2)
                    d_out(sp, c, r)
            with sp.Fori(0, 2) as r:
                d_mask(sp, R * 2 + r + R + 2)
                d_out(sp, 2, r)
            with sp.Fori(2, R) as r:
                d_out(sp, 2, r)
            with sp.Fori(0, R) as r:
                d_out(sp, 3, r)

        def all_steps(eng, step):
            step(eng, -1, False, False, True, False, False)
            step(eng, 0, True, False, True, False, False)
            with eng.Fori(1, R) as i:
                step(eng, i, True, True, True, False, False)
            step(eng, R, True, True, True, True, False)
            with eng.Fori(R + 1, GROUPS - 1) as i:
                step(eng, i, True, True, True, True, True)
            step(eng, GROUPS - 1, True, True, False, True, True)
            step(eng, GROUPS, False, True, False, True, True)
            with eng.Fori(GROUPS + 1, GROUPS + R) as i:
                step(eng, i, False, False, False, True, True)
            step(eng, GROUPS + R, False, False, False, False, True)

        with nc.Block() as block:
            @block.tensor
            def _(pe):
                pe.sem_inc(s_y, 4)
                pe.sem_inc(s_y2, 4)
                pe.wait_ge(t.experts_loaded, 32 * E)
                all_steps(pe, pe_step)

            @block.vector
            def _(dve):
                dve.sem_inc(s_y_read, 2)
                all_steps(dve, v_step)

            @block.scalar
            def _(act):
                for s, n in ((s_m1_read, 1), (s_m2_read, 1), (s_relu, 2), (s_k_read, 1), (s_y2_read, 1), (s_vsum, 1), (s_rstd2, 1)):
                    act.sem_inc(s, n)
                all_steps(act, a_step)

            @block.gpsimd
            def _(pool):
                all_steps(pool, p_step)

            @block.sync
            def _(sp):
                d_all(sp)
                sp.wait_ge(s_out, 16 * C * R)


def build(nc, a, out):
    with ExitStack() as ctx:
        class t:
            pass

        def sb(name, shape, dt=F32):
            return ctx.enter_context(nc.sbuf_tensor(name, shape, dt))

        def sem(name):
            return ctx.enter_context(nc.semaphore(name))

        t.x = sb("x", [P, T, D])
        t.ident, t.ones, t.ident16 = sb("ident", [P, P]), sb("ones", [P, P]), sb("ident16", [P, P], BF16)
        t.w_at, t.b_at = sb("w_at", [P, 3 * D]), sb("b_at", [P, 3 * D])
        t.w_kink, t.b_kink = sb("w_kink", [P, 2 * NPOS * H]), sb("b_kink", [P, 2 * NPOS * H])
        t.w_o, t.b_o = sb("w_o", [P, D]), sb("b_o", [P, D])
        t.w_gate, t.w1, t.w2 = sb("w_gate", [P, E]), sb("w1", [P, E, HID]), sb("w2", [P, E * F, D])
        t.b1, t.b2 = sb("b1", [P, E * F]), sb("b2", [P, E])
        t.w_in, t.s_in, t.b_in = sb("w_in", [P, P]), sb("s_in", [P, K2]), sb("b_in", [P, K2])
        t.w_out, t.b_out = sb("w_out", [P, K2, D]), sb("b_out", [P, 1])
        t.minus_half = sb("minus_half", [P, C])
        t.first_x_loaded, t.rest_x_loaded = sem("first_x_loaded"), sem("rest_x_loaded")
        t.experts_loaded = sem("expert_weights_loaded")
        with ExitStack() as first:
            def sb0(name, shape, dt=F32):
                return first.enter_context(nc.sbuf_tensor(name, shape, dt))

            t.w_qkv, t.w_proj = sb0("w_qkv", [P, 3 * D]), sb0("w_proj", [P, D])
            t.causal = sb0("causal", [P, N])
            t.q_stack, t.k_stack = sb0("q_stack", [P, PAIRS, N], BF16), sb0("k_stack", [P, PAIRS, N], BF16)
            t.v_ext = sb0("v_ext", [P, NQ, H, 32])
            load_and_prepare(nc, a, t, sem)
            causal_attention(nc, a, t, sem)
        experts_and_mixing(nc, a, t, sem, out)


_INS = [
    'L0_attn_batch', 'L0_attn_W_qkv', 'L0_attn_u_qkv', 'L0_attn_sigma_qkv',
    'L0_attn_W_proj', 'L0_attn_u_proj', 'L0_attn_sigma_proj', 'L0_ffn_W_gate',
    'L0_ffn_W1', 'L0_ffn_b1', 'L0_ffn_W2', 'L0_ffn_b2',
    'L1_attn_Wq', 'L1_attn_bq', 'L1_attn_Wk', 'L1_attn_bk',
    'L1_attn_Wv', 'L1_attn_bv', 'L1_attn_Wo', 'L1_attn_bo',
    'L1_attn_pos_emb', 'L1_ffn_Win', 'L1_ffn_bin_', 'L1_ffn_W1',
    'L1_ffn_b1', 'L1_ffn_W2', 'L1_ffn_b2', 'L1_ffn_Wout',
    'L1_ffn_bout',
]
_OUT = (S, N, D)


def kernel(**inputs):
    import numpy as _np
    import concourse.bacc as _bacc
    from concourse import mybir as _mybir
    from concourse.bass_utils import run_bass_kernel_spmd as _run

    nc = _bacc.Bacc("TRN2", target_bir_lowering=False, num_devices=1)
    arrays, a = {}, {}
    for name in _INS:
        v = _np.ascontiguousarray(inputs[name])
        arrays[f"in_{name}_dram"] = v
        a[name] = nc.dram_tensor(f"in_{name}_dram", v.shape, _mybir.dt.from_np(v.dtype), kind="ExternalInput").ap()
    out = nc.dram_tensor("out_dram", _OUT, _mybir.dt.float32, kind="ExternalOutput").ap()
    build(nc, a, out)
    r = _run(nc, [arrays], core_ids=[0])
    return r.results[0]["out_dram"]
```
